# Optimizing a Trainium2 kernel written in Bass

```python
import numpy as np
import jax
import jax.numpy as jnp

def _softmax(x, axis=-1):
    return jax.nn.softmax(x, axis=axis)

def _gelu(x):
    return jax.nn.gelu(x, approximate=True)

def _silu(x):
    return jax.nn.silu(x)

def _sigmoid(x):
    return jax.nn.sigmoid(x)

def _layernorm(x, axis=-1, eps=1e-05):
    m = jnp.mean(x, axis=axis, keepdims=True)
    v = jnp.var(x, axis=axis, keepdims=True)
    return (x - m) / jnp.sqrt(v + eps)

def _scatter_add(tgt, idx, src, axis=0):
    return tgt.at[idx].add(src)

def _segment_sum(src, seg, n):
    return jax.ops.segment_sum(src, seg, n)
kernel_name = 'mk_gnn_resnorm_d2_gnn_r64_d0ba09'

def setup_inputs(seed: int=0):
    np.random.seed(seed)
    _w = jnp.asarray

    def _rec_inputs():
        import jax
        import jax.numpy as jnp
        _gk = jax.random.key(seed)
        x = -0.000202 + 1 * jax.random.normal(jax.random.fold_in(_gk, 1), (100000, 64), jnp.float32)
        src = jax.random.randint(jax.random.fold_in(_gk, 2), (25000,), 0, 100000, jnp.int32)
        dst = jnp.minimum((100000 * jax.random.uniform(jax.random.fold_in(_gk, 3), (25000,)) ** 2.0).astype(jnp.int32), 99999)
        _o = jnp.argsort(dst, stable=True)
        src = src[_o]
        dst = dst[_o]
        edge_type_32 = jax.random.randint(jax.random.fold_in(_gk, 12), (25000,), 0, 32, jnp.int32)
        return (x, src, dst, edge_type_32)
    x, src, dst, edge_type_32 = _rec_inputs()

    def _L0_gnn_setup():
        import jax, jax.numpy as jnp
        import numpy as np
        N_NODES = 100000
        N_EDGES = 25000
        IN_DIM, HID_DIM, OUT_DIM = (64, 128, 64)
        BN_EPS = 1e-05

        def sage_conv(x, src, dst, Wl, Wr, b):
            n = x.shape[0]
            agg = jax.ops.segment_sum(x[src], dst, num_segments=n)
            deg = jax.ops.segment_sum(jnp.ones((src.shape[0],), x.dtype), dst, num_segments=n)
            agg = agg / jnp.clip(deg, 1.0)[:, None]
            return agg @ Wl.T + x @ Wr.T + b

        def batchnorm(x, gamma, beta):
            mu = jnp.mean(x, axis=0)
            var = jnp.mean(jnp.square(x - mu), axis=0)
            return (x - mu) * jax.lax.rsqrt(var + BN_EPS) * gamma + beta
        key = jax.random.key(seed)
        ks = jax.random.split(key, 16)
        x = jax.random.normal(ks[0], (N_NODES, IN_DIM), dtype=jnp.float32)
        edge_index = jax.random.randint(ks[1], (2, N_EDGES), 0, N_NODES, dtype=jnp.int64)

        def lin(k, out_d, in_d):
            bound = 1.0 / np.sqrt(in_d)
            return jax.random.uniform(k, (out_d, in_d), jnp.float32, -bound, bound)
        return {'x': x, 'edge_index': edge_index, 'Wl0': lin(ks[2], HID_DIM, IN_DIM), 'Wr0': lin(ks[3], HID_DIM, IN_DIM), 'b0': jnp.zeros((HID_DIM,), jnp.float32), 'Wl1': lin(ks[4], HID_DIM, HID_DIM), 'Wr1': lin(ks[5], HID_DIM, HID_DIM), 'b1': jnp.zeros((HID_DIM,), jnp.float32), 'Wl2': lin(ks[6], OUT_DIM, HID_DIM), 'Wr2': lin(ks[7], OUT_DIM, HID_DIM), 'b2': jnp.zeros((OUT_DIM,), jnp.float32), 'g0': jnp.ones((HID_DIM,), jnp.float32), 'be0': jnp.zeros((HID_DIM,), jnp.float32), 'g1': jnp.ones((HID_DIM,), jnp.float32), 'be1': jnp.zeros((HID_DIM,), jnp.float32)}
    _L0_gnn_all = _L0_gnn_setup()
    _L0_gnn_in = {k: v for k, v in _L0_gnn_all.items() if k in ('Wl0', 'Wr0', 'b0', 'Wl1', 'Wr1', 'b1', 'Wl2', 'Wr2', 'b2', 'g0', 'be0', 'g1', 'be1')}
    del _L0_gnn_all

    def _L1_gnn_setup():
        import jax, jax.numpy as jnp
        import numpy as np
        N_NODES = 50000
        N_EDGES = 12500
        IN_F = 64
        OUT_F = 64
        N_REL = 32
        N_BASES = 30
        key = jax.random.key(seed)
        ks = jax.random.split(key, 6)
        x = jax.random.normal(ks[0], (N_NODES, IN_F), dtype=jnp.float32)
        edge_index = jax.random.randint(ks[1], (2, N_EDGES), 0, N_NODES, dtype=jnp.int64)
        edge_type = jax.random.randint(ks[2], (N_EDGES,), 0, N_REL, dtype=jnp.int64)
        basis = jax.random.normal(ks[3], (N_BASES, IN_F, OUT_F), dtype=jnp.float32) * 0.01
        coeff = jax.random.normal(ks[4], (N_REL, N_BASES), dtype=jnp.float32) * 0.01
        self_weight = jax.random.normal(ks[5], (IN_F, OUT_F), dtype=jnp.float32) * 0.01
        bias = jnp.zeros((OUT_F,), dtype=jnp.float32)
        return {'x': x, 'edge_index': edge_index, 'edge_type': edge_type, 'num_nodes': N_NODES, 'basis': basis, 'coeff': coeff, 'self_weight': self_weight, 'bias': bias}
    _L1_gnn_all = _L1_gnn_setup()
    _L1_gnn_in = {k: v for k, v in _L1_gnn_all.items() if k in ('basis', 'coeff', 'self_weight', 'bias')}
    del _L1_gnn_all
    return {'x': x, 'src': src, 'dst': dst, 'edge_type_32': edge_type_32, 'L0_gnn_Wl0': _L0_gnn_in['Wl0'], 'L0_gnn_Wr0': _L0_gnn_in['Wr0'], 'L0_gnn_b0': _L0_gnn_in['b0'], 'L0_gnn_Wl1': _L0_gnn_in['Wl1'], 'L0_gnn_Wr1': _L0_gnn_in['Wr1'], 'L0_gnn_b1': _L0_gnn_in['b1'], 'L0_gnn_Wl2': _L0_gnn_in['Wl2'], 'L0_gnn_Wr2': _L0_gnn_in['Wr2'], 'L0_gnn_b2': _L0_gnn_in['b2'], 'L0_gnn_g0': _L0_gnn_in['g0'], 'L0_gnn_be0': _L0_gnn_in['be0'], 'L0_gnn_g1': _L0_gnn_in['g1'], 'L0_gnn_be1': _L0_gnn_in['be1'], 'L1_gnn_basis': _L1_gnn_in['basis'], 'L1_gnn_coeff': _L1_gnn_in['coeff'], 'L1_gnn_self_weight': _L1_gnn_in['self_weight'], 'L1_gnn_bias': _L1_gnn_in['bias']}

def reference(x, src, dst, edge_type_32, L0_gnn_Wl0, L0_gnn_Wr0, L0_gnn_b0, L0_gnn_Wl1, L0_gnn_Wr1, L0_gnn_b1, L0_gnn_Wl2, L0_gnn_Wr2, L0_gnn_b2, L0_gnn_g0, L0_gnn_be0, L0_gnn_g1, L0_gnn_be1, L1_gnn_basis, L1_gnn_coeff, L1_gnn_self_weight, L1_gnn_bias):
    import jax
    import jax.numpy as jnp

    def _L0_gnn_ref(x, edge_index, Wl0, Wr0, b0, Wl1, Wr1, b1, Wl2, Wr2, b2, g0, be0, g1, be1):
        import jax, jax.numpy as jnp
        import numpy as np
        N_NODES = 100000
        N_EDGES = 25000
        IN_DIM, HID_DIM, OUT_DIM = (64, 128, 64)
        BN_EPS = 1e-05

        def sage_conv(x, src, dst, Wl, Wr, b):
            n = x.shape[0]
            agg = jax.ops.segment_sum(x[src], dst, num_segments=n)
            deg = jax.ops.segment_sum(jnp.ones((src.shape[0],), x.dtype), dst, num_segments=n)
            agg = agg / jnp.clip(deg, 1.0)[:, None]
            return agg @ Wl.T + x @ Wr.T + b

        def batchnorm(x, gamma, beta):
            mu = jnp.mean(x, axis=0)
            var = jnp.mean(jnp.square(x - mu), axis=0)
            return (x - mu) * jax.lax.rsqrt(var + BN_EPS) * gamma + beta
        src, dst = (edge_index[0], edge_index[1])
        h = sage_conv(x, src, dst, Wl0, Wr0, b0)
        h = jax.nn.relu(batchnorm(h, g0, be0))
        res = h
        h = sage_conv(h, src, dst, Wl1, Wr1, b1)
        h = jax.nn.relu(batchnorm(h, g1, be1)) + res
        return sage_conv(h, src, dst, Wl2, Wr2, b2)

    def _L1_gnn_ref(x, edge_index, edge_type, num_nodes, basis, coeff, self_weight, bias):
        import jax, jax.numpy as jnp
        import numpy as np
        N_NODES = 50000
        N_EDGES = 12500
        IN_F = 64
        OUT_F = 64
        N_REL = 32
        N_BASES = 30
        rel_weight = jnp.einsum('rb,bio->rio', coeff, basis)
        source_idx = edge_index[0]
        target_idx = edge_index[1]
        src_feats = x[source_idx]

        def body(out, rw_r):
            rw, r = rw_r
            mask = (edge_type == r).astype(jnp.float32)
            msg = src_feats @ rw * mask[:, None]
            return (out.at[target_idx].add(msg), None)
        out0 = jnp.zeros((num_nodes, rel_weight.shape[-1]), dtype=jnp.float32)
        out, _ = jax.lax.scan(body, out0, (rel_weight, jnp.arange(rel_weight.shape[0])))
        in_degree = jnp.zeros((num_nodes,), dtype=jnp.float32).at[target_idx].add(1.0)
        in_degree = jnp.maximum(in_degree, 1.0)
        out = out / in_degree[:, None]
        out = out + x @ self_weight + bias
        return out
    edge_index = jnp.stack([src, dst])
    x = _layernorm(x + _L0_gnn_ref(x, edge_index, L0_gnn_Wl0, L0_gnn_Wr0, L0_gnn_b0, L0_gnn_Wl1, L0_gnn_Wr1, L0_gnn_b1, L0_gnn_Wl2, L0_gnn_Wr2, L0_gnn_b2, L0_gnn_g0, L0_gnn_be0, L0_gnn_g1, L0_gnn_be1), axis=-1)
    x = _layernorm(x + _L1_gnn_ref(x, edge_index, edge_type_32, 100000, L1_gnn_basis, L1_gnn_coeff, L1_gnn_self_weight, L1_gnn_bias), axis=-1)
    return x

_drawn_inputs = setup_inputs


def setup_inputs(seed=0):
    import zlib

    import numpy as np

    out = dict(_drawn_inputs(seed))
    spreads = {'L0_gnn_b0': (0.0, 0.8),
     'L0_gnn_b1': (0.0, 0.8),
     'L0_gnn_b2': (0.0, 0.1),
     'L0_gnn_g0': (1.0, 0.2),
     'L0_gnn_be0': (0.0, 0.1),
     'L0_gnn_g1': (1.0, 0.2),
     'L0_gnn_be1': (0.0, 0.1),
     'L1_gnn_bias': (0.0, 0.1)}
    factors = {'L1_gnn_basis': 8.0, 'L1_gnn_coeff': 8.0}
    for name, (base, spread) in spreads.items():
        noise = np.random.default_rng([zlib.crc32(name.encode()), seed]).standard_normal(out[name].shape)
        drawn = base * np.exp(spread * noise) if base else spread * noise
        out[name] = jnp.asarray(drawn.astype(out[name].dtype))
    for name, factor in factors.items():
        out[name] = (out[name] * factor).astype(out[name].dtype)
    return out
```

```python
from contextlib import ExitStack

import concourse.bass as bass
import concourse.mybir as mybir

ALU = mybir.AluOpType
ACT = mybir.ActivationFunctionType
AX = mybir.AxisListType
F32 = mybir.dt.float32
I32 = mybir.dt.int32

P = 128
N_NODES = 100000
N_EDGES = 25000
IN = 64
HID = 128
OUT = 64
N_REL = 32
N_BASES = 30
J = 4
GROUP = J * P
E_GROUPS = -(-N_EDGES // GROUP)
E_TILES = E_GROUPS * J
E_ROWS = E_TILES * P
ZERO_ROW = E_ROWS
HALF = E_TILES // 2
D_GROUPS = N_NODES // GROUP
TAIL = N_NODES - D_GROUPS * GROUP
TAIL_P = TAIL // J
R_GROUPS = -(-(E_TILES + N_REL - 1) // J)
R_TILES = R_GROUPS * J
PAD_DST = 1 << 23
BN_EPS = 1e-5
LN_EPS = 1e-5
assert TAIL_P * J == TAIL and 2 * IN == P and HID == P


def at(ap, g):
    if isinstance(g, int):
        return ap[g]
    names = "abcdefg"[: len(ap.shape) - 1]
    spaced = " ".join(names)
    rest = " ".join(names[1:])
    return ap[bass.ds(g, 1)].rearrange(f"z {spaced} -> (z {names[0]}) {rest}")


def cols(ap, start, n):
    return ap[:, bass.ds(start, n)] if not isinstance(start, int) else ap[:, start:start + n]


def later(slot, turn, k, ring):
    return (slot + k) % ring, turn + (slot + k) // ring


def loop(eng, n, unroll, body):
    turns = n // unroll
    if turns > 1:
        with eng.Fori(0, turns) as turn:
            for slot in range(unroll):
                body(turn * unroll + slot, slot, turn)
        first = turns * unroll
    else:
        first = 0
    for g in range(first, n):
        body(g, g % unroll, g // unroll)


def tools(nc, ctx, block):
    sems = []

    def clear():
        nc.clear_and_free_semaphores(sems)
        nc.all_engine_barrier()
    ctx.callback(clear)

    def sb(name, shape, dt=F32):
        return ctx.enter_context(nc.sbuf_tensor(f"{block}_{name}", shape, dt))

    def psum(name, banks=1):
        return ctx.enter_context(nc.psum_tensor(f"{block}_{name}", [P, 512] if banks == 1 else [P, banks, 512], F32))

    def sem(name):
        sems.append(nc.alloc_semaphore(f"{block}_{name}"))
        return sems[-1]

    def ring(name, n=2):
        return [sem(f"{name}{i}") for i in range(n)]

    return sb, psum, sem, ring


def loop_from(eng, first, n, unroll, body):
    turns = (n - first) // unroll
    with eng.Fori(0, turns) as k:
        turn = k + first // unroll
        for slot in range(unroll):
            body(turn * unroll + slot, slot, turn)
    for g in range(first + turns * unroll, n):
        body(g, g % unroll, g // unroll)


class Steps:

    def __init__(self, eng, sem, base=0):
        self.eng, self.sem, self.base, self.n = eng, sem, base, 0

    def did(self, instruction):
        instruction.then_inc(self.sem, 1)
        self.n += 1
        return self.base + self.n

    def settle(self):
        self.eng.wait_ge(self.sem, self.base + self.n)


class RunSums:

    def __init__(self, makers, dst_rows, dst_col, prev_last, width):
        sb, psum, sem, ring = makers
        self.dst_rows, self.dst_col, self.prev_last, self.width = dst_rows, dst_col, prev_last, width
        self.dst_tile = sb("run_dst_tile", [P, 2, GROUP], I32)
        self.S = sb("run_S", [P, 2, J, P])
        self.Q = sb("run_Q", [P, 2, J, P])
        self.kept = sb("run_kept", [P, 2, width])
        self.sums = psum("run_sums", 2)
        self.loaded = [sem(f"run_loaded{i}") for i in range(2)]
        self.selected = sem("run_selected")
        self.summed = sem("run_summed")
        self.copied = sem("run_copied")
        self.scaled = sem("run_scaled")

    def load(self, eng, g, slot):
        row = self.dst_rows[g:g + 1] if isinstance(g, int) else self.dst_rows[bass.ds(g, 1)]
        eng.dma_start(self.dst_tile[:, slot, :], row.rearrange("a c -> (a c)").partition_broadcast(P))\
            .then_inc(self.loaded[slot], 16)

    def start_vector(self, eng):
        eng.memset(self.kept[:, 1, :], 0.0).then_inc(self.copied, 1)

    def select(self, eng, g, slot, turn):
        eng.wait_ge(self.loaded[slot], 16 * turn + 16)
        tile = self.dst_tile[:, slot, :].rearrange("p (j c) -> p j c", j=J)
        for to, col in ((self.S, self.dst_col), (self.Q, self.prev_last)):
            eng.tensor_tensor(to[:, slot], tile, cols(col, g * J, J).unsqueeze(2).to_broadcast([P, J, P]),
                              ALU.is_equal).then_inc(self.selected, 1)

    def add(self, eng, g, slot, j, message):
        t = g * J + j
        if j == 0:
            eng.wait_ge(self.selected, 2 * g + 2)
        to = self.sums[:, j % 2, 0:self.width]
        eng.matmul(to, self.S[:, slot, j, :], message, start=True, stop=False)
        eng.wait_ge(self.copied, t + 1)
        eng.matmul(to, self.Q[:, slot, j, :], self.kept[:, (j + 1) % 2, :], start=False, stop=True)\
            .then_inc(self.summed, 1)

    def keep(self, eng, g, j):
        eng.wait_ge(self.summed, g * J + j + 1)
        eng.wait_ge(self.scaled, g * J + j + 1)
        eng.tensor_copy(self.kept[:, j % 2, :], self.sums[:, j % 2, 0:self.width]).then_inc(self.copied, 1)

    def scale(self, eng, g, j, to, weight_col):
        eng.wait_ge(self.copied, g * J + j + 2)
        eng.activation(to, self.kept[:, j % 2, 0:to.shape[-1]], ACT.Copy,
                       scale=cols(weight_col, g * J + j, 1)).then_inc(self.scaled, 1)


def gnn_program(nc, x, src, dst, edge_type_32, Wl0, Wr0, b0, Wl1, Wr1, b1, Wl2, Wr2, b2,
                g0, be0, g1, be1, basis, coeff, self_weight, bias, out):
    persistent = ExitStack()

    def scratch(name, shape, dt=F32):
        return nc.dram_tensor(name, shape, dt).ap()

    dst_flat = scratch("dst_flat", [E_ROWS + P], I32)
    x_src = scratch("x_src", [E_GROUPS, P, J * IN])
    x_dst = scratch("x_dst", [E_GROUPS, P, J * IN])
    agg0 = scratch("agg0", [E_ROWS + 1, IN])
    agg1 = scratch("agg1", [E_ROWS + 1, HID])
    agg2 = scratch("agg2", [E_ROWS + 1, OUT])
    h0_src = scratch("h0_src", [E_GROUPS, P, GROUP])
    h0_dst = scratch("h0_dst", [E_GROUPS, P, GROUP])
    h1_dst = scratch("h1_dst", [E_GROUPS, P, GROUP])
    u_src = scratch("u_src", [E_GROUPS, P, J * OUT])
    u_dst = scratch("u_dst", [E_GROUPS, P, J * OUT])
    x1_by_rel = scratch("x1_by_rel", [R_TILES * P, OUT])
    msg_by_rel = scratch("msg_by_rel", [R_TILES * P, OUT])
    rel_weights = scratch("rel_weights", [N_REL, IN, OUT])

    def grouped(a, width):
        return a[0:E_ROWS].rearrange("(g p j) f -> g p (j f)", p=P, j=J)

    slot_home = scratch("slot_home", [P, E_TILES], I32)
    rel_home = scratch("rel_home", [P, E_TILES], I32)
    weight_home = scratch("weight_home", [P, R_TILES // 2], I32)
    out_home = scratch("out_home", [P, E_TILES], I32)

    agg0_g, agg1_g, agg2_g = grouped(agg0, IN), grouped(agg1, HID), grouped(agg2, OUT)
    dst_table = dst_flat[0:E_ROWS].rearrange("(t c) -> t c", c=P)
    dst_next = dst_flat[1:E_ROWS + 1].rearrange("(t c) -> t c", c=P)

    def keep(name, shape, dt=F32):
        return persistent.enter_context(nc.sbuf_tensor(name, shape, dt))

    with persistent:
        ident = keep("ident", [P, P])
        ones = keep("ones", [P, P])
        src_col = keep("src_col", [P, E_TILES])
        dst_col = keep("dst_col", [P, E_TILES])
        typ_col = keep("typ_col", [P, E_TILES])
        prev_last = keep("prev_last", [P, E_TILES])
        last_col = keep("last_col", [P, E_TILES])
        weight_col = keep("weight_col", [P, E_TILES])
        slot_idx = keep("slot_idx", [P, E_TILES], I32)
        rel_pos = keep("rel_pos", [P, E_TILES], I32)
        out_idx = keep("out_idx", [P, E_TILES], I32)
        W0 = keep("W0", [P, HID])
        W0_top = keep("W0_top", [P, HID])
        W0_bot = keep("W0_bot", [P, HID])
        Wr1T = keep("Wr1T", [P, HID])
        Wl1T = keep("Wl1T", [P, HID])
        W2_msg = keep("W2_msg", [P, 2 * OUT])
        U_h = keep("U_h", [P, 2 * OUT])
        U_x = keep("U_x", [P, 4 * OUT])
        Ws2 = keep("Ws2", [P, 2 * OUT])
        b2_pair = keep("b2_pair", [P, 1])
        b2_row = keep("b2_row", [P, OUT])
        bias_row = keep("bias_row", [P, OUT])
        biasC_row = keep("biasC_row", [P, OUT])
        bn = keep("bn", [P, 16])
        G0, BE0, B0, G1, BE1, B1 = (bn[:, i:i + 1] for i in range(6))
        SC0, SH0, SH0D, SC1, SH1 = (bn[:, i:i + 1] for i in range(6, 11))
        gram = keep("gram", [P, P])
        zsum = keep("zsum", [P, 1])
        is_127 = keep("is_127", [P, 1])

        with ExitStack() as ctx:
            sb, psum, sem, ring = makers = tools(nc, ctx, "layout")
            rows_i = sb("rows_i", [HALF, 4, 2, P], I32)
            rows_f = sb("rows_f", [HALF, 4, 2, P])
            wraw = sb("wraw", [P, 7, P])
            w2raw = sb("w2raw", [OUT, 2, HID])
            ws_sb = sb("ws_sb", [IN, OUT])
            coeff_sb = sb("coeff_sb", [N_REL, N_BASES])
            coeffT = sb("coeffT", [N_BASES, N_REL])
            basis_sb = sb("basis_sb", [N_BASES, IN * OUT])
            rw_sb = sb("rw_sb", [N_REL, IN * OUT])
            zeros = sb("zeros", [P, 2048])
            rsel = sb("rsel", [P, 4])
            idT = sb("idT", [IN, P])
            r2cT = sb("r2cT", [OUT, P])
            mean_c = sb("mean_c", [P, 4])
            p = [psum(f"p{i}") for i in range(8)]
            s_loaded, s_edges, s_weights = sem("s_loaded"), sem("s_edges"), sem("s_weights")
            s_dst_out, s_next, s_next_set = sem("s_dst_out"), sem("s_next"), sem("s_next_set")
            s_const, s_zero, s_zeroed, s_pool = sem("s_const"), sem("s_zero"), sem("s_zeroed"), sem("s_pool")
            s_dve, s_pe, s_rw, s_rw_out = sem("s_dve"), sem("s_pe"), sem("s_rw"), sem("s_rw_out")
            block = ctx.enter_context(nc.Block())
            FULL = N_EDGES // P
            REST = N_EDGES - FULL * P

            @block.gpsimd
            def _(eng):
                eng.memset(ident[:], 0.0).then_inc(s_pool, 1)
                eng.iota(rsel[:, 0:1].bitcast(I32), [[0, 1]], base=0, channel_multiplier=1).then_inc(s_pool, 1)
                eng.wait_ge(s_pool, 2)
                eng.affine_select(out=ident[:], in_=ident[:], compare_op=ALU.not_equal, fill=1.0,
                                  base=0, pattern=[[-1, P]], channel_multiplier=1).then_inc(s_const, 1)

            @block.sync
            def _(eng):
                eng.wait_ge(s_edges, 2)
                for n, a in enumerate((src, dst, edge_type_32)):
                    eng.dma_start(rows_i[:, n, 0, :], a[0:HALF * P].rearrange("(t c) -> t c", c=P)).then_inc(s_loaded, 16)
                    eng.dma_start(rows_i[0:FULL - HALF, n, 1, :],
                                  a[HALF * P:FULL * P].rearrange("(t c) -> t c", c=P)).then_inc(s_loaded, 16)
                    eng.dma_start(rows_i[FULL - HALF:FULL - HALF + 1, n, 1, 0:REST],
                                  a[FULL * P:N_EDGES].rearrange("(t c) -> t c", t=1)).then_inc(s_loaded, 16)
                eng.wait_ge(s_zero, 4)
                for d, s in ((wraw[:, 0, 0:IN], Wr0), (wraw[:, 0, IN:], Wl0), (wraw[:, 1, 0:IN], Wr0),
                             (wraw[:, 2, IN:], Wr0), (wraw[:, 3, :], Wr1), (wraw[:, 4, :], Wl1),
                             (w2raw[:, 0, :], Wl2), (w2raw[:, 1, :], Wr2), (ws_sb[:], self_weight),
                             (coeff_sb[:], coeff), (basis_sb[:], basis.rearrange("b i o -> b (i o)")),
                             (Ws2[0:IN, 0:OUT], self_weight), (Ws2[IN:P, OUT:], self_weight),
                             (b2_pair[0:IN], b2.rearrange("(p a) -> p a", a=1)),
                             (b2_pair[IN:P], b2.rearrange("(p a) -> p a", a=1)),
                             (b2_row[:], b2.partition_broadcast(P)), (bias_row[:], bias.partition_broadcast(P)),
                             (G0, g0.rearrange("(p a) -> p a", a=1)), (BE0, be0.rearrange("(p a) -> p a", a=1)),
                             (B0, b0.rearrange("(p a) -> p a", a=1)), (G1, g1.rearrange("(p a) -> p a", a=1)),
                             (BE1, be1.rearrange("(p a) -> p a", a=1)), (B1, b1.rearrange("(p a) -> p a", a=1))):
                    eng.dma_start(d, s).then_inc(s_weights, 16)
                eng.wait_ge(s_loaded, 16 * 9)
                eng.dma_start(dst_table[0:HALF], rows_i[:, 1, 0, :]).then_inc(s_dst_out, 16)
                eng.dma_start(dst_table[HALF:E_TILES], rows_i[:, 1, 1, :]).then_inc(s_dst_out, 16)
                eng.dma_start(dst_flat[E_ROWS:E_ROWS + P].rearrange("(t c) -> t c", t=1),
                              rows_i[HALF - 1:HALF, 3, 0, :]).then_inc(s_dst_out, 16)
                eng.wait_ge(s_dst_out, 48)
                eng.dma_start(rows_i[:, 3, 0, :], dst_next[0:HALF]).then_inc(s_next, 16)
                eng.dma_start(rows_i[:, 3, 1, :], dst_next[HALF:E_TILES]).then_inc(s_next, 16)
                for a in (agg0, agg1, agg2):
                    eng.dma_start(a[E_ROWS:E_ROWS + 1], zeros[0:1, 0:a.shape[1]]).then_inc(s_zeroed, 16)
                flat = x1_by_rel.rearrange("(p q) f -> p (q f)", p=P)
                width, n = flat.shape[1], 0
                for c in range(0, width, 2048):
                    w = min(2048, width - c)
                    eng.dma_start(flat[:, c:c + w], zeros[:, 0:w]).then_inc(s_zeroed, 16)
                    n += 1
                eng.wait_ge(s_rw, 8)
                eng.dma_start(rel_weights.rearrange("r i o -> r (i o)"), rw_sb[:]).then_inc(s_rw_out, 16)
                eng.wait_ge(s_zeroed, 16 * (3 + n))
                eng.wait_ge(s_rw_out, 16)

            @block.tensor
            def _(eng):
                t = Steps(eng, s_pe)
                eng.wait_ge(s_const, 1)
                eng.wait_ge(s_weights, 16 * 23)
                for n in range(4):
                    t.did(eng.transpose(p[0][:, n * P:(n + 1) * P], wraw[:, n, :], ident[:]))
                t.did(eng.transpose(p[1][:, 0:P], wraw[:, 4, :], ident[:]))
                for n in range(2):
                    t.did(eng.transpose(p[1][:, P + n * OUT:P + (n + 1) * OUT], w2raw[:, n, :], ident[0:OUT, 0:OUT]))
                t.did(eng.transpose(p[1][0:N_BASES, 256:256 + N_REL], coeff_sb[:], ident[0:N_REL, 0:N_REL]))
                eng.wait_ge(s_next_set, 1)
                for n in range(4):
                    for h in range(2):
                        t.did(eng.transpose(p[2 + n][:, h * HALF:(h + 1) * HALF], rows_f[:, n, h, :],
                                            ident[0:HALF, 0:HALF]))
                eng.wait_ge(s_dve, 8)
                for c in range(8):
                    if c >= 2:
                        eng.wait_ge(s_rw, c - 1)
                    t.did(eng.matmul(p[6 + c % 2][0:N_REL, :], coeffT[:], basis_sb[:, c * 512:(c + 1) * 512],
                                     start=True, stop=True))
                eng.wait_ge(s_dve, 13)
                t.did(eng.matmul(p[0][:, 0:OUT], idT[:], ws_sb[:], start=True, stop=True))
                t.did(eng.transpose(p[1][0:OUT, 0:P], U_h[:, 0:OUT], ident[:]))
                eng.wait_ge(s_dve, 14)
                t.did(eng.matmul(p[0][:, OUT:2 * OUT], r2cT[:], ws_sb[:], start=True, stop=True))

            @block.vector
            def _(eng):
                eng.memset(rows_i[:], 0).then_inc(s_edges, 1)
                eng.wait_ge(s_edges, 1)
                eng.memset(rows_i[:, 1:4:2, :, :], PAD_DST).then_inc(s_edges, 1)
                eng.memset(wraw[:], 0.0).then_inc(s_zero, 1)
                eng.memset(Ws2[:], 0.0).then_inc(s_zero, 1)
                eng.memset(zeros[:], 0.0).then_inc(s_zero, 1)
                eng.memset(ones[:], 1.0).then_inc(s_zero, 1)
                eng.wait_ge(s_loaded, 16 * 9)
                eng.wait_ge(s_next, 32)
                eng.tensor_copy(rows_f[:], rows_i[:]).then_inc(s_next_set, 1)
                t = Steps(eng, s_dve)
                eng.wait_ge(s_pe, 8)
                for n, w in enumerate((W0, W0_top, W0_bot, Wr1T)):
                    t.did(eng.tensor_copy(w[:], p[0][:, n * P:(n + 1) * P]))
                t.did(eng.tensor_copy(Wl1T[:], p[1][:, 0:P]))
                t.did(eng.tensor_copy(W2_msg[:], p[1][:, P:2 * P]))
                t.did(eng.tensor_copy(coeffT[:], p[1][0:N_BASES, 256:256 + N_REL]))
                t.did(eng.tensor_reduce(mean_c[:, 0:1], p[1][:, P + OUT:2 * P], AX.X, ALU.add))
                t.settle()
                t.did(eng.tensor_scalar(mean_c[:, 0:1], mean_c[:, 0:1], -1.0 / OUT, None, ALU.mult))
                t.settle()
                t.did(eng.tensor_scalar(U_h[:, 0:OUT], W2_msg[:, OUT:], mean_c[:, 0:1], None, ALU.add))
                for h in range(2):
                    t.did(eng.tensor_scalar(idT[:, h * OUT:(h + 1) * OUT], ident[0:OUT, 0:OUT], -1.0 / OUT, None, ALU.add))
                t.did(eng.memset(U_x[:], 0.0))
                eng.wait_ge(s_pe, 26)
                t.did(eng.tensor_copy(r2cT[:], p[1][0:OUT, 0:P]))
                t.settle()
                for h in range(2):
                    q = slice(h * IN, (h + 1) * IN)
                    t.did(eng.tensor_scalar(U_x[q, h * P:h * P + OUT], ident[q, q], -1.0 / OUT, None, ALU.add))
                eng.wait_ge(s_pe, 27)
                t.settle()
                t.did(eng.tensor_tensor(U_h[:, OUT:], U_h[:, 0:OUT], p[0][:, OUT:2 * OUT], ALU.add))
                for h in range(2):
                    q = slice(h * IN, (h + 1) * IN)
                    t.did(eng.tensor_tensor(U_x[q, h * P + OUT:(h + 1) * P], U_x[q, h * P:h * P + OUT],
                                            p[0][q, 0:OUT], ALU.add))
                t.settle()
                t.did(eng.tensor_reduce(mean_c[:, 1:2], U_h[:, OUT:], AX.X, ALU.add))
                for h in range(2):
                    q = slice(h * IN, (h + 1) * IN)
                    t.did(eng.tensor_reduce(mean_c[q, 2:3], U_x[q, h * P + OUT:(h + 1) * P], AX.X, ALU.add))
                t.did(eng.tensor_reduce(mean_c[:, 3:4], bias_row[:], AX.X, ALU.add))
                t.settle()
                t.did(eng.tensor_scalar(mean_c[:], mean_c[:], -1.0 / OUT, None, ALU.mult))
                t.settle()
                t.did(eng.tensor_scalar(U_h[:, OUT:], U_h[:, OUT:], mean_c[:, 1:2], None, ALU.add))
                for h in range(2):
                    q = slice(h * IN, (h + 1) * IN)
                    ux = U_x[q, h * P + OUT:(h + 1) * P]
                    t.did(eng.tensor_scalar(ux, ux, mean_c[q, 2:3], None, ALU.add))
                t.did(eng.tensor_scalar(biasC_row[:], bias_row[:], mean_c[:, 3:4], None, ALU.add))
                eng.wait_ge(s_pe, 16)
                t.did(eng.tensor_copy(src_col[:], p[2][:, 0:E_TILES]))
                t.did(eng.tensor_copy(dst_col[:], p[3][:, 0:E_TILES]))
                t.did(eng.tensor_copy(typ_col[:], p[4][:, 0:E_TILES]))
                t.did(eng.tensor_copy(rsel[:, 1:2], rsel[:, 0:1].bitcast(I32)))
                t.settle()
                t.did(eng.tensor_tensor(last_col[:], dst_col[:], p[5][:, 0:E_TILES], ALU.not_equal))
                t.did(eng.tensor_scalar(prev_last[:], dst_col[:], float(N_NODES), None, ALU.is_lt))
                t.did(eng.tensor_scalar(is_127[:], rsel[:, 1:2], float(P - 1), None, ALU.is_equal))
                t.settle()
                t.did(eng.tensor_tensor(last_col[:], last_col[:], prev_last[:], ALU.mult))
                t.settle()
                t.did(eng.memset(prev_last[:, 0:1], -1.0))
                t.did(eng.tensor_scalar(prev_last[:, 1:], dst_col[:, 0:E_TILES - 1], 1.0, is_127[:],
                                        ALU.add, ALU.mult))
                t.settle()
                t.did(eng.tensor_scalar(prev_last[:, 1:], prev_last[:, 1:], -1.0, None, ALU.add))
                t.did(eng.tensor_scalar(weight_col[:], dst_col[:], -float(PAD_DST), None, ALU.add))
                t.settle()
                t.did(eng.tensor_tensor(weight_col[:], weight_col[:], last_col[:], ALU.mult))
                t.settle()
                t.did(eng.tensor_scalar(out_idx[:], weight_col[:], float(PAD_DST), None, ALU.add))
                t.settle()

            @block.scalar
            def _(eng):
                for c in range(8):
                    eng.wait_ge(s_pe, 17 + c)
                    eng.activation(rw_sb[:, c * 512:(c + 1) * 512], p[6 + c % 2][0:N_REL, :], ACT.Copy).then_inc(s_rw, 1)

        RING = 4
        DRING = 8
        with ExitStack() as ctx:
            sb, psum, sem, ring = makers = tools(nc, ctx, "lookup")
            xd = sb("xd", [P, DRING, J * IN])
            xg = sb("xg", [P, RING, J * IN])
            tab = sb("tab", [P, RING, J, P], I32)
            idx = sb("idx", [P, 3, RING, J], I32)
            dst_in = sb("dst_in", [P, E_TILES])
            tile_first = sb("tile_first", [P, E_TILES])
            tile_of = sb("tile_of", [P, E_TILES])
            tile_i = sb("tile_i", [P, 2, E_TILES], I32)
            tile_f = sb("tile_f", [P, 2, E_TILES])
            hit = sb("hit", [P, E_TILES])
            less = sb("less", [P, E_TILES])
            junk = sb("junk", [P, J, E_TILES])
            number = sb("number", [P, P])
            match = sb("match", [P, 2, J, P])
            before = sb("before", [P, P])
            sel_row = sb("sel_row", [P, P])
            ramp = sb("ramp", [P, R_TILES], I32)
            ramp_f = sb("ramp_f", [P, R_TILES])
            hot = sb("hot", [P, N_REL, E_TILES])
            within = sb("within", [P, N_REL, E_TILES])
            count = sb("count", [P, N_REL, E_TILES])
            upto = sb("upto", [P, N_REL, E_TILES])
            rel = sb("rel", [P, 8, N_REL])
            rel_i = sb("rel_i", [P, N_REL], I32)
            part_id = sb("part_id", [P, 2], I32)
            cmp = sb("cmp", [P, R_TILES // 2, N_REL])
            rel_of = sb("rel_of", [P, R_TILES])
            rel_start = sb("rel_start", [P, 2])
            weight_row = sb("weight_row", [P, R_TILES // 2], I32)
            xsum = sb("xsum", [P, IN])
            zero = sb("zero", [P, 256])
            pGram = psum("pGram")
            pSum = psum("pSum")
            pFirst = psum("pFirst")
            pRel = psum("pRel", 4)
            s_const, s_dve = sem("s_const"), sem("s_dve")
            d_free, d_gram = sem("d_free"), sem("d_gram")
            d_loaded = [sem(f"d_loaded{i}") for i in range(DRING)]
            s_first, s_in = sem("s_first"), sem("s_in")
            s_hot, s_rel, s_rel_got = sem("s_hot"), sem("s_rel"), sem("s_rel_got")
            s_tile = sem("s_tile")
            idx_ready = [sem(f"idx_ready{i}") for i in range(3)]
            got = [[sem(f"got{w}_{i}") for i in range(RING)] for w in range(3)]
            kept = [[sem(f"kept{w}_{i}") for i in range(RING)] for w in range(2)]
            s_begun, s_matched = sem("s_begun"), sem("s_matched")
            s_count, s_hit = sem("s_count"), sem("s_hit")
            s_slots, s_homes = sem("s_slots"), sem("s_homes")
            block = ctx.enter_context(nc.Block())
            x_dense = x[0:D_GROUPS * GROUP].rearrange("(g p q) f -> g p (q f)", p=P, q=J)
            x_tail = x[D_GROUPS * GROUP:N_NODES].rearrange("(p q) f -> p (q f)", q=J)
            hot_flat, within_flat, count_flat = (a[:].rearrange("p r t -> p (r t)") for a in (hot, within, count))
            WIDTH = N_REL * E_TILES
            CHUNKS = [(c, min(512, WIDTH - c)) for c in range(0, WIDTH, 512)]

            @block.sync
            def _(eng):
                def load(g, slot, turn):
                    eng.wait_ge(d_free, g + 1)
                    eng.dma_start(xd[:, slot, :], at(x_dense, g)).then_inc(d_loaded[slot], 16)
                loop(eng, D_GROUPS, DRING, load)
                eng.wait_ge(d_free, D_GROUPS + 1)
                slot = D_GROUPS % DRING
                eng.dma_start(xd[0:TAIL_P, slot, :], x_tail).then_inc(d_loaded[slot], 16)
                eng.dma_start(out_home, out_idx[:]).then_inc(s_homes, 16)
                eng.wait_ge(s_slots, 1)
                eng.dma_start(rel_home, rel_pos[:]).then_inc(s_homes, 16)
                eng.dma_start(weight_home, weight_row[:]).then_inc(s_homes, 16)
                eng.dma_start(slot_home, slot_idx[:]).then_inc(s_homes, 16)
                eng.wait_ge(s_homes, 64)

            @block.gpsimd
            def _(eng):
                eng.iota(ramp[:], [[1, R_TILES]], base=0, channel_multiplier=0).then_inc(s_const, 1)
                eng.memset(before[:], 0.0).then_inc(s_const, 1)
                for h in range(2):
                    eng.iota(part_id[:, h:h + 1], [[0, 1]], base=-IN * h, channel_multiplier=1).then_inc(s_const, 1)
                eng.wait_ge(s_const, 4)
                eng.affine_select(out=before[:], in_=before[:], compare_op=ALU.is_ge, fill=1.0,
                                  base=0, pattern=[[-1, P]], channel_multiplier=1).then_inc(s_const, 1)
                for w in range(2):
                    def gather_x(g, slot, turn, w=w):
                        eng.wait_ge(idx_ready[w], g + 1)
                        eng.sem_inc(s_begun, 1)
                        for j in range(J):
                            eng.indirect_dma_start(
                                xg[:, slot, j * IN:(j + 1) * IN], None, x,
                                bass.IndirectOffsetOnAxis(ap=idx[:, w, slot, j:j + 1], axis=0)).then_inc(got[w][slot], 16)
                    loop(eng, E_GROUPS, RING, gather_x)

                def gather_dst(g, slot, turn):
                    eng.wait_ge(idx_ready[2], g + 1)
                    eng.sem_inc(s_begun, 1)
                    for j in range(J):
                        eng.indirect_dma_start(
                            tab[:, slot, j, :], None, dst_table,
                            bass.IndirectOffsetOnAxis(ap=idx[:, 2, slot, j:j + 1], axis=0)).then_inc(got[2][slot], 16)
                loop(eng, E_GROUPS, RING, gather_dst)

            @block.scalar
            def _(eng):
                for slot in range(RING):
                    eng.sem_inc(kept[0][slot], 16)
                for w, column, home in ((0, src_col, x_src), (1, dst_in, x_dst)):
                    if w == 1:
                        eng.wait_ge(s_in, 1)
                        for slot in range(RING):
                            turns = len(range(slot, E_GROUPS, RING))
                            eng.wait_ge(kept[0][slot], 16 * turns + 16)
                            eng.sem_inc(kept[1][slot], 16)

                    def stage(g, slot, w=w, column=column):
                        eng.activation(idx[:, w, slot, :], cols(column, g * J, J), ACT.Copy).then_inc(idx_ready[w], 1)

                    def store(g, slot, turn, w=w, home=home):
                        eng.wait_ge(got[w][slot], 16 * J * turn + 16 * J)
                        eng.dma_start(at(home, g), xg[:, slot, :]).then_inc(kept[w][slot], 16)

                    def both(g, slot, turn):
                        store(g, slot, turn)
                        ahead = (slot + 2) % RING
                        eng.wait_ge(kept[w][ahead], 16 * (turn + (slot + 2) // RING) + 16)
                        stage(g + 2, ahead)
                    stage(0, 0)
                    stage(1, 1)
                    loop(eng, E_GROUPS - 2, RING, both)
                    for g in range(E_GROUPS - 2, E_GROUPS):
                        store(g, g % RING, g // RING)

                eng.wait_ge(s_tile, 1)

                def stage_tile(g, slot, turn):
                    eng.wait_ge(s_matched, g + 1)
                    eng.activation(idx[:, 2, slot, :], cols(tile_of, g * J, J), ACT.Copy).then_inc(idx_ready[2], 1)
                loop(eng, E_GROUPS, RING, stage_tile)
                for slot in range(RING):
                    eng.wait_ge(kept[1][slot], 16 * len(range(slot, E_GROUPS, RING)) + 16)

            @block.tensor
            def _(eng):
                eng.wait_ge(s_dve, 3)
                eng.matmul(pFirst[:, 0:E_TILES], sel_row[:], dst_col[:], start=True, stop=True).then_inc(s_first, 1)
                eng.matmul(pGram[0:IN, 0:IN], zero[:, 0:IN], zero[:, 0:IN], start=True, stop=False)
                eng.matmul(pSum[:, 0:J * IN], zero[:, 0:P], zero[:], start=True, stop=False)
                eng.sem_inc(d_free, DRING)

                def add(g, slot, turn, p=P, last=False):
                    eng.wait_ge(d_loaded[slot], 16 * turn + 16)
                    for q in range(J):
                        rows = xd[0:p, slot, q * IN:(q + 1) * IN]
                        eng.matmul(pGram[0:IN, 0:IN], rows, rows, start=False, stop=last and q == J - 1)
                    eng.matmul(pSum[:, 0:J * IN], ones[0:p, :], xd[0:p, slot, :], start=False,
                               stop=last).then_inc(d_free, 1)
                loop(eng, D_GROUPS, DRING, add)
                add(D_GROUPS, D_GROUPS % DRING, D_GROUPS // DRING, TAIL_P, True)
                eng.wait_ge(s_hot, 1)
                eng.wait_ge(s_const, 5)
                for n, (c, w) in enumerate(CHUNKS):
                    if n >= 2:
                        eng.wait_ge(s_rel_got, 2 * (n - 1))
                    eng.matmul(pRel[:, n % 2, 0:w], before[:], hot_flat[:, c:c + w], start=True, stop=True).then_inc(s_rel, 1)
                    eng.matmul(pRel[:, 2 + n % 2, 0:w], ones[:], hot_flat[:, c:c + w], start=True, stop=True).then_inc(s_rel, 1)

            @block.vector
            def _(eng):
                t = Steps(eng, s_dve)
                t.did(eng.memset(zero[:], 0.0))
                t.did(eng.memset(sel_row[:], 1.0))
                t.settle()
                t.did(eng.tensor_scalar(sel_row[:], sel_row[:], ident[:, 0:1], None, ALU.mult))
                eng.tensor_scalar(dst_in[:], dst_col[:], float(N_NODES - 1), None, ALU.min).then_inc(s_in, 1)
                eng.wait_ge(s_const, 5)
                t.did(eng.tensor_copy(ramp_f[:], ramp[:]))
                t.settle()
                t.did(eng.tensor_scalar(number[:], ramp_f[:, 0:P], 1.0, None, ALU.add))
                eng.wait_ge(s_first, 1)
                t.did(eng.tensor_copy(tile_first[:], pFirst[:, 0:E_TILES]))
                t.settle()

                def below(g, slot, turn):
                    for j in range(J):
                        eng.wait_ge(s_count, g * J + j + 1)
                        eng.tensor_scalar(junk[:, j, :], tile_first[:], cols(src_col, g * J + j, 1), 0.0,
                                          ALU.is_le, ALU.add, accum_out=cols(tile_of, g * J + j, 1)).then_inc(s_count, 1)
                eng.sem_inc(s_count, J)
                loop(eng, E_GROUPS, 1, below)
                eng.wait_ge(s_count, J + E_TILES)
                t.did(eng.tensor_scalar(tile_of[:], tile_of[:], -1.0, 0.0, ALU.add, ALU.max))
                t.settle()
                eng.tensor_copy(tile_i[:, 0, :], tile_of[:]).then_inc(s_tile, 1)
                eng.sem_inc(s_matched, RING)
                relid = ramp_f[:, 0:N_REL].unsqueeze(2).to_broadcast([P, N_REL, E_TILES])
                eng.tensor_tensor(hot[:], typ_col[:].unsqueeze(1).to_broadcast([P, N_REL, E_TILES]), relid,
                                  ALU.is_equal).then_inc(s_hot, 1)
                for n, (c, w) in enumerate(CHUNKS):
                    eng.wait_ge(s_rel, 2 * n + 1)
                    eng.tensor_copy(within_flat[:, c:c + w], pRel[:, n % 2, 0:w]).then_inc(s_rel_got, 1)
                    eng.wait_ge(s_rel, 2 * n + 2)
                    eng.tensor_copy(count_flat[:, c:c + w], pRel[:, 2 + n % 2, 0:w]).then_inc(s_rel_got, 1)
                eng.wait_ge(s_rel_got, 2 * len(CHUNKS))
                upto_flat = upto[:].rearrange("p r t -> p (r t)")
                t.did(eng.tensor_tensor_scan(upto_flat, ones[:, 0:1].to_broadcast([P, WIDTH]), count_flat, 0.0,
                                             ALU.mult, ALU.add))
                t.settle()
                ends, starts, size, pends, pstarts, shift = (rel[:, i, :] for i in range(6))
                t.did(eng.tensor_copy(ends, upto[:, :, E_TILES - 1]))
                t.did(eng.memset(starts[:, 0:1], 0.0))
                t.did(eng.memset(pstarts[:, 0:1], 0.0))
                t.settle()
                t.did(eng.tensor_copy(starts[:, 1:], ends[:, 0:N_REL - 1]))
                t.settle()
                t.did(eng.tensor_tensor(size, ends, starts, ALU.subtract))
                t.settle()
                t.did(eng.tensor_scalar(rel_i[:], size, float(P - 1), None, ALU.add))
                t.settle()
                t.did(eng.tensor_scalar(rel_i[:], rel_i[:], 7, 7, ALU.arith_shift_right, ALU.logical_shift_left))
                t.settle()
                t.did(eng.tensor_copy(size, rel_i[:]))
                t.settle()
                t.did(eng.tensor_tensor_scan(pends, ones[:, 0:N_REL], size, 0.0, ALU.mult, ALU.add))
                t.settle()
                t.did(eng.tensor_copy(pstarts[:, 1:], pends[:, 0:N_REL - 1]))
                t.settle()
                t.did(eng.tensor_tensor(shift, pstarts, starts, ALU.subtract))
                t.did(eng.tensor_tensor(upto[:], upto[:], count[:], ALU.subtract))
                t.settle()
                t.did(eng.tensor_tensor(within[:], within[:], upto[:], ALU.add))
                t.settle()
                t.did(eng.tensor_tensor(within[:], within[:], shift.unsqueeze(2).to_broadcast([P, N_REL, E_TILES]), ALU.add))
                t.settle()
                t.did(eng.tensor_tensor(within[:], within[:], hot[:], ALU.mult))
                t.settle()
                t.did(eng.tensor_reduce(hit[:], within[:].rearrange("p r t -> p t r"), AX.X, ALU.add))
                t.settle()
                t.did(eng.tensor_copy(rel_pos[:], hit[:]))
                t.did(eng.tensor_scalar(ramp_f[:], ramp_f[:], float(P), None, ALU.mult))
                t.settle()
                for h in range(2):
                    part = slice(h * R_TILES // 2, (h + 1) * R_TILES // 2)
                    shape = [P, R_TILES // 2, N_REL]
                    t.did(eng.tensor_tensor(cmp[:], pends.unsqueeze(1).to_broadcast(shape),
                                            ramp_f[:, part].unsqueeze(2).to_broadcast(shape), ALU.is_le))
                    t.settle()
                    t.did(eng.tensor_reduce(rel_of[:, part], cmp[:], AX.X, ALU.add))
                    t.settle()
                t.did(eng.tensor_scalar(rel_of[:], rel_of[:], float(N_REL - 1), float(IN), ALU.min, ALU.mult))
                t.did(eng.tensor_copy(rel_start[:], part_id[:]))
                t.settle()
                for h in range(2):
                    q = slice(h * IN, (h + 1) * IN)
                    t.did(eng.tensor_scalar(weight_row[q], rel_of[q].rearrange("p (m h) -> p m h", h=2)[:, :, h],
                                            rel_start[q, h:h + 1], None, ALU.add))
                before_search = t.n

                def search(g, slot, turn):
                    eng.wait_ge(got[2][slot], 16 * J * turn + 16 * J)
                    for j in range(J):
                        ins = eng.scalar_tensor_tensor(match[:, slot % 2, j, :], tab[:, slot, j, :],
                                                       cols(src_col, g * J + j, 1), number[:], ALU.is_equal, ALU.mult)
                    ins.then_inc(s_matched, 1)
                    eng.wait_ge(s_matched, g + 1 + RING)
                    eng.tensor_reduce(cols(hit, g * J, J), match[:, slot % 2, :, :], AX.X, ALU.max).then_inc(s_hit, 1)
                eng.wait_ge(s_dve, before_search)
                loop(eng, E_GROUPS, RING, search)
                eng.wait_ge(s_hit, E_GROUPS)
                t.did(eng.tensor_scalar(tile_i[:, 1, :], tile_i[:, 0, :], J - 1, None, ALU.bitwise_and))
                t.settle()
                t.did(eng.tensor_scalar(tile_i[:, 0, :], tile_i[:, 0, :], 2, 9, ALU.arith_shift_right, ALU.logical_shift_left))
                t.did(eng.tensor_scalar(less[:], hit[:], 0.0, None, ALU.is_gt))
                t.settle()
                t.did(eng.tensor_copy(tile_f[:], tile_i[:]))
                t.did(eng.tensor_scalar(hit[:], hit[:], -1.0, float(J), ALU.add, ALU.mult))
                t.settle()
                t.did(eng.tensor_tensor(hit[:], hit[:], tile_f[:, 0, :], ALU.add))
                t.settle()
                t.did(eng.tensor_tensor(hit[:], hit[:], tile_f[:, 1, :], ALU.add))
                t.settle()
                t.did(eng.tensor_scalar(hit[:], hit[:], -float(ZERO_ROW), None, ALU.add))
                t.settle()
                t.did(eng.tensor_tensor(hit[:], hit[:], less[:], ALU.mult))
                t.settle()
                eng.tensor_scalar(slot_idx[:], hit[:], float(ZERO_ROW), None, ALU.add).then_inc(s_slots, 1)
                eng.wait_ge(d_free, DRING + D_GROUPS + 1)
                t.did(eng.tensor_copy(gram[0:IN, 0:IN], pGram[0:IN, 0:IN]))
                t.did(eng.tensor_reduce(xsum[:], pSum[:, 0:J * IN].rearrange("p (q f) -> p f q", q=J), AX.X, ALU.add))
                t.settle()
                t.did(eng.tensor_tensor(xsum[0:IN], xsum[0:IN], ident[0:IN, 0:IN], ALU.mult))
                t.settle()
                t.did(eng.tensor_reduce(zsum[0:IN], xsum[0:IN], AX.X, ALU.add))
                t.settle()

        dst_rows = dst_flat[0:E_ROWS].rearrange("(g c) -> g c", c=GROUP)
        with ExitStack() as ctx:
            sb, psum, sem, ring = makers = tools(nc, ctx, "agg0")
            runs = RunSums(makers, dst_rows, dst_col, prev_last, IN + 1)
            xs = sb("xs", [P, 2, J, IN + 1])
            Z = sb("Z", [P, 2, J, P + 1])
            wy = sb("wy", [P, HID + 1])
            recip = sb("recip", [P, J])
            st = sb("st", [P, 8])
            pZ = psum("pZ")
            pBN = psum("pBN")
            z_loaded = [sem(f"z_loaded{i}") for i in range(2)]
            z_stored = [sem(f"z_stored{i}") for i in range(2)]
            s_ones, s_weighed, s_gram = sem("s_ones"), sem("s_weighed"), sem("s_gram")
            s_dve, s_pe, s_recip = sem("s_dve"), sem("s_pe"), sem("s_recip")
            s_var, s_std = sem("s_var"), sem("s_std")
            block = ctx.enter_context(nc.Block())

            @block.sync
            def _(eng):
                def load(g, slot):
                    runs.load(eng, g, slot)
                    eng.dma_start(xs[:, slot, :, 0:IN], at(x_src, g).rearrange("p (j f) -> p j f", j=J))\
                        .then_inc(z_loaded[slot], 16)
                    eng.dma_start(Z[:, slot, :, 0:IN], at(x_dst, g).rearrange("p (j f) -> p j f", j=J))\
                        .then_inc(z_loaded[slot], 16)

                def store(g, slot):
                    eng.wait_ge(runs.scaled, J * g + J + 2)
                    eng.dma_start(at(agg0_g, g).rearrange("p (j f) -> p j f", j=J), Z[:, slot, :, IN:P])\
                        .then_inc(z_stored[slot], 16)

                def both(g, slot, turn):
                    store(g, slot)
                    eng.wait_ge(s_gram, g + 1)
                    load(g + 2, slot)
                load(0, 0)
                load(1, 1)
                loop(eng, E_GROUPS - 2, 2, both)
                for g in range(E_GROUPS - 2, E_GROUPS):
                    store(g, g % 2)
                for slot in range(2):
                    eng.wait_ge(z_stored[slot], 16 * len(range(slot, E_GROUPS, 2)) + 16)

            @block.tensor
            def _(eng):
                eng.wait_ge(s_ones, 3)
                eng.matmul(pZ[:, 0:P + 1], wy[:, 0:P], wy[:], start=True, stop=False)

                def group(g, slot, turn, last=False):
                    def gram_of(j):
                        eng.wait_ge(runs.scaled, g * J + j + 3)
                        rows = Z[:, slot, j, :]
                        return eng.matmul(pZ[:, 0:P + 1], rows[:, 0:P], rows, start=False, stop=last and j == J - 1)
                    eng.wait_ge(z_loaded[slot], 32 * turn + 32)
                    for j in range(J):
                        runs.add(eng, g, slot, j, xs[:, slot, j, :])
                        if j:
                            gram_of(j - 1)
                    gram_of(J - 1).then_inc(s_gram, 1)
                loop(eng, E_GROUPS - 1, 2, group)
                group(E_GROUPS - 1, (E_GROUPS - 1) % 2, (E_GROUPS - 1) // 2, True)
                t = Steps(eng, s_pe)
                eng.wait_ge(s_dve, 4)
                t.did(eng.matmul(pBN[:, 0:HID], gram[:], W0[:], start=True, stop=True))
                t.did(eng.matmul(pBN[:, HID:HID + 1], W0[:], zsum[:], start=True, stop=True))
                t.did(eng.matmul(pBN[:, HID + 1:HID + 2], W0_top[:], b2_pair[:], start=True, stop=True))
                eng.wait_ge(s_dve, 5)
                t.did(eng.matmul(pBN[:, HID + 2:HID + 3], wy[:, 0:HID], ones[:, 0:1], start=True, stop=True))

            @block.scalar
            def _(eng):
                for slot in range(2):
                    eng.sem_inc(z_stored[slot], 16)
                eng.sem_inc(runs.scaled, 2)

                def group(g, slot, turn):
                    eng.wait_ge(z_stored[slot], 16 * turn + 16)
                    for j in range(J):
                        eng.wait_ge(s_weighed, g * J + j + 1)
                        runs.scale(eng, g, j, Z[:, slot, j, IN:P], weight_col)
                loop(eng, E_GROUPS, 2, group)
                eng.wait_ge(s_var, 1)
                eng.activation(st[:, 4:5], st[:, 2:3], ACT.Sqrt).then_inc(s_std, 1)

            @block.vector
            def _(eng):
                eng.memset(xs[:, :, :, IN:], 1.0).then_inc(s_ones, 1)
                eng.memset(Z[:, :, :, P:], 1.0).then_inc(s_ones, 1)
                eng.memset(wy[:], 0.0).then_inc(s_ones, 1)
                runs.start_vector(eng)

                def group(g, slot, turn):
                    runs.select(eng, g, slot, turn)
                    for j in range(J):
                        runs.keep(eng, g, j)
                        eng.reciprocal(recip[:, j:j + 1], runs.sums[:, j % 2, IN:IN + 1]).then_inc(s_recip, 1)
                        eng.wait_ge(s_recip, g * J + j + 1)
                        eng.tensor_tensor(cols(weight_col, g * J + j, 1), cols(last_col, g * J + j, 1),
                                          recip[:, j:j + 1], ALU.mult).then_inc(s_weighed, 1)
                loop(eng, E_GROUPS, 2, group)
                t = Steps(eng, s_dve)
                eng.wait_ge(s_gram, E_GROUPS)
                t.did(eng.tensor_copy(gram[0:IN, IN:P], pZ[0:IN, IN:P]))
                t.did(eng.tensor_copy(gram[IN:P, :], pZ[IN:P, 0:P]))
                t.did(eng.tensor_copy(zsum[IN:P], pZ[IN:P, P:P + 1]))
                t.settle()
                t.did(eng.memset(st[:], 0.0))
                eng.wait_ge(s_pe, 3)
                t.did(eng.tensor_tensor(wy[:, 0:HID], W0[:], pBN[:, 0:HID], ALU.mult))
                mean, ex2, var, tmp = (st[:, i:i + 1] for i in range(4))
                eng.wait_ge(s_pe, 4)
                t.settle()
                t.did(eng.tensor_scalar(mean, pBN[:, HID:HID + 1], 1.0 / N_NODES, None, ALU.mult))
                t.did(eng.tensor_scalar(ex2, pBN[:, HID + 2:HID + 3], 1.0 / N_NODES, None, ALU.mult))
                t.settle()
                t.did(eng.tensor_tensor(var, mean, mean, ALU.mult))
                t.settle()
                t.did(eng.tensor_tensor(var, ex2, var, ALU.subtract))
                t.settle()
                eng.tensor_scalar(var, var, 0.0, BN_EPS, ALU.max, ALU.add).then_inc(s_var, 1)
                eng.wait_ge(s_std, 1)
                t.did(eng.reciprocal(var, st[:, 4:5]))
                t.settle()
                t.did(eng.tensor_tensor(SC0, G0, var, ALU.mult))
                t.did(eng.tensor_tensor(tmp, mean, B0, ALU.add))
                t.settle()
                t.did(eng.tensor_tensor(tmp, B0, tmp, ALU.subtract))
                t.settle()
                t.did(eng.tensor_tensor(tmp, tmp, SC0, ALU.mult))
                t.settle()
                t.did(eng.tensor_tensor(SH0, BE0, tmp, ALU.add))
                t.settle()
                t.did(eng.tensor_tensor(tmp, SC0, pBN[:, HID + 1:HID + 2], ALU.mult))
                t.settle()
                t.did(eng.tensor_tensor(SH0D, SH0, tmp, ALU.subtract))
                t.settle()

        statD = keep("statD", [P, (D_GROUPS + 1) * 6])
        with ExitStack() as ctx:
            sb, psum, sem, ring = makers = tools(nc, ctx, "layer1")
            runs = RunSums(makers, dst_rows, dst_col, prev_last, HID)
            xd = sb("xd", [P, DRING, J * IN])
            xT = sb("xT", [P, 2, GROUP // 2])
            h0d = sb("h0d", [P, 2, GROUP])
            Z = sb("Z", [P, 2, J, P])
            idx = sb("idx", [P, 2, J], I32)
            zT = sb("zT", [P, GROUP])
            h0e = sb("h0e", [P, 2, GROUP])
            msg = sb("msg", [P, 2, J, HID])
            agg_out = sb("agg_out", [P, 2, J * HID])
            pXT, pH0, pH1, pZT, pHE, pM = (psum(n) for n in ("pXT", "pH0", "pH1", "pZT", "pHE", "pM"))
            d_loaded = ring("d_loaded", DRING)
            d_transposed, d_xT, d_h0, d_relu, d_h1, d_stats = (
                sem(n) for n in ("d_transposed", "d_xT", "d_h0", "d_relu", "d_h1", "d_stats"))
            x_loaded, i_loaded, gathered = ring("x_loaded"), ring("i_loaded"), ring("gathered")
            h0_stored, agg_stored = ring("h0_stored"), ring("agg_stored")
            e_transposed, e_zT, e_h0, e_relu, e_msgT, e_msg = (
                sem(n) for n in ("e_transposed", "e_zT", "e_h0", "e_relu", "e_msgT", "e_msg"))
            s_begun = sem("s_begun")
            block = ctx.enter_context(nc.Block())
            LAST = E_GROUPS - 1
            assert E_GROUPS * J == D_GROUPS + 1

            def rows_of(d):
                return TAIL_P if isinstance(d, int) and d == D_GROUPS else P

            @block.sync
            def _(eng):
                def load_rows(h, slot):
                    eng.dma_start(idx[:, slot, :], cols(slot_home, h * J, J)).then_inc(i_loaded[slot], 16)
                    eng.dma_start(Z[:, slot, :, 0:IN], at(x_src, h).rearrange("p (j f) -> p j f", j=J))\
                        .then_inc(x_loaded[slot], 16)

                def load_dense(d, slot):
                    if isinstance(d, int) and d > D_GROUPS:
                        return
                    p = rows_of(d)
                    eng.dma_start(xd[0:p, slot, :], at(x_dense, d) if p == P else x_tail).then_inc(d_loaded[slot], 16)

                def store_h0(h, slot):
                    eng.wait_ge(e_relu, h + 2)
                    eng.dma_start(at(h0_src, h), h0e[:, slot, :]).then_inc(h0_stored[slot], 16)

                def group(g, slot, turn):
                    for j in range(J):
                        if not isinstance(g, int) or g * J + j + DRING <= D_GROUPS:
                            eng.wait_ge(d_transposed, g * J + j + 1)
                            load_dense(g * J + j + DRING, (slot * J + j) % DRING)
                    if not isinstance(g, int) or g + 3 < E_GROUPS:
                        eng.wait_ge(e_transposed, g + 2)
                        load_rows(g + 3, (slot + 1) % 2)
                    eng.wait_ge(runs.scaled, J * g + J + 2)
                    eng.dma_start(at(agg1_g, g), agg_out[:, slot, :]).then_inc(agg_stored[slot], 16)
                    if not isinstance(g, int) or g + 2 < E_GROUPS:
                        runs.load(eng, g + 2, slot)
                    if not isinstance(g, int) or g + 1 < E_GROUPS:
                        store_h0(g + 1, (slot + 1) % 2)
                for h in range(2):
                    load_rows(h, h)
                    runs.load(eng, h, h)
                for d in range(DRING):
                    load_dense(d, d)
                eng.wait_ge(e_transposed, 1)
                load_rows(2, 0)
                store_h0(0, 0)
                loop(eng, E_GROUPS - 3, 2, group)
                for g in range(E_GROUPS - 3, E_GROUPS):
                    group(g, g % 2, g // 2)
                for slot in range(2):
                    eng.wait_ge(h0_stored[slot], 16 * len(range(slot, E_GROUPS, 2)) + 16)
                    eng.wait_ge(agg_stored[slot], 16 * len(range(slot, E_GROUPS, 2)) + 16)

            @block.gpsimd
            def _(eng):
                def gather(h, slot, turn):
                    eng.wait_ge(i_loaded[slot], 16 * turn + 16)
                    eng.sem_inc(s_begun, 1)
                    for j in range(J):
                        eng.indirect_dma_start(Z[:, slot, j, IN:P], None, agg0,
                                               bass.IndirectOffsetOnAxis(ap=idx[:, slot, j:j + 1], axis=0))\
                            .then_inc(gathered[slot], 16)
                loop(eng, E_GROUPS, 2, gather)

            @block.tensor
            def _(eng):
                def transpose_dense(d, slot, turn):
                    p = rows_of(d)
                    eng.wait_ge(d_loaded[slot], 16 * turn + 16)
                    eng.wait_ge(d_xT, d + 1)
                    for h in range(2):
                        ins = eng.transpose(pXT[:, h * p:(h + 1) * p], xd[0:p, slot, h * P:(h + 1) * P], ident[0:p, 0:p])
                    ins.then_inc(d_transposed, 1)

                def first_dense(d, slot):
                    w = 2 * rows_of(d)
                    eng.wait_ge(d_xT, d + 2)
                    eng.wait_ge(d_relu, d + 1)
                    eng.matmul(pH0[:, 0:w], W0_top[:], xT[:, slot % 2, 0:w], start=True, stop=True)
                    eng.matmul(pH0[:, w:2 * w], W0_bot[:], xT[:, slot % 2, 0:w], start=True, stop=True).then_inc(d_h0, 1)

                def second_dense(d, slot):
                    w = 4 * rows_of(d)
                    eng.wait_ge(d_relu, d + 2)
                    eng.wait_ge(d_stats, d + 1)
                    eng.matmul(pH1[:, 0:w], Wr1T[:], h0d[:, slot % 2, 0:w], start=True, stop=True).then_inc(d_h1, 1)

                def transpose_rows(g, slot, turn):
                    eng.wait_ge(x_loaded[slot], 16 * turn + 16)
                    eng.wait_ge(gathered[slot], 16 * J * turn + 16 * J)
                    eng.wait_ge(e_zT, g + 1)
                    for j in range(J):
                        ins = eng.transpose(pZT[:, j * P:(j + 1) * P], Z[:, slot, j, :], ident[:])
                    ins.then_inc(e_transposed, 1)

                def first_rows(g):
                    eng.wait_ge(e_zT, g + 2)
                    eng.wait_ge(e_relu, g + 1)
                    eng.matmul(pHE[:], W0[:], zT[:], start=True, stop=True).then_inc(e_h0, 1)

                def message(g, slot):
                    eng.wait_ge(e_relu, g + 2)
                    eng.wait_ge(e_msg, g + 1)
                    for j in range(J):
                        ins = eng.transpose(pM[:, j * P:(j + 1) * P], h0e[:, slot, j * P:(j + 1) * P], ident[:])
                    ins.then_inc(e_msgT, 1)

                def group(g, slot, turn):
                    more = not isinstance(g, int) or g + 1 < E_GROUPS
                    s1, t1 = later(slot, turn, 1, 2)
                    eng.wait_ge(e_msg, g + 2)
                    for j in range(J):
                        runs.add(eng, g, slot, j, msg[:, slot, j, :])
                        d = g * J + j
                        if not isinstance(d, int) or d + 2 <= D_GROUPS:
                            transpose_dense(d + 2, *later(slot * J + j, turn, 2, DRING))
                        if not isinstance(d, int) or d + 1 <= D_GROUPS:
                            first_dense(d + 1, slot * J + j + 1)
                        second_dense(d, slot * J + j)
                        if more and j == 0:
                            transpose_rows(g + 1, s1, t1)
                        if more and j == 1:
                            first_rows(g + 1)
                        if more and j == 3:
                            message(g + 1, s1)
                transpose_rows(0, 0, 0)
                transpose_dense(0, 0, 0)
                first_rows(0)
                transpose_dense(1, 1, 0)
                first_dense(0, 0)
                message(0, 0)
                loop(eng, E_GROUPS - 1, 2, group)
                group(LAST, LAST % 2, LAST // 2)

            @block.scalar
            def _(eng):
                eng.sem_inc(runs.scaled, 2)
                eng.sem_inc(e_zT, 1)
                eng.sem_inc(e_relu, 1)
                eng.sem_inc(d_relu, 1)
                for slot in range(2):
                    eng.sem_inc(agg_stored[slot], 16)
                    eng.sem_inc(h0_stored[slot], 16)

                def relu_dense(d, slot):
                    w = 4 * rows_of(d)
                    eng.wait_ge(d_h0, d + 1)
                    eng.activation(h0d[:, slot % 2, 0:w], pH0[:, 0:w], ACT.Relu, bias=SH0D, scale=SC0).then_inc(d_relu, 1)

                def copy_rows(g):
                    eng.wait_ge(e_transposed, g + 1)
                    eng.activation(zT[:], pZT[:], ACT.Copy).then_inc(e_zT, 1)

                def relu_rows(g, slot, turn):
                    eng.wait_ge(e_h0, g + 1)
                    eng.wait_ge(h0_stored[slot], 16 * turn + 16)
                    eng.activation(h0e[:, slot, :], pHE[:], ACT.Relu, bias=SH0, scale=SC0).then_inc(e_relu, 1)

                def group(g, slot, turn):
                    more = not isinstance(g, int) or g + 1 < E_GROUPS
                    eng.wait_ge(agg_stored[slot], 16 * turn + 16)
                    for j in range(J):
                        runs.scale(eng, g, j, agg_out[:, slot, j * HID:(j + 1) * HID], weight_col)
                        d = g * J + j
                        if not isinstance(d, int) or d + 1 <= D_GROUPS:
                            relu_dense(d + 1, slot * J + j + 1)
                        if more and j == 0:
                            copy_rows(g + 1)
                        if more and j == 1:
                            relu_rows(g + 1, *later(slot, turn, 1, 2))
                copy_rows(0)
                relu_rows(0, 0, 0)
                relu_dense(0, 0)
                loop(eng, E_GROUPS - 1, 2, group)
                group(LAST, LAST % 2, LAST // 2)

            @block.vector
            def _(eng):
                eng.sem_inc(e_msg, 1)
                eng.sem_inc(d_xT, 1)
                eng.sem_inc(d_stats, 1)
                runs.start_vector(eng)

                def copy_dense(d, slot):
                    w = 2 * rows_of(d)
                    eng.wait_ge(d_transposed, d + 1)
                    eng.tensor_scalar(xT[:, slot % 2, 0:w], pXT[:, 0:w], b2_pair[:], None, ALU.add).then_inc(d_xT, 1)

                def stats_dense(d):
                    w = 4 * rows_of(d)
                    eng.wait_ge(d_h1, d + 1)
                    eng.bn_stats(cols(statD, d * 6, 6), pH1[:, 0:w]).then_inc(d_stats, 1)

                def copy_message(g, slot):
                    eng.wait_ge(e_msgT, g + 1)
                    eng.tensor_copy(msg[:, slot], pM[:].rearrange("p (j f) -> p j f", j=J)).then_inc(e_msg, 1)

                def group(g, slot, turn):
                    more = not isinstance(g, int) or g + 1 < E_GROUPS
                    for j in range(J):
                        runs.keep(eng, g, j)
                        d = g * J + j
                        if not isinstance(d, int) or d + 2 <= D_GROUPS:
                            copy_dense(d + 2, slot * J + j + 2)
                        stats_dense(d)
                        if more and j == 0:
                            runs.select(eng, g + 1, *later(slot, turn, 1, 2))
                        if more and j == 3:
                            copy_message(g + 1, (slot + 1) % 2)
                runs.select(eng, 0, 0, 0)
                copy_dense(0, 0)
                copy_dense(1, 1)
                copy_message(0, 0)
                loop(eng, E_GROUPS - 1, 2, group)
                group(LAST, LAST % 2, LAST // 2)

        with ExitStack() as ctx:
            sb, psum, sem, ring = makers = tools(nc, ctx, "bn1")
            Z = sb("Z", [P, 2, J, P])
            A = sb("A", [P, 2, J, HID])
            zT = sb("zT", [P, GROUP])
            aT = sb("aT", [P, 2, GROUP])
            h0 = sb("h0", [P, 2, GROUP])
            h0v = sb("h0v", [P, 2, GROUP])
            h1 = sb("h1", [P, 2, GROUP])
            statT = sb("statT", [P, E_GROUPS * 6])
            statV = sb("statV", [P, E_GROUPS * 6])
            st = sb("st", [P, 16])
            pZ, pA, pH0, pV0, pH1, pV1 = (psum(n) for n in ("pZ", "pA", "pH0", "pV0", "pH1", "pV1"))
            loaded, h0_stored, h1_stored = ring("loaded"), ring("h0_stored"), ring("h1_stored")
            s_Z, s_A, s_H0, s_V0, s_H1, s_V1 = (sem(f"s_{n}") for n in ("Z", "A", "H0", "V0", "H1", "V1"))
            c_z, c_a, c_h0, c_v0 = (sem(f"c_{n}") for n in ("z", "a", "h0", "v0"))
            c_h1, c_v1, s_copy = sem("c_h1"), sem("c_v1"), sem("s_copy")
            s_dve, s_var, s_std = sem("s_dve"), sem("s_var"), sem("s_std")
            block = ctx.enter_context(nc.Block())
            LAST = E_GROUPS - 1

            @block.sync
            def _(eng):
                def load(h, slot):
                    for to, of in ((Z[:, slot, :, 0:IN], x_dst), (Z[:, slot, :, IN:P], agg0_g), (A[:, slot], agg1_g)):
                        eng.dma_start(to, at(of, h).rearrange("p (j f) -> p j f", j=J)).then_inc(loaded[slot], 16)

                def store_h0(h, slot):
                    eng.wait_ge(c_h0, h + 2)
                    eng.dma_start(at(h0_dst, h), h0[:, slot, :]).then_inc(h0_stored[slot], 16)

                def group(g, slot, turn):
                    if not isinstance(g, int) or g + 1 < E_GROUPS:
                        store_h0(g + 1, (slot + 1) % 2)
                    if not isinstance(g, int) or g + 3 < E_GROUPS:
                        eng.wait_ge(s_A, g + 2)
                        load(g + 3, (slot + 1) % 2)
                    eng.wait_ge(s_copy, g + 1)
                    eng.dma_start(at(h1_dst, g), h1[:, slot, :]).then_inc(h1_stored[slot], 16)
                load(0, 0)
                load(1, 1)
                eng.wait_ge(s_A, 1)
                load(2, 0)
                store_h0(0, 0)
                loop(eng, E_GROUPS - 3, 2, group)
                for g in range(E_GROUPS - 3, E_GROUPS):
                    group(g, g % 2, g // 2)
                for slot in range(2):
                    eng.wait_ge(h0_stored[slot], 16 * len(range(slot, E_GROUPS, 2)) + 16)
                    eng.wait_ge(h1_stored[slot], 16 * len(range(slot, E_GROUPS, 2)) + 16)

            @block.tensor
            def _(eng):
                def turn_rows(g, slot, turn):
                    eng.wait_ge(loaded[slot], 48 * turn + 48)
                    eng.wait_ge(c_z, g + 1)
                    for j in range(J):
                        ins = eng.transpose(pZ[:, j * P:(j + 1) * P], Z[:, slot, j, :], ident[:])
                    ins.then_inc(s_Z, 1)
                    eng.wait_ge(c_a, g + 1)
                    for j in range(J):
                        ins = eng.transpose(pA[:, j * P:(j + 1) * P], A[:, slot, j, :], ident[:])
                    ins.then_inc(s_A, 1)

                def first(g):
                    eng.wait_ge(c_z, g + 2)
                    eng.wait_ge(c_h0, g + 1)
                    eng.matmul(pH0[:], W0[:], zT[:], start=True, stop=True).then_inc(s_H0, 1)
                    eng.wait_ge(c_v0, g + 1)
                    eng.matmul(pV0[:], W0_top[:], zT[:], start=True, stop=True).then_inc(s_V0, 1)

                def second(g, slot):
                    eng.wait_ge(c_h0, g + 2)
                    eng.wait_ge(c_a, g + 2)
                    eng.wait_ge(c_h1, g + 1)
                    eng.matmul(pH1[:], Wr1T[:], h0[:, slot, :], start=True, stop=False)
                    eng.matmul(pH1[:], Wl1T[:], aT[:, slot, :], start=False, stop=True).then_inc(s_H1, 1)
                    eng.wait_ge(c_v0, g + 2)
                    eng.wait_ge(c_v1, g + 1)
                    eng.matmul(pV1[:], Wr1T[:], h0v[:, slot, :], start=True, stop=True).then_inc(s_V1, 1)

                def group(g, slot, turn):
                    if not isinstance(g, int) or g + 1 < E_GROUPS:
                        turn_rows(g + 1, *later(slot, turn, 1, 2))
                        first(g + 1)
                    second(g, slot)
                turn_rows(0, 0, 0)
                first(0)
                loop(eng, LAST, 2, group)
                group(LAST, LAST % 2, LAST // 2)

            @block.scalar
            def _(eng):
                for s in (c_z, c_a, c_h0, c_v0):
                    eng.sem_inc(s, 1)
                for slot in range(2):
                    eng.sem_inc(h0_stored[slot], 16)

                def group(g, slot, turn):
                    eng.wait_ge(s_Z, g + 1)
                    eng.activation(zT[:], pZ[:], ACT.Copy).then_inc(c_z, 1)
                    eng.wait_ge(s_A, g + 1)
                    eng.activation(aT[:, slot, :], pA[:], ACT.Copy).then_inc(c_a, 1)
                    eng.wait_ge(s_H0, g + 1)
                    eng.wait_ge(h0_stored[slot], 16 * turn + 16)
                    eng.activation(h0[:, slot, :], pH0[:], ACT.Relu, bias=SH0, scale=SC0).then_inc(c_h0, 1)
                    eng.wait_ge(s_V0, g + 1)
                    eng.activation(h0v[:, slot, :], pV0[:], ACT.Relu, bias=SH0, scale=SC0).then_inc(c_v0, 1)
                loop(eng, E_GROUPS, 2, group)
                eng.wait_ge(s_var, 1)
                eng.activation(st[:, 11:12], st[:, 10:11], ACT.Sqrt).then_inc(s_std, 1)

            @block.vector
            def _(eng):
                for s in (c_h1, c_v1):
                    eng.sem_inc(s, 1)
                for slot in range(2):
                    eng.sem_inc(h1_stored[slot], 16)

                def group(g, slot, turn):
                    eng.wait_ge(s_H1, g + 1)
                    eng.wait_ge(h1_stored[slot], 16 * turn + 16)
                    eng.tensor_copy(h1[:, slot, :], pH1[:]).then_inc(s_copy, 1)
                    eng.bn_stats(cols(statT, g * 6, 6), pH1[:]).then_inc(c_h1, 1)
                    eng.wait_ge(s_V1, g + 1)
                    eng.bn_stats(cols(statV, g * 6, 6), pV1[:]).then_inc(c_v1, 1)
                loop(eng, E_GROUPS, 2, group)
                t = Steps(eng, s_dve)
                eng.wait_ge(c_h1, E_GROUPS + 1)
                eng.wait_ge(c_v1, E_GROUPS + 1)
                mD, vD, mT, vT, mV, vV, a, b, c, delta, var, std = (st[:, i:i + 1] for i in range(12))
                t.did(eng.bn_aggr(st[:, 0:2], statD[:]))
                t.did(eng.bn_aggr(st[:, 2:4], statT[:]))
                t.did(eng.bn_aggr(st[:, 4:6], statV[:]))
                t.settle()
                SHARE = E_ROWS / N_NODES
                t.did(eng.tensor_tensor(a, mT, mD, ALU.subtract))
                t.did(eng.tensor_tensor(b, mV, mD, ALU.subtract))
                t.did(eng.tensor_tensor(delta, mT, mV, ALU.subtract))
                t.did(eng.tensor_tensor(c, vT, vV, ALU.subtract))
                t.settle()
                t.did(eng.tensor_scalar(delta, delta, SHARE, None, ALU.mult))
                t.did(eng.tensor_tensor(a, a, a, ALU.mult))
                t.did(eng.tensor_tensor(b, b, b, ALU.mult))
                t.settle()
                t.did(eng.tensor_tensor(c, c, a, ALU.add))
                t.settle()
                t.did(eng.tensor_tensor(c, c, b, ALU.subtract))
                t.did(eng.tensor_tensor(a, delta, delta, ALU.mult))
                t.settle()
                t.did(eng.scalar_tensor_tensor(var, c, SHARE, vD, ALU.mult, ALU.add))
                t.settle()
                t.did(eng.tensor_tensor(var, var, a, ALU.subtract))
                t.did(eng.tensor_tensor(mD, mD, delta, ALU.add))
                t.settle()
                eng.tensor_scalar(var, var, 0.0, BN_EPS, ALU.max, ALU.add).then_inc(s_var, 1)
                eng.wait_ge(s_std, 1)
                t.did(eng.reciprocal(var, std))
                t.did(eng.tensor_tensor(a, mD, B1, ALU.add))
                t.settle()
                t.did(eng.tensor_tensor(SC1, G1, var, ALU.mult))
                t.did(eng.tensor_tensor(b, B1, a, ALU.subtract))
                t.settle()
                t.did(eng.tensor_tensor(b, b, SC1, ALU.mult))
                t.settle()
                t.did(eng.tensor_tensor(SH1, BE1, b, ALU.add))
                t.settle()

        with ExitStack() as ctx:
            sb, psum, sem, ring = makers = tools(nc, ctx, "layer2")
            runs = RunSums(makers, dst_rows, dst_col, prev_last, OUT)
            idx = sb("idx", [P, 2, J], I32)
            A = sb("A", [P, 2, J, HID])
            aT = sb("aT", [P, GROUP])
            h0 = sb("h0", [P, 2, GROUP])
            h2 = sb("h2", [P, 2, GROUP])
            xe = sb("xe", [P, 2, J * IN])
            h0t = sb("h0t", [P, 2, GROUP])
            h1t = sb("h1t", [P, 2, GROUP])
            h2t = sb("h2t", [P, 2, GROUP])
            xt = sb("xt", [P, 2, J * IN])
            msg = sb("msg", [P, 2, J, OUT])
            ue = sb("ue", [P, 2, J, OUT])
            ut = sb("ut", [P, 2, J, OUT])
            agg_out = sb("agg_out", [P, 2, J * OUT])
            pA, pH1, pO, pOT = (psum(n) for n in ("pA", "pH1", "pO", "pOT"))
            i_loaded, gathered = ring("i_loaded"), ring("gathered")
            e_loaded, t_loaded = ring("e_loaded"), ring("t_loaded")
            e_stored, t_stored, agg_stored = ring("e_stored"), ring("t_stored"), ring("agg_stored")
            s_A, s_H1, s_O, s_OT = (sem(f"s_{n}") for n in ("A", "H1", "O", "OT"))
            c_A, c_relu, c_h2, c_O = (sem(f"c_{n}") for n in ("A", "relu", "h2", "O"))
            c_relut, c_h2t, c_OT = (sem(f"c_{n}") for n in ("relut", "h2t", "OT"))
            s_ux, s_uxt, s_u, s_ut, s_begun = (sem(n) for n in ("s_ux", "s_uxt", "s_u", "s_ut", "s_begun"))
            block = ctx.enter_context(nc.Block())
            LAST = E_GROUPS - 1

            @block.sync
            def _(eng):
                def load_e(h, slot):
                    eng.dma_start(h0[:, slot, :], at(h0_src, h)).then_inc(e_loaded[slot], 16)
                    eng.dma_start(xe[:, slot, :], at(x_src, h)).then_inc(e_loaded[slot], 16)

                def load_idx(h, slot):
                    eng.dma_start(idx[:, slot, :], cols(slot_home, h * J, J)).then_inc(i_loaded[slot], 16)

                def load_t(h, slot):
                    eng.dma_start(h0t[:, slot, :], at(h0_dst, h)).then_inc(t_loaded[slot], 16)
                    eng.dma_start(h1t[:, slot, :], at(h1_dst, h)).then_inc(t_loaded[slot], 16)
                    eng.dma_start(xt[:, slot, :], at(x_dst, h)).then_inc(t_loaded[slot], 16)

                def store_u(h, slot):
                    eng.wait_ge(s_u, h + 1)
                    eng.dma_start(at(u_src, h), ue[:, slot].rearrange("p j f -> p (j f)")).then_inc(e_stored[slot], 16)
                    eng.wait_ge(s_ut, h + 1)
                    eng.dma_start(at(u_dst, h), ut[:, slot].rearrange("p j f -> p (j f)")).then_inc(t_stored[slot], 16)

                def group(g, slot, turn):
                    if not isinstance(g, int) or g + 3 < E_GROUPS:
                        eng.wait_ge(s_A, g + 2)
                        load_idx(g + 3, (slot + 1) % 2)
                    eng.wait_ge(runs.scaled, J * g + J + 2)
                    eng.dma_start(at(agg2_g, g), agg_out[:, slot, :]).then_inc(agg_stored[slot], 16)
                    if not isinstance(g, int) or g + 2 < E_GROUPS:
                        runs.load(eng, g + 2, slot)
                    if not isinstance(g, int) or g + 1 < E_GROUPS:
                        store_u(g + 1, (slot + 1) % 2)
                    if not isinstance(g, int) or g + 3 < E_GROUPS:
                        load_e(g + 3, (slot + 1) % 2)
                        load_t(g + 3, (slot + 1) % 2)
                for h in range(2):
                    load_idx(h, h)
                    load_e(h, h)
                    load_t(h, h)
                    runs.load(eng, h, h)
                eng.wait_ge(s_A, 1)
                load_idx(2, 0)
                store_u(0, 0)
                load_e(2, 0)
                load_t(2, 0)
                loop(eng, E_GROUPS - 3, 2, group)
                for g in range(E_GROUPS - 3, E_GROUPS):
                    group(g, g % 2, g // 2)
                for slot in range(2):
                    n = 16 * len(range(slot, E_GROUPS, 2)) + 16
                    eng.wait_ge(e_stored[slot], n)
                    eng.wait_ge(t_stored[slot], n)
                    eng.wait_ge(agg_stored[slot], n)

            @block.gpsimd
            def _(eng):
                def gather(h, slot, turn):
                    eng.wait_ge(i_loaded[slot], 16 * turn + 16)
                    eng.sem_inc(s_begun, 1)
                    for j in range(J):
                        eng.indirect_dma_start(A[:, slot, j, :], None, agg1,
                                               bass.IndirectOffsetOnAxis(ap=idx[:, slot, j:j + 1], axis=0))\
                            .then_inc(gathered[slot], 16)
                loop(eng, E_GROUPS, 2, gather)

            @block.tensor
            def _(eng):
                def turn_rows(g, slot, turn):
                    eng.wait_ge(gathered[slot], 16 * J * turn + 16 * J)
                    eng.wait_ge(c_A, g + 1)
                    for j in range(J):
                        ins = eng.transpose(pA[:, j * P:(j + 1) * P], A[:, slot, j, :], ident[:])
                    ins.then_inc(s_A, 1)

                def second(g, slot, turn):
                    eng.wait_ge(e_loaded[slot], 32 * turn + 32)
                    eng.wait_ge(c_A, g + 2)
                    eng.wait_ge(c_relu, g + 1)
                    eng.matmul(pH1[:], Wr1T[:], h0[:, slot, :], start=True, stop=False)
                    eng.matmul(pH1[:], Wl1T[:], aT[:], start=False, stop=True).then_inc(s_H1, 1)

                def third_t(g, slot):
                    eng.wait_ge(c_h2t, g + 1)
                    eng.wait_ge(c_OT, g + 1)
                    for j in range(J):
                        ins = eng.matmul(pOT[:, j * OUT:(j + 1) * OUT], h2t[:, slot, j * P:(j + 1) * P],
                                         W2_msg[:, OUT:], start=True, stop=True)
                    ins.then_inc(s_OT, 1)

                def third(g, slot):
                    eng.wait_ge(c_h2, g + 1)
                    eng.wait_ge(c_O, g + 1)
                    for j in range(J):
                        ins = eng.matmul(pO[:, j * P:(j + 1) * P], h2[:, slot, j * P:(j + 1) * P],
                                         W2_msg[:], start=True, stop=True)
                    ins.then_inc(s_O, 1)

                def group(g, slot, turn):
                    more = not isinstance(g, int) or g + 1 < E_GROUPS
                    s1, t1 = later(slot, turn, 1, 2)
                    eng.wait_ge(c_O, g + 2)
                    for j in range(J):
                        runs.add(eng, g, slot, j, msg[:, slot, j, :])
                        if more:
                            (lambda: turn_rows(g + 1, s1, t1), lambda: second(g + 1, s1, t1),
                             lambda: third_t(g + 1, s1), lambda: third(g + 1, s1))[j]()
                turn_rows(0, 0, 0)
                second(0, 0, 0)
                third_t(0, 0)
                third(0, 0)
                loop(eng, LAST, 2, group)
                group(LAST, LAST % 2, LAST // 2)

            @block.scalar
            def _(eng):
                eng.sem_inc(runs.scaled, 2)
                eng.sem_inc(c_A, 1)
                eng.sem_inc(c_relu, 1)
                for slot in range(2):
                    eng.sem_inc(agg_stored[slot], 16)

                def relu_t(g, slot, turn):
                    eng.wait_ge(t_loaded[slot], 48 * turn + 48)
                    eng.activation(h2t[:, slot, :], h1t[:, slot, :], ACT.Relu, bias=SH1, scale=SC1).then_inc(c_relut, 1)

                def copy(g):
                    eng.wait_ge(s_A, g + 1)
                    eng.activation(aT[:], pA[:], ACT.Copy).then_inc(c_A, 1)

                def relu(g, slot):
                    eng.wait_ge(s_H1, g + 1)
                    eng.activation(h2[:, slot, :], pH1[:], ACT.Relu, bias=SH1, scale=SC1).then_inc(c_relu, 1)

                def group(g, slot, turn):
                    more = not isinstance(g, int) or g + 1 < E_GROUPS
                    s1, t1 = later(slot, turn, 1, 2)
                    eng.wait_ge(agg_stored[slot], 16 * turn + 16)
                    for j in range(J):
                        runs.scale(eng, g, j, agg_out[:, slot, j * OUT:(j + 1) * OUT], weight_col)
                        if more and j < 3:
                            (lambda: copy(g + 1), lambda: relu_t(g + 1, s1, t1), lambda: relu(g + 1, s1))[j]()
                copy(0)
                relu_t(0, 0, 0)
                relu(0, 0)
                loop(eng, LAST, 2, group)
                group(LAST, LAST % 2, LAST // 2)

            @block.vector
            def _(eng):
                eng.sem_inc(c_O, 1)
                eng.sem_inc(c_OT, 1)
                for slot in range(2):
                    eng.sem_inc(e_stored[slot], 16)
                    eng.sem_inc(t_stored[slot], 16)
                runs.start_vector(eng)
                b2_all = b2_row[:].unsqueeze(1).to_broadcast([P, J, OUT])

                def residual_t(g, slot):
                    eng.wait_ge(c_relut, g + 1)
                    eng.tensor_tensor(h2t[:, slot, :], h2t[:, slot, :], h0t[:, slot, :], ALU.add).then_inc(c_h2t, 1)

                def residual(g, slot):
                    eng.wait_ge(c_relu, g + 2)
                    eng.tensor_tensor(h2[:, slot, :], h2[:, slot, :], h0[:, slot, :], ALU.add).then_inc(c_h2, 1)

                def sum_t(g, slot, turn):
                    eng.wait_ge(s_OT, g + 1)
                    eng.wait_ge(t_stored[slot], 16 * turn + 16)
                    eng.tensor_tensor(ut[:, slot], pOT[:, 0:J * OUT].rearrange("p (j f) -> p j f", j=J),
                                      xt[:, slot, :].rearrange("p (j f) -> p j f", j=J), ALU.add).then_inc(c_OT, 1)
                    eng.wait_ge(c_OT, g + 2)
                    eng.tensor_tensor(ut[:, slot], ut[:, slot], b2_all, ALU.add).then_inc(s_ut, 1)

                def sum_e(g, slot, turn):
                    eng.wait_ge(s_O, g + 1)
                    eng.wait_ge(e_stored[slot], 16 * turn + 16)
                    both = pO[:].rearrange("p (j f) -> p j f", j=J)
                    eng.tensor_tensor(ue[:, slot], both[:, :, OUT:], xe[:, slot, :].rearrange("p (j f) -> p j f", j=J),
                                      ALU.add).then_inc(s_ux, 1)
                    eng.tensor_copy(msg[:, slot], both[:, :, 0:OUT]).then_inc(c_O, 1)
                    eng.wait_ge(s_ux, g + 1)
                    eng.tensor_tensor(ue[:, slot], ue[:, slot], b2_all, ALU.add).then_inc(s_u, 1)

                def group(g, slot, turn):
                    more = not isinstance(g, int) or g + 1 < E_GROUPS
                    s1, t1 = later(slot, turn, 1, 2)
                    for j in range(J):
                        runs.keep(eng, g, j)
                        if more:
                            if j == 0:
                                runs.select(eng, g + 1, s1, t1)
                            if j == 1:
                                residual_t(g + 1, s1)
                            if j == 2:
                                residual(g + 1, s1)
                            if j == 3:
                                sum_t(g + 1, s1, t1)
                                sum_e(g + 1, s1, t1)
                runs.select(eng, 0, 0, 0)
                residual_t(0, 0)
                residual(0, 0)
                sum_t(0, 0, 0)
                sum_e(0, 0, 0)
                loop(eng, LAST, 2, group)
                group(LAST, LAST % 2, LAST // 2)

        out_dense = out[0:D_GROUPS * GROUP].rearrange("(g p q) f -> g p (q f)", p=P, q=J)
        out_tail = out[D_GROUPS * GROUP:N_NODES].rearrange("(p q) f -> p (q f)", q=J)
        with ExitStack() as ctx:
            sb, psum, sem, ring = makers = tools(nc, ctx, "dense")
            xd = sb("xd", [P, DRING, J * IN])
            xT = sb("xT", [P, 4, GROUP // 2])
            h0 = sb("h0", [P, 4, GROUP])
            h2 = sb("h2", [P, 2, GROUP])
            sq1 = sb("sq1", [P, 2, J, OUT])
            sq2 = sb("sq2", [P, 2, J, OUT])
            y = sb("y", [P, 2, J, OUT])
            o = sb("o", [P, 4, J, OUT])
            small = sb("small", [P, 8, 2, J])
            mean1, var1, std1, r1, mean2, var2, std2, r2 = (small[:, i] for i in range(8))
            pXT, pH0, pH1, pU = psum("pXT"), psum("pH0"), psum("pH1"), psum("pU", 2)
            d_loaded, d_stored = ring("d_loaded", DRING), ring("d_stored", 4)
            d_T, d_X, d_H0, d_R0, d_H1, d_R1, d_h2, d_U = (
                sem(f"d_{n}") for n in ("T", "X", "H0", "R0", "H1", "R1", "h2", "U"))
            d_q1, d_m1, d_v1, d_s1, d_r1, d_y, d_yb = (
                sem(f"d_{n}") for n in ("q1", "m1", "v1", "s1", "r1", "y", "yb"))
            d_q2, d_m2, d_v2, d_s2, d_r2, d_out = (sem(f"d_{n}") for n in ("q2", "m2", "v2", "s2", "r2", "out"))
            idx = sb("idx", [P, 2, 2, J], I32)
            ue = sb("ue", [P, 2, J, OUT])
            A = sb("A", [P, 2, J, OUT])
            x1 = sb("x1", [P, 2, J, OUT])
            stats = sb("stats", [P, 2, J, 6])
            mv = sb("mv", [P, 2, J, 2])
            rstd = sb("rstd", [P, 2, 2, J])
            e_idx, e_loaded, gathered, scattered = ring("e_idx"), ring("e_loaded"), ring("gathered"), ring("scattered")
            e_sum, e_st, e_mv, e_var, e_std, e_r, e_x1, e_begun, s_begun = (
                sem(n) for n in ("e_sum", "e_st", "e_mv", "e_var", "e_std", "e_r", "e_x1", "e_begun", "s_begun"))
            block = ctx.enter_context(nc.Block())
            N_TILES = D_GROUPS + 1

            def exists(d):
                return not isinstance(d, int) or 0 <= d < N_TILES

            @block.sync
            def _(eng):
                def load_e(h, slot):
                    eng.dma_start(idx[:, slot, 0, :], cols(slot_home, h * J, J)).then_inc(e_idx[slot], 16)
                    eng.dma_start(idx[:, slot, 1, :], cols(rel_home, h * J, J)).then_inc(e_idx[slot], 16)
                    eng.dma_start(ue[:, slot].rearrange("p j f -> p (j f)"), at(u_src, h)).then_inc(e_loaded[slot], 16)

                def load_d(d, slot):
                    p = rows_of(d)
                    eng.dma_start(xd[0:p, slot, :], at(x_dense, d) if p == P else x_tail).then_inc(d_loaded[slot], 16)

                def group(g, slot, turn):
                    for j in range(J):
                        d = g * J + j
                        if exists(d + DRING):
                            eng.wait_ge(d_T, d + 1)
                            load_d(d + DRING, (slot * J + j) % DRING)
                        eng.wait_ge(d_out, d + 1)
                        p = rows_of(d)
                        eng.dma_start(at(out_dense, d) if p == P else out_tail,
                                      o[0:p, j].rearrange("p q f -> p (q f)")).then_inc(d_stored[j], 16)
                    if not isinstance(g, int) or g + 2 < E_GROUPS:
                        eng.wait_ge(scattered[slot], 16 * J * turn + 16 * J)
                        load_e(g + 2, slot)
                for h in range(2):
                    load_e(h, h)
                for d in range(DRING):
                    load_d(d, d)
                loop(eng, E_GROUPS - 3, 2, group)
                for g in range(E_GROUPS - 3, E_GROUPS):
                    group(g, g % 2, g // 2)
                for j in range(4):
                    eng.wait_ge(d_stored[j], 16 * E_GROUPS + 16)

            @block.gpsimd
            def _(eng):
                def gather(h, slot, turn):
                    eng.wait_ge(e_idx[slot], 32 * turn + 32)
                    eng.sem_inc(s_begun, 1)
                    for j in range(J):
                        eng.indirect_dma_start(A[:, slot, j, :], None, agg2,
                                               bass.IndirectOffsetOnAxis(ap=idx[:, slot, 0, j:j + 1], axis=0))\
                            .then_inc(gathered[slot], 16)

                def scatter(h, slot):
                    eng.wait_ge(e_x1, h + 1)
                    eng.sem_inc(s_begun, 1)
                    for j in range(J):
                        eng.indirect_dma_start(x1_by_rel, bass.IndirectOffsetOnAxis(ap=idx[:, slot, 1, j:j + 1], axis=0),
                                               x1[:, slot, j, :], None).then_inc(scattered[slot], 16)

                def group(g, slot, turn):
                    if not isinstance(g, int) or g + 1 < E_GROUPS:
                        gather(g + 1, *later(slot, turn, 1, 2))
                    scatter(g, slot)
                gather(0, 0, 0)
                loop(eng, E_GROUPS - 1, 2, group)
                group(E_GROUPS - 1, (E_GROUPS - 1) % 2, (E_GROUPS - 1) // 2)
                for slot in range(2):
                    eng.wait_ge(scattered[slot], 16 * J * len(range(slot, E_GROUPS, 2)))

            @block.tensor
            def _(eng):
                def turn_rows(d, slot, turn):
                    p = rows_of(d)
                    eng.wait_ge(d_loaded[slot], 16 * turn + 16)
                    eng.wait_ge(d_X, d + 1)
                    for h in range(2):
                        ins = eng.transpose(pXT[:, h * p:(h + 1) * p], xd[0:p, slot, h * P:(h + 1) * P], ident[0:p, 0:p])
                    ins.then_inc(d_T, 1)

                def first(d, slot):
                    w = 2 * rows_of(d)
                    eng.wait_ge(d_X, d + 2)
                    eng.wait_ge(d_R0, d + 1)
                    eng.matmul(pH0[:, 0:w], W0_top[:], xT[:, slot % 4, 0:w], start=True, stop=True)
                    eng.matmul(pH0[:, w:2 * w], W0_bot[:], xT[:, slot % 4, 0:w], start=True, stop=True).then_inc(d_H0, 1)

                def second(d, slot):
                    w = 4 * rows_of(d)
                    eng.wait_ge(d_R0, d + 2)
                    eng.wait_ge(d_R1, d + 1)
                    eng.matmul(pH1[:, 0:w], Wr1T[:], h0[:, slot % 4, 0:w], start=True, stop=True).then_inc(d_H1, 1)

                def third(d, slot):
                    p = rows_of(d)
                    eng.wait_ge(d_h2, d + 1)
                    eng.wait_ge(d_y, d + 1)
                    for h in range(2):
                        eng.matmul(pU[0:p, slot % 2, h * 256:(h + 1) * 256], xT[:, slot % 4, h * p:(h + 1) * p],
                                   U_x[:], start=True, stop=False)
                        for k in range(2):
                            q = 2 * h + k
                            ins = eng.matmul(pU[0:p, slot % 2, q * P:(q + 1) * P],
                                             h2[:, slot % 2, (2 * k + h) * p:(2 * k + h + 1) * p],
                                             U_h[:], start=False, stop=k == 1)
                    ins.then_inc(d_U, 1)

                def group(g, slot, turn):
                    for j in range(J):
                        d, s = g * J + j, slot * J + j
                        third(d, s)
                        if exists(d + 1):
                            second(d + 1, s + 1)
                        if exists(d + 2):
                            first(d + 2, s + 2)
                        if exists(d + 3):
                            turn_rows(d + 3, *later(s, turn, 3, DRING))
                for d in range(3):
                    turn_rows(d, d, 0)
                    if d >= 1:
                        first(d - 1, d - 1)
                second(0, 0)
                loop(eng, E_GROUPS - 1, 2, group)
                group(E_GROUPS - 1, (E_GROUPS - 1) % 2, (E_GROUPS - 1) // 2)

            @block.scalar
            def _(eng):
                eng.sem_inc(d_R0, 1)
                eng.sem_inc(d_R1, 1)

                def relu0(d, slot):
                    w = 4 * rows_of(d)
                    eng.wait_ge(d_H0, d + 1)
                    eng.activation(h0[:, slot % 4, 0:w], pH0[:, 0:w], ACT.Relu, bias=SH0D, scale=SC0).then_inc(d_R0, 1)

                def relu1(d, slot):
                    w = 4 * rows_of(d)
                    eng.wait_ge(d_H1, d + 1)
                    eng.activation(h2[:, slot % 2, 0:w], pH1[:, 0:w], ACT.Relu, bias=SH1, scale=SC1).then_inc(d_R1, 1)

                def square_u(d, slot):
                    p = rows_of(d)
                    eng.wait_ge(d_U, d + 1)
                    u = pU[0:p, slot % 2].rearrange("p (q f) -> p q f", q=J)[:, :, 0:OUT]
                    eng.activation(sq1[0:p, slot % 2], u, ACT.Square).then_inc(d_q1, 1)

                def square_y(d, slot):
                    p = rows_of(d)
                    eng.wait_ge(d_yb, d + 1)
                    eng.activation(sq2[0:p, slot % 2], y[0:p, slot % 2], ACT.Square).then_inc(d_q2, 1)

                def root(d, slot, known, var, std, done):
                    p = rows_of(d)
                    eng.wait_ge(known, d + 1)
                    eng.activation(std[0:p, slot % 2], var[0:p, slot % 2], ACT.Sqrt).then_inc(done, 1)

                def group(g, slot, turn):
                    for j in range(J):
                        d, s = g * J + j, slot * J + j
                        back = not isinstance(d, int) or d > 0
                        if back:
                            square_y(d - 1, s + 7)
                        square_u(d, s)
                        if exists(d + 1):
                            relu1(d + 1, s + 1)
                        root(d, s, d_v1, var1, std1, d_s1)
                        if exists(d + 2):
                            relu0(d + 2, s + 2)
                        if back:
                            root(d - 1, s + 7, d_v2, var2, std2, d_s2)
                        if j == 2:
                            eng.wait_ge(e_var, g + 1)
                            eng.activation(rstd[:, slot, 0, :], mv[:, slot, :, 1], ACT.Sqrt).then_inc(e_std, 1)
                relu0(0, 0)
                relu0(1, 1)
                relu1(0, 0)
                group(0, 0, 0)
                group(1, 1, 0)
                loop_from(eng, 2, E_GROUPS - 1, 2, group)
                group(E_GROUPS - 1, (E_GROUPS - 1) % 2, (E_GROUPS - 1) // 2)
                square_y(N_TILES - 1, (N_TILES - 1) % 8)
                root(N_TILES - 1, (N_TILES - 1) % 8, d_v2, var2, std2, d_s2)

            @block.vector
            def _(eng):
                eng.sem_inc(d_X, 1)
                eng.sem_inc(d_y, 2)
                for j in range(4):
                    eng.sem_inc(d_stored[j], 16)

                def copy(d, slot):
                    w = 2 * rows_of(d)
                    eng.wait_ge(d_T, d + 1)
                    eng.tensor_scalar(xT[:, slot % 4, 0:w], pXT[:, 0:w], b2_pair[:], None, ALU.add).then_inc(d_X, 1)

                def residual(d, slot):
                    w = 4 * rows_of(d)
                    eng.wait_ge(d_R1, d + 2)
                    eng.tensor_tensor(h2[:, slot % 2, 0:w], h2[:, slot % 2, 0:w], h0[:, slot % 4, 0:w], ALU.add).then_inc(d_h2, 1)

                def variance(d, slot, squared, sq, mean, var, s_mean, s_var):
                    p = rows_of(d)
                    eng.wait_ge(squared, d + 1)
                    eng.tensor_reduce(mean[0:p, slot % 2], sq[0:p, slot % 2], AX.X, ALU.add).then_inc(s_mean, 1)
                    eng.wait_ge(s_mean, d + 1)
                    eng.tensor_scalar(var[0:p, slot % 2], mean[0:p, slot % 2], 1.0 / OUT, LN_EPS, ALU.mult, ALU.add).then_inc(s_var, 1)

                def first_norm(d, slot):
                    p = rows_of(d)
                    eng.wait_ge(d_s1, d + 1)
                    eng.reciprocal(r1[0:p, slot % 2], std1[0:p, slot % 2]).then_inc(d_r1, 1)
                    um = pU[0:p, slot % 2].rearrange("p (q f) -> p q f", q=J)[:, :, OUT:]
                    eng.wait_ge(d_r1, d + 1)
                    eng.tensor_tensor(y[0:p, slot % 2], um, r1[0:p, slot % 2].unsqueeze(2).to_broadcast([p, J, OUT]),
                                      ALU.mult).then_inc(d_y, 1)
                    eng.wait_ge(d_y, d + 3)
                    eng.tensor_tensor(y[0:p, slot % 2], y[0:p, slot % 2],
                                      biasC_row[0:p].unsqueeze(1).to_broadcast([p, J, OUT]), ALU.add).then_inc(d_yb, 1)

                def second_norm(d, slot, turn):
                    p = rows_of(d)
                    eng.wait_ge(d_s2, d + 1)
                    eng.reciprocal(r2[0:p, slot % 2], std2[0:p, slot % 2]).then_inc(d_r2, 1)
                    eng.wait_ge(d_r2, d + 1)
                    eng.wait_ge(d_stored[slot % 4], 16 * (turn * 2 + slot // 4) + 16)
                    eng.tensor_tensor(o[0:p, slot % 4], y[0:p, slot % 2],
                                      r2[0:p, slot % 2].unsqueeze(2).to_broadcast([p, J, OUT]), ALU.mult).then_inc(d_out, 1)

                def rows(g, slot, turn, part):
                    if part == 0:
                        eng.wait_ge(e_loaded[slot], 16 * turn + 16)
                        eng.wait_ge(gathered[slot], 16 * J * turn + 16 * J)
                        eng.tensor_tensor(ue[:, slot], ue[:, slot], A[:, slot], ALU.add).then_inc(e_sum, 1)
                        eng.wait_ge(e_sum, g + 1)
                        for q in range(J):
                            ins = eng.bn_stats(stats[:, slot, q, :], ue[:, slot, q, :])
                        ins.then_inc(e_st, 1)
                    if part == 1:
                        eng.wait_ge(e_st, g + 1)
                        eng.sem_inc(e_begun, 1)
                        for q in range(J):
                            ins = eng.bn_aggr(mv[:, slot, q, :], stats[:, slot, q, :])
                        ins.then_inc(e_mv, 1)
                    if part == 2:
                        eng.wait_ge(e_mv, g + 1)
                        eng.tensor_scalar(mv[:, slot, :, 1], mv[:, slot, :, 1], LN_EPS, None, ALU.add).then_inc(e_var, 1)
                    if part == 3:
                        eng.wait_ge(e_std, g + 1)
                        eng.reciprocal(rstd[:, slot, 1, :], rstd[:, slot, 0, :]).then_inc(e_r, 1)
                        eng.wait_ge(e_r, g + 1)
                        for q in range(J):
                            ins = eng.tensor_scalar(x1[:, slot, q, :], ue[:, slot, q, :], mv[:, slot, q, 0:1],
                                                    rstd[:, slot, 1, q:q + 1], ALU.subtract, ALU.mult)
                        ins.then_inc(e_x1, 1)

                def group(g, slot, turn):
                    for j in range(J):
                        d, s = g * J + j, slot * J + j
                        back = not isinstance(d, int) or d > 0
                        variance(d, s, d_q1, sq1, mean1, var1, d_m1, d_v1)
                        if exists(d + 3):
                            copy(d + 3, s + 3)
                        first_norm(d, s)
                        if back:
                            variance(d - 1, s + 7, d_q2, sq2, mean2, var2, d_m2, d_v2)
                        if exists(d + 1):
                            residual(d + 1, s + 1)
                        if back:
                            bs = (s + 7) % 8
                            second_norm(d - 1, bs, turn - 1 if s == 0 else turn)
                        rows(g, slot, turn, j)
                for d in range(3):
                    copy(d, d)
                residual(0, 0)
                group(0, 0, 0)
                group(1, 1, 0)
                loop_from(eng, 2, E_GROUPS - 1, 2, group)
                group(E_GROUPS - 1, (E_GROUPS - 1) % 2, (E_GROUPS - 1) // 2)
                d = N_TILES - 1
                variance(d, d % 8, d_q2, sq2, mean2, var2, d_m2, d_v2)
                second_norm(d, d % 8, d // 8)

        with ExitStack() as ctx:
            sb, psum, sem, ring = makers = tools(nc, ctx, "relations")
            idx = sb("idx", [P, 2, 2], I32)
            W = sb("W", [P, 2, 2, OUT])
            xr = sb("xr", [P, 2, J, IN])
            xrT = sb("xrT", [P, 2, 2 * P])
            msg = sb("msg", [P, 2, J, OUT])
            pT, pM = psum("pT", 2), psum("pM", 4)
            i_loaded, x_loaded, w_got, m_stored = (ring(n) for n in ("i_loaded", "x_loaded", "w_got", "m_stored"))
            s_T, c_T, s_M, c_M, s_begun = (sem(n) for n in ("s_T", "c_T", "s_M", "c_M", "s_begun"))
            block = ctx.enter_context(nc.Block())
            x_tiles = x1_by_rel.rearrange("(m q p) f -> m p q f", q=J, p=P)
            msg_tiles = msg_by_rel.rearrange("(m q p) f -> m p q f", q=J, p=P)
            weight_rows = rel_weights.rearrange("r i o -> (r i) o")

            @block.sync
            def _(eng):
                def load(m, slot):
                    eng.dma_start(idx[:, slot, :], cols(weight_home, m * 2, 2)).then_inc(i_loaded[slot], 16)
                    eng.dma_start(xr[:, slot], at(x_tiles, m)).then_inc(x_loaded[slot], 16)

                def group(m, slot, turn):
                    eng.wait_ge(s_M, m + 1)
                    if not isinstance(m, int) or m + 2 < R_GROUPS:
                        load(m + 2, slot)
                    eng.wait_ge(c_M, m + 3)
                    eng.dma_start(at(msg_tiles, m), msg[:, slot]).then_inc(m_stored[slot], 16)
                load(0, 0)
                load(1, 1)
                loop(eng, R_GROUPS - 2, 2, group)
                for m in range(R_GROUPS - 2, R_GROUPS):
                    group(m, m % 2, m // 2)
                for slot in range(2):
                    eng.wait_ge(m_stored[slot], 16 * len(range(slot, R_GROUPS, 2)) + 16)

            @block.gpsimd
            def _(eng):
                def gather(m, slot, turn):
                    eng.wait_ge(i_loaded[slot], 16 * turn + 16)
                    eng.sem_inc(s_begun, 1)
                    for h in range(2):
                        eng.indirect_dma_start(W[:, slot, h, :], None, weight_rows,
                                               bass.IndirectOffsetOnAxis(ap=idx[:, slot, h:h + 1], axis=0))\
                            .then_inc(w_got[slot], 16)
                loop(eng, R_GROUPS, 2, gather)

            @block.tensor
            def _(eng):
                def turn_rows(m, slot, turn):
                    eng.wait_ge(x_loaded[slot], 16 * turn + 16)
                    eng.wait_ge(c_T, m + 1)
                    for h in range(2):
                        ins = eng.transpose(pT[:, slot, h * P:(h + 1) * P], xr[:, slot, 2 * h:2 * h + 2, :], ident[:])
                    ins.then_inc(s_T, 1)

                def products(m, slot, turn):
                    eng.wait_ge(w_got[slot], 32 * turn + 32)
                    eng.wait_ge(c_T, m + 3)
                    eng.wait_ge(c_M, m + 2)
                    for h in range(2):
                        for k in range(2):
                            half = slice(k * IN, (k + 1) * IN)
                            ins = eng.matmul(pM[:, 2 * slot + k, h * OUT:(h + 1) * OUT], xrT[half, slot, h * P:(h + 1) * P],
                                             W[half, slot, h, :], start=True, stop=True)
                    ins.then_inc(s_M, 1)

                def group(m, slot, turn):
                    if not isinstance(m, int) or m + 1 < R_GROUPS:
                        turn_rows(m + 1, *later(slot, turn, 1, 2))
                    products(m, slot, turn)
                turn_rows(0, 0, 0)
                loop(eng, R_GROUPS - 1, 2, group)
                m = R_GROUPS - 1
                group(m, m % 2, m // 2)

            @block.scalar
            def _(eng):
                eng.sem_inc(c_T, 2)

                def copy(m, slot, turn):
                    eng.wait_ge(s_T, m + 1)
                    eng.wait_ge(c_M, m + 1)
                    eng.activation(xrT[:, slot, :], pT[:, slot, 0:2 * P], ACT.Copy).then_inc(c_T, 1)
                loop(eng, R_GROUPS, 2, copy)

            @block.vector
            def _(eng):
                eng.sem_inc(c_M, 2)
                for slot in range(2):
                    eng.sem_inc(m_stored[slot], 16)

                def copy(m, slot, turn):
                    eng.wait_ge(s_M, m + 1)
                    eng.wait_ge(m_stored[slot], 16 * turn + 16)
                    eng.tensor_copy(msg[:, slot].rearrange("p (h k) f -> p k h f", k=2),
                                    pM[:, 2 * slot:2 * slot + 2, 0:P].rearrange("p k (h f) -> p k h f", h=2))\
                        .then_inc(c_M, 1)
                loop(eng, R_GROUPS, 2, copy)

        RING = 4
        with ExitStack() as ctx:
            sb, psum, sem, ring = makers = tools(nc, ctx, "final")
            runs = RunSums(makers, dst_rows, dst_col, prev_last, OUT)
            idx = sb("idx", [P, RING, 2, J], I32)
            M = sb("M", [P, RING, J, OUT])
            v = sb("v", [P, RING, J, OUT])
            A2 = sb("A2", [P, RING, J, OUT])
            A3 = sb("A3", [P, RING, J, OUT])
            x1 = sb("x1", [P, RING, J, OUT])
            x1T = sb("x1T", [P, 2, 2 * P])
            y = sb("y", [P, RING, J, OUT])
            o = sb("o", [P, RING, J, OUT])
            stats = sb("stats", [P, 2, RING, J, 6])
            mv = sb("mv", [P, 2, RING, J, 2])
            std = sb("std", [P, 2, RING, 2, J])
            pT, pY = psum("pT"), psum("pY")
            i_loaded, t_loaded, gathered, scattered = (ring(n, RING) for n in ("i_loaded", "t_loaded", "gathered", "scattered"))
            s_v, s_x1, s_T, c_T, s_Y, c_Y, s_yb, s_y, s_o, s_begun, s_wait = (
                sem(n) for n in ("s_v", "s_x1", "s_T", "c_T", "s_Y", "c_Y", "s_yb", "s_y", "s_o", "s_begun", "s_wait"))
            n_stats, n_mv, n_var, n_std, n_r = ([sem(f"{n}{i}") for i in range(2)]
                                                for n in ("n_stats", "n_mv", "n_var", "n_std", "n_r"))
            block = ctx.enter_context(nc.Block())

            def has(h):
                return not isinstance(h, int) or 0 <= h < E_GROUPS

            @block.sync
            def _(eng):
                def load(h, slot):
                    eng.dma_start(idx[:, slot, 0, :], cols(rel_home, h * J, J)).then_inc(i_loaded[slot], 16)
                    eng.dma_start(idx[:, slot, 1, :], cols(out_home, h * J, J)).then_inc(i_loaded[slot], 16)
                    eng.dma_start(v[:, slot].rearrange("p j f -> p (j f)"), at(u_dst, h)).then_inc(t_loaded[slot], 16)
                    eng.dma_start(A2[:, slot].rearrange("p j f -> p (j f)"), at(agg2_g, h)).then_inc(t_loaded[slot], 16)

                def group(g, slot, turn):
                    if has(g + 2):
                        eng.wait_ge(runs.scaled, J * g + J + 2)
                        runs.load(eng, g + 2, slot % 2)
                    if has(g + 3) and (not isinstance(g, int) or g > 0):
                        s3, t3 = later(slot, turn, 3, RING)
                        eng.wait_ge(scattered[s3], 16 * J * t3)
                        load(g + 3, s3)
                for h in range(RING):
                    load(h, h)
                for h in range(2):
                    runs.load(eng, h, h)
                for g in range(RING):
                    group(g, g, 0)
                loop_from(eng, RING, E_GROUPS - 3, RING, group)
                for g in range(E_GROUPS - 3, E_GROUPS):
                    group(g, g % RING, g // RING)

            @block.gpsimd
            def _(eng):
                def gather(h, slot, turn):
                    eng.wait_ge(i_loaded[slot], 32 * turn + 32)
                    eng.sem_inc(s_begun, 1)
                    for j in range(J):
                        eng.indirect_dma_start(M[:, slot, j, :], None, msg_by_rel,
                                               bass.IndirectOffsetOnAxis(ap=idx[:, slot, 0, j:j + 1], axis=0))\
                            .then_inc(gathered[slot], 16)

                def scatter(h, slot):
                    eng.wait_ge(s_o, h + 1)
                    eng.sem_inc(s_begun, 1)
                    for j in range(J):
                        eng.indirect_dma_start(out, bass.IndirectOffsetOnAxis(ap=idx[:, slot, 1, j:j + 1], axis=0),
                                               o[:, slot, j, :], None, bounds_check=N_NODES - 1, oob_is_err=False)\
                            .then_inc(scattered[slot], 16)

                def group(g, slot, turn):
                    if has(g + 2):
                        gather(g + 2, *later(slot, turn, 2, RING))
                    scatter(g, slot)
                gather(0, 0, 0)
                gather(1, 1, 0)
                loop(eng, E_GROUPS - 2, RING, group)
                for g in range(E_GROUPS - 2, E_GROUPS):
                    group(g, g % RING, g // RING)
                for slot in range(RING):
                    eng.wait_ge(scattered[slot], 16 * J * len(range(slot, E_GROUPS, RING)))

            @block.tensor
            def _(eng):
                def turn_rows(h, slot):
                    eng.wait_ge(s_x1, h + 1)
                    eng.wait_ge(c_T, h + 1)
                    for i in range(2):
                        ins = eng.transpose(pT[:, i * P:(i + 1) * P], x1[:, slot, 2 * i:2 * i + 2, :], ident[:])
                    ins.then_inc(s_T, 1)

                def own(h, slot):
                    eng.wait_ge(c_T, h + 2)
                    eng.wait_ge(c_Y, h + 1)
                    for i in range(2):
                        ins = eng.matmul(pY[:, i * P:(i + 1) * P], x1T[:, slot % 2, i * P:(i + 1) * P], Ws2[:],
                                         start=True, stop=True)
                    ins.then_inc(s_Y, 1)

                def group(g, slot, turn):
                    eng.wait_ge(gathered[slot], 16 * J * turn + 16 * J)
                    for j in range(J):
                        runs.add(eng, g, slot % 2, j, M[:, slot, j, :])
                        if has(g + 1) and j == 0:
                            turn_rows(g + 1, (slot + 1) % RING)
                        if has(g + 1) and j == 2:
                            own(g + 1, (slot + 1) % RING)
                turn_rows(0, 0)
                own(0, 0)
                loop(eng, E_GROUPS - 1, RING, group)
                g = E_GROUPS - 1
                group(g, g % RING, g // RING)

            @block.scalar
            def _(eng):
                eng.sem_inc(runs.scaled, 2)
                eng.sem_inc(c_T, 1)

                def copy(h, slot):
                    eng.wait_ge(s_T, h + 1)
                    eng.wait_ge(c_Y, h + 1)
                    eng.activation(x1T[:, slot % 2, :], pT[:, 0:2 * P], ACT.Copy).then_inc(c_T, 1)

                def root(n, h, slot):
                    eng.wait_ge(n_var[n], h + 1)
                    eng.activation(std[:, n, slot, 0, :], mv[:, n, slot, :, 1], ACT.Sqrt).then_inc(n_std[n], 1)

                def group(g, slot, turn):
                    for j in range(J):
                        runs.scale(eng, g, j, A3[:, slot, j, :], weight_col)
                        if has(g + 1) and j == 0:
                            copy(g + 1, (slot + 1) % RING)
                        if has(g + 2) and j == 1:
                            root(0, g + 2, (slot + 2) % RING)
                        if has(g - 1) and j == 1:
                            root(1, g - 1, (slot + 3) % RING)
                root(0, 0, 0)
                copy(0, 0)
                root(0, 1, 1)
                for g in range(RING):
                    group(g, g, 0)
                loop_from(eng, RING, E_GROUPS - 2, RING, group)
                for g in range(E_GROUPS - 2, E_GROUPS):
                    group(g, g % RING, g // RING)
                root(1, E_GROUPS - 1, (E_GROUPS - 1) % RING)

            @block.vector
            def _(eng):
                eng.sem_inc(c_Y, 1)
                runs.start_vector(eng)
                bias_all = bias_row[:].unsqueeze(1).to_broadcast([P, J, OUT])

                def moments(n, h, slot, rows, ready):
                    eng.wait_ge(ready, h + 1)
                    for q in range(J):
                        ins = eng.bn_stats(stats[:, n, slot, q, :], rows[:, slot, q, :])
                    ins.then_inc(n_stats[n], 1)

                def aggregate(n, h, slot):
                    eng.wait_ge(n_stats[n], h + 1)
                    eng.sem_inc(s_wait, 1)
                    for q in range(J):
                        ins = eng.bn_aggr(mv[:, n, slot, q, :], stats[:, n, slot, q, :])
                    ins.then_inc(n_mv[n], 1)
                    eng.wait_ge(n_mv[n], h + 1)
                    eng.tensor_scalar(mv[:, n, slot, :, 1], mv[:, n, slot, :, 1], LN_EPS, None, ALU.add)\
                        .then_inc(n_var[n], 1)

                def normalize(n, h, slot, rows, to, done):
                    eng.wait_ge(n_std[n], h + 1)
                    eng.reciprocal(std[:, n, slot, 1, :], std[:, n, slot, 0, :]).then_inc(n_r[n], 1)
                    eng.wait_ge(n_r[n], h + 1)
                    for q in range(J):
                        ins = eng.tensor_scalar(to[:, slot, q, :], rows[:, slot, q, :], mv[:, n, slot, q, 0:1],
                                                std[:, n, slot, 1, q:q + 1], ALU.subtract, ALU.mult)
                    ins.then_inc(done, 1)

                def first_sum(h, slot, turn):
                    eng.wait_ge(t_loaded[slot], 32 * turn + 32)
                    eng.tensor_tensor(v[:, slot], v[:, slot], A2[:, slot], ALU.add).then_inc(s_v, 1)
                    moments(0, h, slot, v, s_v)

                def own_sum(h, slot):
                    eng.wait_ge(s_Y, h + 1)
                    eng.tensor_tensor(y[:, slot], pY[:, 0:J * OUT].rearrange("p (j f) -> p j f", j=J), x1[:, slot],
                                      ALU.add).then_inc(c_Y, 1)
                    eng.wait_ge(c_Y, h + 2)
                    eng.tensor_tensor(y[:, slot], y[:, slot], bias_all, ALU.add).then_inc(s_yb, 1)

                def second_sum(h, slot):
                    eng.wait_ge(s_yb, h + 1)
                    eng.wait_ge(runs.scaled, J * h + J + 2)
                    eng.tensor_tensor(y[:, slot], y[:, slot], A3[:, slot], ALU.add).then_inc(s_y, 1)
                    moments(1, h, slot, y, s_y)

                def group(g, slot, turn):
                    nxt, ahead, back = (slot + 1) % RING, (slot + 2) % RING, (slot + 3) % RING
                    for j in range(J):
                        runs.keep(eng, g, j)
                        if j == 0:
                            if has(g - 1):
                                second_sum(g - 1, back)
                            if has(g + 2):
                                first_sum(g + 2, *later(slot, turn, 2, RING))
                        if j == 1:
                            if has(g + 2):
                                aggregate(0, g + 2, ahead)
                            if has(g - 1):
                                aggregate(1, g - 1, back)
                            if has(g + 1):
                                runs.select(eng, g + 1, nxt % 2, later(slot, turn, 1, RING)[1] * 2 + nxt // 2)
                        if j == 2 and has(g - 1):
                            normalize(1, g - 1, back, y, o, s_o)
                        if j == 3:
                            if has(g + 2):
                                normalize(0, g + 2, ahead, v, x1, s_x1)
                            if has(g + 1):
                                own_sum(g + 1, nxt)
                for h in range(2):
                    first_sum(h, h, 0)
                    aggregate(0, h, h)
                    normalize(0, h, h, v, x1, s_x1)
                runs.select(eng, 0, 0, 0)
                own_sum(0, 0)
                for g in range(RING):
                    group(g, g, 0)
                loop_from(eng, RING, E_GROUPS - 2, RING, group)
                for g in range(E_GROUPS - 2, E_GROUPS):
                    group(g, g % RING, g // RING)
                g = E_GROUPS - 1
                second_sum(g, g % RING)
                aggregate(1, g, g % RING)
                normalize(1, g, g % RING, y, o, s_o)


_INS = ['x', 'src', 'dst', 'edge_type_32', 'L0_gnn_Wl0', 'L0_gnn_Wr0', 'L0_gnn_b0', 'L0_gnn_Wl1', 'L0_gnn_Wr1',
        'L0_gnn_b1', 'L0_gnn_Wl2', 'L0_gnn_Wr2', 'L0_gnn_b2', 'L0_gnn_g0', 'L0_gnn_be0', 'L0_gnn_g1', 'L0_gnn_be1',
        'L1_gnn_basis', 'L1_gnn_coeff', 'L1_gnn_self_weight', 'L1_gnn_bias']


def kernel(**inputs):
    import numpy as _np
    import concourse.bacc as _bacc
    from concourse import mybir as _mybir
    from concourse.bass_utils import run_bass_kernel_spmd as _run

    nc = _bacc.Bacc("TRN2", target_bir_lowering=False, num_devices=1)
    arrays, args = {}, []
    for name in _INS:
        a = _np.ascontiguousarray(inputs[name])
        arrays[f"in_{name}"] = a
        args.append(nc.dram_tensor(f"in_{name}", a.shape, _mybir.dt.from_np(a.dtype), kind="ExternalInput").ap())
    args.append(nc.dram_tensor("out_0", (N_NODES, OUT), F32, kind="ExternalOutput").ap())
    gnn_program(nc, *args)
    return _run(nc, [arrays], core_ids=[0]).results[0]["out_0"]
```

```python
from contextlib import ExitStack

import concourse.bass as bass
import concourse.mybir as mybir

ALU = mybir.AluOpType
ACT = mybir.ActivationFunctionType
AX = mybir.AxisListType
F32 = mybir.dt.float32
I32 = mybir.dt.int32

P = 128
N_NODES = 100000
N_EDGES = 25000
IN = 64
HID = 128
OUT = 64
N_REL = 32
N_BASES = 30
J = 4
GROUP = J * P
E_GROUPS = -(-N_EDGES // GROUP)
E_TILES = E_GROUPS * J
E_ROWS = E_TILES * P
ZERO_ROW = E_ROWS
HALF = E_TILES // 2
D_GROUPS = N_NODES // GROUP
TAIL = N_NODES - D_GROUPS * GROUP
TAIL_P = TAIL // J
R_GROUPS = -(-(E_TILES + N_REL - 1) // J)
R_TILES = R_GROUPS * J
PAD_DST = 1 << 23
BN_EPS = 1e-5
LN_EPS = 1e-5
assert TAIL_P * J == TAIL and 2 * IN == P and HID == P


def at(ap, g):
    if isinstance(g, int):
        return ap[g]
    names = "abcdefg"[: len(ap.shape) - 1]
    spaced = " ".join(names)
    rest = " ".join(names[1:])
    return ap[bass.ds(g, 1)].rearrange(f"z {spaced} -> (z {names[0]}) {rest}")


def cols(ap, start, n):
    return ap[:, bass.ds(start, n)] if not isinstance(start, int) else ap[:, start:start + n]


def later(slot, turn, k, ring):
    return (slot + k) % ring, turn + (slot + k) // ring


def loop(eng, n, unroll, body):
    turns = n // unroll
    if turns > 1:
        with eng.Fori(0, turns) as turn:
            for slot in range(unroll):
                body(turn * unroll + slot, slot, turn)
        first = turns * unroll
    else:
        first = 0
    for g in range(first, n):
        body(g, g % unroll, g // unroll)


def tools(nc, ctx, block):
    sems = []

    def clear():
        nc.clear_and_free_semaphores(sems)
        nc.all_engine_barrier()
    ctx.callback(clear)

    def sb(name, shape, dt=F32):
        return ctx.enter_context(nc.sbuf_tensor(f"{block}_{name}", shape, dt))

    def psum(name, banks=1):
        return ctx.enter_context(nc.psum_tensor(f"{block}_{name}", [P, 512] if banks == 1 else [P, banks, 512], F32))

    def sem(name):
        sems.append(nc.alloc_semaphore(f"{block}_{name}"))
        return sems[-1]

    def ring(name, n=2):
        return [sem(f"{name}{i}") for i in range(n)]

    return sb, psum, sem, ring


def loop_from(eng, first, n, unroll, body):
    turns = (n - first) // unroll
    with eng.Fori(0, turns) as k:
        turn = k + first // unroll
        for slot in range(unroll):
            body(turn * unroll + slot, slot, turn)
    for g in range(first + turns * unroll, n):
        body(g, g % unroll, g // unroll)


class Steps:

    def __init__(self, eng, sem, base=0):
        self.eng, self.sem, self.base, self.n = eng, sem, base, 0

    def did(self, instruction):
        instruction.then_inc(self.sem, 1)
        self.n += 1
        return self.base + self.n

    def settle(self):
        self.eng.wait_ge(self.sem, self.base + self.n)


class RunSums:

    def __init__(self, makers, dst_rows, dst_col, prev_last, width):
        sb, psum, sem, ring = makers
        self.dst_rows, self.dst_col, self.prev_last, self.width = dst_rows, dst_col, prev_last, width
        self.dst_tile = sb("run_dst_tile", [P, 2, GROUP], I32)
        self.S = sb("run_S", [P, 2, J, P])
        self.Q = sb("run_Q", [P, 2, J, P])
        self.kept = sb("run_kept", [P, 2, width])
        self.sums = psum("run_sums", 2)
        self.loaded = [sem(f"run_loaded{i}") for i in range(2)]
        self.selected = sem("run_selected")
        self.summed = sem("run_summed")
        self.copied = sem("run_copied")
        self.scaled = sem("run_scaled")

    def load(self, eng, g, slot):
        row = self.dst_rows[g:g + 1] if isinstance(g, int) else self.dst_rows[bass.ds(g, 1)]
        eng.dma_start(self.dst_tile[:, slot, :], row.rearrange("a c -> (a c)").partition_broadcast(P))\
            .then_inc(self.loaded[slot], 16)

    def start_vector(self, eng):
        eng.memset(self.kept[:, 1, :], 0.0).then_inc(self.copied, 1)

    def select(self, eng, g, slot, turn):
        eng.wait_ge(self.loaded[slot], 16 * turn + 16)
        tile = self.dst_tile[:, slot, :].rearrange("p (j c) -> p j c", j=J)
        for to, col in ((self.S, self.dst_col), (self.Q, self.prev_last)):
            eng.tensor_tensor(to[:, slot], tile, cols(col, g * J, J).unsqueeze(2).to_broadcast([P, J, P]),
                              ALU.is_equal).then_inc(self.selected, 1)

    def add(self, eng, g, slot, j, message):
        t = g * J + j
        if j == 0:
            eng.wait_ge(self.selected, 2 * g + 2)
        to = self.sums[:, j % 2, 0:self.width]
        eng.matmul(to, self.S[:, slot, j, :], message, start=True, stop=False)
        eng.wait_ge(self.copied, t + 1)
        eng.matmul(to, self.Q[:, slot, j, :], self.kept[:, (j + 1) % 2, :], start=False, stop=True)\
            .then_inc(self.summed, 1)

    def keep(self, eng, g, j):
        eng.wait_ge(self.summed, g * J + j + 1)
        eng.wait_ge(self.scaled, g * J + j + 1)
        eng.tensor_copy(self.kept[:, j % 2, :], self.sums[:, j % 2, 0:self.width]).then_inc(self.copied, 1)

    def scale(self, eng, g, j, to, weight_col):
        eng.wait_ge(self.copied, g * J + j + 2)
        eng.activation(to, self.kept[:, j % 2, 0:to.shape[-1]], ACT.Copy,
                       scale=cols(weight_col, g * J + j, 1)).then_inc(self.scaled, 1)


class GroupSums:

    FIRST = [0, J, 2 * J - 1, 3 * J - 3]

    def __init__(self, makers, dst_rows, dst_col, prev_last, width):
        sb, psum, sem, ring = makers
        self.dst_rows, self.dst_col, self.prev_last, self.width = dst_rows, dst_col, prev_last, width
        self.dst_tile = sb("run_dst_tile", [P, 2, GROUP], I32)
        self.R = sb("run_R", [P, 2, J * (J + 1) // 2, P])
        self.Q = sb("run_Q", [P, 2, J, P])
        self.kept = sb("run_kept", [P, 2, width])
        self.sums = psum("run_sums", 2)
        self.loaded = [sem(f"run_loaded{i}") for i in range(2)]
        self.selected = sem("run_selected")
        self.summed = sem("run_summed")
        self.copied = sem("run_copied")
        self.read = sem("run_read")

    def load(self, eng, g, slot):
        row = self.dst_rows[g:g + 1] if isinstance(g, int) else self.dst_rows[bass.ds(g, 1)]
        eng.dma_start(self.dst_tile[:, slot, :], row.rearrange("a c -> (a c)").partition_broadcast(P))\
            .then_inc(self.loaded[slot], 16)

    def start_vector(self, eng):
        eng.memset(self.kept[:, 1, :], 0.0).then_inc(self.copied, 1)
        eng.sem_inc(self.read, 1)

    def select(self, eng, g, slot, turn):
        eng.wait_ge(self.loaded[slot], 16 * turn + 16)
        for i in range(J):
            to = self.R[:, slot, self.FIRST[i]:self.FIRST[i] + J - i, :].rearrange("p j c -> p (j c)")
            eng.tensor_scalar(to, self.dst_tile[:, slot, i * P:], cols(self.dst_col, g * J + i, 1), None,
                              ALU.is_equal).then_inc(self.selected, 1)
        eng.tensor_scalar(self.Q[:, slot].rearrange("p j c -> p (j c)"), self.dst_tile[:, slot, :],
                          cols(self.prev_last, g * J, 1), None, ALU.is_equal).then_inc(self.selected, 1)

    def place(self, slot, j):
        return self.sums[:, slot, j * self.width:(j + 1) * self.width]

    def add(self, eng, g, slot, message):
        eng.wait_ge(self.selected, (J + 1) * g + J + 1)
        eng.wait_ge(self.read, g + 1)
        for j in range(J):
            for i in range(j + 1):
                eng.matmul(self.place(slot, j), self.R[:, slot, self.FIRST[i] + j - i, :], message(i),
                           start=j == 0 and i == 0, stop=False)

    def carry(self, eng, g, slot):
        eng.wait_ge(self.copied, g + 1)
        for j in range(J):
            ins = eng.matmul(self.place(slot, j), self.Q[:, slot, j, :], self.kept[:, (slot + 1) % 2, :],
                             start=False, stop=j == J - 1)
        ins.then_inc(self.summed, 1)

    def keep(self, eng, g, slot):
        eng.wait_ge(self.summed, g + 1)
        eng.tensor_copy(self.kept[:, slot, :], self.place(slot, J - 1)).then_inc(self.copied, 1)

    def means(self, eng, slot, to, weight_col, g):
        n = to.shape[-1]
        rows = self.sums[:, slot, 0:J * self.width].rearrange("p (j f) -> p j f", j=J)[:, :, 0:n]
        eng.tensor_tensor(to, rows, cols(weight_col, g * J, J).unsqueeze(2).to_broadcast([P, J, n]), ALU.mult)\
            .then_inc(self.read, 1)


def gnn_program(nc, x, src, dst, edge_type_32, Wl0, Wr0, b0, Wl1, Wr1, b1, Wl2, Wr2, b2,
                g0, be0, g1, be1, basis, coeff, self_weight, bias, out):
    persistent = ExitStack()

    def scratch(name, shape, dt=F32):
        return nc.dram_tensor(name, shape, dt).ap()

    src_flat = scratch("src_flat", [E_ROWS], I32)
    dst_flat = scratch("dst_flat", [E_ROWS + P], I32)
    typ_flat = scratch("typ_flat", [E_ROWS], I32)
    edge_sorted = scratch("edge_sorted", [E_ROWS, 3], I32)
    x_src = scratch("x_src", [E_GROUPS, P, J * IN])
    x_dst = scratch("x_dst", [E_GROUPS, P, J * IN])
    agg0 = scratch("agg0", [E_ROWS + 1, IN])
    agg1 = scratch("agg1", [E_ROWS + 1, HID])
    agg2 = scratch("agg2", [E_ROWS + 1, OUT])
    h0_src = scratch("h0_src", [E_GROUPS, P, GROUP])
    h0_dst = scratch("h0_dst", [E_GROUPS, P, GROUP])
    h1_dst = scratch("h1_dst", [E_GROUPS, P, GROUP])
    u_src = scratch("u_src", [E_GROUPS, P, J * OUT])
    u_dst = scratch("u_dst", [E_GROUPS, P, J * OUT])
    x1_by_rel = scratch("x1_by_rel", [R_TILES * P, OUT])
    msg_by_rel = scratch("msg_by_rel", [R_TILES * P, OUT])
    rel_weights = scratch("rel_weights", [N_REL, IN, OUT])

    def grouped(a, width):
        return a[0:E_ROWS].rearrange("(g p j) f -> g p (j f)", p=P, j=J)

    slot_home = scratch("slot_home", [P, E_TILES], I32)
    rel_home = scratch("rel_home", [P, E_TILES], I32)
    weight_home = scratch("weight_home", [P, R_TILES // 2], I32)
    out_home = scratch("out_home", [P, E_TILES], I32)

    agg0_g, agg1_g, agg2_g = grouped(agg0, IN), grouped(agg1, HID), grouped(agg2, OUT)
    src_table = src_flat.rearrange("(t c) -> t c", c=P)
    dst_table = dst_flat[0:E_ROWS].rearrange("(t c) -> t c", c=P)
    typ_table = typ_flat.rearrange("(t c) -> t c", c=P)
    dst_next = dst_flat[1:E_ROWS + 1].rearrange("(t c) -> t c", c=P)

    with ExitStack() as ctx:
        sb, psum, sem, ring = makers = tools(nc, ctx, "order")
        rows_i = sb("rows_i", [HALF, 4, 2, P], I32)
        falls = sb("falls", [HALF, 2, P])
        n_falls = sb("n_falls", [HALF, 2])
        any_fall = sb("any_fall", [1, 1], I32)
        col_i = sb("col_i", [P, 3, E_TILES], I32)
        dst_f = sb("dst_f", [P, E_TILES])
        every = sb("every", [P, E_ROWS], I32)
        SEG = E_ROWS // 8
        junk = sb("junk", [P, SEG])
        lower = sb("lower", [P, P])
        tie = sb("tie", [P, P])
        counts = sb("counts", [P, 9])
        rank = sb("rank", [P, 1])
        rank_i = sb("rank_i", [P, 2, 1], I32)
        edge = sb("edge", [P, 2, 3], I32)
        pF = psum("pF")
        s_edges, s_loaded, s_out, s_next = sem("s_edges"), sem("s_loaded"), sem("s_out"), sem("s_next")
        s_falls, s_summed, s_flag = sem("s_falls"), sem("s_summed"), sem("s_flag")
        s_cols, s_lower, s_float, s_count = sem("s_cols"), sem("s_lower"), sem("s_float"), sem("s_count")
        s_staged, s_gone, s_free, s_back = sem("s_staged"), ring("s_gone"), sem("s_free"), sem("s_back")
        block = ctx.enter_context(nc.Block())
        FULL = N_EDGES // P
        REST = N_EDGES - FULL * P
        tables = (src_table, dst_table, typ_table)
        flats = (src_flat, dst_flat[0:E_ROWS], typ_flat)

        @block.sync
        def _(eng):
            eng.wait_ge(s_edges, 2)
            for n, a in enumerate((src, dst, edge_type_32)):
                eng.dma_start(rows_i[:, n, 0, :], a[0:HALF * P].rearrange("(t c) -> t c", c=P)).then_inc(s_loaded, 16)
                eng.dma_start(rows_i[0:FULL - HALF, n, 1, :],
                              a[HALF * P:FULL * P].rearrange("(t c) -> t c", c=P)).then_inc(s_loaded, 16)
                eng.dma_start(rows_i[FULL - HALF:FULL - HALF + 1, n, 1, 0:REST],
                              a[FULL * P:N_EDGES].rearrange("(t c) -> t c", t=1)).then_inc(s_loaded, 16)
            eng.wait_ge(s_loaded, 16 * 9)
            for n in range(3):
                for h in range(2):
                    eng.dma_start(tables[n][h * HALF:(h + 1) * HALF], rows_i[:, n, h, :]).then_inc(s_out, 16)
            eng.dma_start(dst_flat[E_ROWS:E_ROWS + P].rearrange("(t c) -> t c", t=1),
                          rows_i[HALF - 1:HALF, 3, 0, :]).then_inc(s_out, 16)
            eng.wait_ge(s_out, 16 * 7)
            for h in range(2):
                eng.dma_start(rows_i[:, 3, h, :], dst_next[h * HALF:(h + 1) * HALF]).then_inc(s_next, 16)
            eng.wait_ge(s_flag, 1)
            with eng.If(eng.value_load(any_fall[0:1, 0:1]) != 0), \
                    nc.allow_non_contiguous_dma(reason="only where edges come out of order"):
                for n in range(3):
                    for c in range(0, E_TILES, 28):
                        eng.dma_start(col_i[:, n, c:c + 28], flats[n][c * P:(c + 28) * P].rearrange("(t p) -> p t", p=P))\
                            .then_inc(s_cols, 16)
                eng.dma_start(every[:], flats[1].partition_broadcast(P)).then_inc(s_cols, 16)
                eng.wait_ge(s_free, 2 + E_TILES)
                for n in range(3):
                    for c in range(0, E_TILES, 28):
                        rows = slice(c * P, (c + 28) * P)
                        eng.dma_start(flats[n][rows].rearrange("(e a) -> e a", a=1), edge_sorted[rows, n:n + 1])\
                            .then_inc(s_back, 16)
                eng.wait_ge(s_back, 16 * 3 * (E_TILES // 28))

        @block.tensor
        def _(eng):
            eng.wait_ge(s_falls, 2)
            eng.matmul(pF[0:1, 0:1], n_falls[:, 0:1], n_falls[:, 1:2], start=True, stop=True).then_inc(s_summed, 1)

        @block.gpsimd
        def _(eng):
            eng.wait_ge(s_flag, 1)
            with eng.If(eng.value_load(any_fall[0:1, 0:1]) != 0):
                eng.memset(lower[:], 1.0).then_inc(s_lower, 1)
                eng.wait_ge(s_lower, 1)
                eng.affine_select(out=lower[:], in_=lower[:], compare_op=ALU.is_gt, fill=0.0,
                                  base=0, pattern=[[-1, P]], channel_multiplier=1).then_inc(s_lower, 1)

                def scatter(t, slot, turn):
                    eng.wait_ge(s_staged, 2 * t + 2)
                    eng.sem_inc(s_lower, 1)
                    eng.indirect_dma_start(edge_sorted, bass.IndirectOffsetOnAxis(ap=rank_i[:, slot, :], axis=0),
                                           edge[:, slot, :], None).then_inc(s_gone[slot], 16)
                    eng.wait_ge(s_gone[slot], 16 * turn + 16)
                    eng.sem_inc(s_free, 1)
                loop(eng, E_TILES, 2, scatter)

        @block.vector
        def _(eng):
            eng.memset(rows_i[:], 0).then_inc(s_edges, 1)
            eng.wait_ge(s_edges, 1)
            eng.memset(rows_i[:, 1:4:2, :, :], PAD_DST).then_inc(s_edges, 1)
            eng.memset(n_falls[:, 1:2], 1.0).then_inc(s_falls, 1)
            eng.wait_ge(s_loaded, 16 * 9)
            eng.wait_ge(s_next, 32)
            eng.tensor_tensor(falls[:], rows_i[:, 1], rows_i[:, 3], ALU.is_gt).then_inc(s_count, 1)
            eng.wait_ge(s_count, 1)
            eng.tensor_reduce(n_falls[:, 0:1], falls[:], AX.XY, ALU.add).then_inc(s_falls, 1)
            eng.wait_ge(s_summed, 1)
            eng.tensor_copy(any_fall[:], pF[0:1, 0:1]).then_inc(s_flag, 1)
            eng.wait_ge(s_flag, 1)
            with eng.If(eng.value_load(any_fall[0:1, 0:1]) != 0):
                eng.wait_ge(s_cols, 16 * (3 * (E_TILES // 28) + 1))
                eng.wait_ge(s_lower, 2)
                eng.tensor_copy(dst_f[:], col_i[:, 1, :]).then_inc(s_float, 1)
                every_f = every[:].bitcast(F32)
                eng.tensor_copy(every_f, every[:]).then_inc(s_float, 1)
                eng.wait_ge(s_float, 2)
                eng.sem_inc(s_free, 2)
                STEPS = 12

                def count(t, slot, turn):
                    own = cols(every_f, t * P, P)
                    mine = cols(dst_f, t, 1)
                    n = t * STEPS + 1
                    for i in range(8):
                        eng.tensor_scalar(junk[:], every_f[:, i * SEG:(i + 1) * SEG], mine, 0.0, ALU.is_lt, ALU.add,
                                          accum_out=counts[:, i:i + 1]).then_inc(s_count, 1)
                        eng.wait_ge(s_count, n + i + 1)
                    eng.scalar_tensor_tensor(tie[:], own, mine, lower[:], ALU.is_equal, ALU.mult).then_inc(s_count, 1)
                    eng.wait_ge(s_count, n + 9)
                    eng.tensor_reduce(counts[:, 8:9], tie[:], AX.X, ALU.add).then_inc(s_count, 1)
                    eng.tensor_scalar(own, own, -0.5, None, ALU.add).then_inc(s_count, 1)
                    eng.wait_ge(s_count, n + 11)
                    eng.tensor_reduce(rank[:], counts[:], AX.X, ALU.add).then_inc(s_count, 1)
                    eng.wait_ge(s_count, n + 12)
                    eng.wait_ge(s_free, t + 1)
                    eng.tensor_copy(rank_i[:, slot, :], rank[:]).then_inc(s_staged, 1)
                    eng.tensor_copy(edge[:, slot, :].unsqueeze(2), col_i[:, :, bass.ds(t, 1)]).then_inc(s_staged, 1)
                    eng.wait_ge(s_staged, 2 * t + 2)
                loop(eng, E_TILES, 2, count)

    def keep(name, shape, dt=F32):
        return persistent.enter_context(nc.sbuf_tensor(name, shape, dt))

    with persistent:
        ident = keep("ident", [P, P])
        ones = keep("ones", [P, P])
        src_col = keep("src_col", [P, E_TILES])
        dst_col = keep("dst_col", [P, E_TILES])
        typ_col = keep("typ_col", [P, E_TILES])
        prev_last = keep("prev_last", [P, E_TILES])
        last_col = keep("last_col", [P, E_TILES])
        weight_col = keep("weight_col", [P, E_TILES])
        slot_idx = keep("slot_idx", [P, E_TILES], I32)
        rel_pos = keep("rel_pos", [P, E_TILES], I32)
        out_idx = keep("out_idx", [P, E_TILES], I32)
        W0 = keep("W0", [P, HID])
        W0_top = keep("W0_top", [P, HID])
        W0_bot = keep("W0_bot", [P, HID])
        Wr1T = keep("Wr1T", [P, HID])
        Wl1T = keep("Wl1T", [P, HID])
        W2_msg = keep("W2_msg", [P, 2 * OUT])
        U_h = keep("U_h", [P, 2 * OUT])
        U_x = keep("U_x", [P, 4 * OUT])
        Ws2 = keep("Ws2", [P, 2 * OUT])
        b2_pair = keep("b2_pair", [P, 1])
        b2_row = keep("b2_row", [P, OUT])
        bias_row = keep("bias_row", [P, OUT])
        biasC_row = keep("biasC_row", [P, OUT])
        bn = keep("bn", [P, 16])
        G0, BE0, B0, G1, BE1, B1 = (bn[:, i:i + 1] for i in range(6))
        SC0, SH0, SH0D, SC1, SH1 = (bn[:, i:i + 1] for i in range(6, 11))
        gram = keep("gram", [P, P])
        zsum = keep("zsum", [P, 1])
        is_127 = keep("is_127", [P, 1])
        number = keep("number", [P, P])
        tile_of = keep("tile_of", [P, E_TILES])
        slot_base = keep("slot_base", [P, E_TILES])
        dst_in = keep("dst_in", [P, E_TILES])

        with ExitStack() as ctx:
            sb, psum, sem, ring = makers = tools(nc, ctx, "layout")
            rows_i = sb("rows_i", [HALF, 4, 2, P], I32)
            rows_f = sb("rows_f", [HALF, 4, 2, P])
            wraw = sb("wraw", [P, 7, P])
            w2raw = sb("w2raw", [OUT, 2, HID])
            ws_sb = sb("ws_sb", [IN, OUT])
            coeff_sb = sb("coeff_sb", [N_REL, N_BASES])
            coeffT = sb("coeffT", [N_BASES, N_REL])
            basis_sb = sb("basis_sb", [N_BASES, IN * OUT])
            rw_sb = sb("rw_sb", [N_REL, IN * OUT])
            zeros = sb("zeros", [P, 2048])
            rsel = sb("rsel", [P, 4])
            idT = sb("idT", [IN, P])
            r2cT = sb("r2cT", [OUT, P])
            mean_c = sb("mean_c", [P, 4])
            p = [psum(f"p{i}") for i in range(8)]
            s_loaded, s_weights = sem("s_loaded"), sem("s_weights")
            s_set = sem("s_set")
            s_const, s_zero, s_zeroed, s_pool = sem("s_const"), sem("s_zero"), sem("s_zeroed"), sem("s_pool")
            s_dve, s_pe, s_rw, s_rw_out = sem("s_dve"), sem("s_pe"), sem("s_rw"), sem("s_rw_out")
            block = ctx.enter_context(nc.Block())

            @block.gpsimd
            def _(eng):
                eng.memset(ident[:], 0.0).then_inc(s_pool, 1)
                eng.iota(rsel[:, 0:1].bitcast(I32), [[0, 1]], base=0, channel_multiplier=1).then_inc(s_pool, 1)
                eng.wait_ge(s_pool, 2)
                eng.affine_select(out=ident[:], in_=ident[:], compare_op=ALU.not_equal, fill=1.0,
                                  base=0, pattern=[[-1, P]], channel_multiplier=1).then_inc(s_const, 1)

            @block.sync
            def _(eng):
                for n, table in enumerate((src_table, dst_table, typ_table, dst_next)):
                    for h in range(2):
                        eng.dma_start(rows_i[:, n, h, :], table[h * HALF:(h + 1) * HALF]).then_inc(s_loaded, 16)
                eng.wait_ge(s_zero, 4)
                for d, s in ((wraw[:, 0, 0:IN], Wr0), (wraw[:, 0, IN:], Wl0), (wraw[:, 1, 0:IN], Wr0),
                             (wraw[:, 2, IN:], Wr0), (wraw[:, 3, :], Wr1), (wraw[:, 4, :], Wl1),
                             (w2raw[:, 0, :], Wl2), (w2raw[:, 1, :], Wr2), (ws_sb[:], self_weight),
                             (coeff_sb[:], coeff), (basis_sb[:], basis.rearrange("b i o -> b (i o)")),
                             (Ws2[0:IN, 0:OUT], self_weight), (Ws2[IN:P, OUT:], self_weight),
                             (b2_pair[0:IN], b2.rearrange("(p a) -> p a", a=1)),
                             (b2_pair[IN:P], b2.rearrange("(p a) -> p a", a=1)),
                             (b2_row[:], b2.partition_broadcast(P)), (bias_row[:], bias.partition_broadcast(P)),
                             (G0, g0.rearrange("(p a) -> p a", a=1)), (BE0, be0.rearrange("(p a) -> p a", a=1)),
                             (B0, b0.rearrange("(p a) -> p a", a=1)), (G1, g1.rearrange("(p a) -> p a", a=1)),
                             (BE1, be1.rearrange("(p a) -> p a", a=1)), (B1, b1.rearrange("(p a) -> p a", a=1))):
                    eng.dma_start(d, s).then_inc(s_weights, 16)
                for a in (agg0, agg1, agg2):
                    eng.dma_start(a[E_ROWS:E_ROWS + 1], zeros[0:1, 0:a.shape[1]]).then_inc(s_zeroed, 16)
                flat = x1_by_rel.rearrange("(p q) f -> p (q f)", p=P)
                width, n = flat.shape[1], 0
                for c in range(0, width, 2048):
                    w = min(2048, width - c)
                    eng.dma_start(flat[:, c:c + w], zeros[:, 0:w]).then_inc(s_zeroed, 16)
                    n += 1
                eng.wait_ge(s_rw, 8)
                eng.dma_start(rel_weights.rearrange("r i o -> r (i o)"), rw_sb[:]).then_inc(s_rw_out, 16)
                eng.wait_ge(s_zeroed, 16 * (3 + n))
                eng.wait_ge(s_rw_out, 16)

            @block.tensor
            def _(eng):
                t = Steps(eng, s_pe)
                eng.wait_ge(s_const, 1)
                eng.wait_ge(s_weights, 16 * 23)
                for n in range(4):
                    t.did(eng.transpose(p[0][:, n * P:(n + 1) * P], wraw[:, n, :], ident[:]))
                t.did(eng.transpose(p[1][:, 0:P], wraw[:, 4, :], ident[:]))
                for n in range(2):
                    t.did(eng.transpose(p[1][:, P + n * OUT:P + (n + 1) * OUT], w2raw[:, n, :], ident[0:OUT, 0:OUT]))
                t.did(eng.transpose(p[1][0:N_BASES, 256:256 + N_REL], coeff_sb[:], ident[0:N_REL, 0:N_REL]))
                eng.wait_ge(s_set, 1)
                for n in range(4):
                    for h in range(2):
                        t.did(eng.transpose(p[2 + n][:, h * HALF:(h + 1) * HALF], rows_f[:, n, h, :],
                                            ident[0:HALF, 0:HALF]))
                eng.wait_ge(s_dve, 8)
                for c in range(8):
                    if c >= 2:
                        eng.wait_ge(s_rw, c - 1)
                    t.did(eng.matmul(p[6 + c % 2][0:N_REL, :], coeffT[:], basis_sb[:, c * 512:(c + 1) * 512],
                                     start=True, stop=True))
                eng.wait_ge(s_dve, 13)
                t.did(eng.matmul(p[0][:, 0:OUT], idT[:], ws_sb[:], start=True, stop=True))
                t.did(eng.transpose(p[1][0:OUT, 0:P], U_h[:, 0:OUT], ident[:]))
                eng.wait_ge(s_dve, 14)
                t.did(eng.matmul(p[0][:, OUT:2 * OUT], r2cT[:], ws_sb[:], start=True, stop=True))

            @block.vector
            def _(eng):
                eng.memset(wraw[:], 0.0).then_inc(s_zero, 1)
                eng.memset(Ws2[:], 0.0).then_inc(s_zero, 1)
                eng.memset(zeros[:], 0.0).then_inc(s_zero, 1)
                eng.memset(ones[:], 1.0).then_inc(s_zero, 1)
                eng.wait_ge(s_loaded, 16 * 8)
                eng.tensor_copy(rows_f[:], rows_i[:]).then_inc(s_set, 1)
                t = Steps(eng, s_dve)
                eng.wait_ge(s_pe, 8)
                for n, w in enumerate((W0, W0_top, W0_bot, Wr1T)):
                    t.did(eng.tensor_copy(w[:], p[0][:, n * P:(n + 1) * P]))
                t.did(eng.tensor_copy(Wl1T[:], p[1][:, 0:P]))
                t.did(eng.tensor_copy(W2_msg[:], p[1][:, P:2 * P]))
                t.did(eng.tensor_copy(coeffT[:], p[1][0:N_BASES, 256:256 + N_REL]))
                t.did(eng.tensor_reduce(mean_c[:, 0:1], p[1][:, P + OUT:2 * P], AX.X, ALU.add))
                t.settle()
                t.did(eng.tensor_scalar(mean_c[:, 0:1], mean_c[:, 0:1], -1.0 / OUT, None, ALU.mult))
                t.settle()
                t.did(eng.tensor_scalar(U_h[:, 0:OUT], W2_msg[:, OUT:], mean_c[:, 0:1], None, ALU.add))
                for h in range(2):
                    t.did(eng.tensor_scalar(idT[:, h * OUT:(h + 1) * OUT], ident[0:OUT, 0:OUT], -1.0 / OUT, None, ALU.add))
                t.did(eng.memset(U_x[:], 0.0))
                eng.wait_ge(s_pe, 26)
                t.did(eng.tensor_copy(r2cT[:], p[1][0:OUT, 0:P]))
                t.settle()
                for h in range(2):
                    q = slice(h * IN, (h + 1) * IN)
                    t.did(eng.tensor_scalar(U_x[q, h * P:h * P + OUT], ident[q, q], -1.0 / OUT, None, ALU.add))
                eng.wait_ge(s_pe, 27)
                t.settle()
                t.did(eng.tensor_tensor(U_h[:, OUT:], U_h[:, 0:OUT], p[0][:, OUT:2 * OUT], ALU.add))
                for h in range(2):
                    q = slice(h * IN, (h + 1) * IN)
                    t.did(eng.tensor_tensor(U_x[q, h * P + OUT:(h + 1) * P], U_x[q, h * P:h * P + OUT],
                                            p[0][q, 0:OUT], ALU.add))
                t.settle()
                t.did(eng.tensor_reduce(mean_c[:, 1:2], U_h[:, OUT:], AX.X, ALU.add))
                for h in range(2):
                    q = slice(h * IN, (h + 1) * IN)
                    t.did(eng.tensor_reduce(mean_c[q, 2:3], U_x[q, h * P + OUT:(h + 1) * P], AX.X, ALU.add))
                t.did(eng.tensor_reduce(mean_c[:, 3:4], bias_row[:], AX.X, ALU.add))
                t.settle()
                t.did(eng.tensor_scalar(mean_c[:], mean_c[:], -1.0 / OUT, None, ALU.mult))
                t.settle()
                t.did(eng.tensor_scalar(U_h[:, OUT:], U_h[:, OUT:], mean_c[:, 1:2], None, ALU.add))
                for h in range(2):
                    q = slice(h * IN, (h + 1) * IN)
                    ux = U_x[q, h * P + OUT:(h + 1) * P]
                    t.did(eng.tensor_scalar(ux, ux, mean_c[q, 2:3], None, ALU.add))
                t.did(eng.tensor_scalar(biasC_row[:], bias_row[:], mean_c[:, 3:4], None, ALU.add))
                eng.wait_ge(s_pe, 16)
                t.did(eng.tensor_copy(src_col[:], p[2][:, 0:E_TILES]))
                t.did(eng.tensor_copy(dst_col[:], p[3][:, 0:E_TILES]))
                t.did(eng.tensor_copy(typ_col[:], p[4][:, 0:E_TILES]))
                t.did(eng.tensor_copy(rsel[:, 1:2], rsel[:, 0:1].bitcast(I32)))
                t.settle()
                t.did(eng.tensor_tensor(last_col[:], dst_col[:], p[5][:, 0:E_TILES], ALU.not_equal))
                t.did(eng.tensor_scalar(prev_last[:], dst_col[:], float(N_NODES), None, ALU.is_lt))
                t.did(eng.tensor_scalar(is_127[:], rsel[:, 1:2], float(P - 1), None, ALU.is_equal))
                t.settle()
                t.did(eng.tensor_tensor(last_col[:], last_col[:], prev_last[:], ALU.mult))
                t.settle()
                t.did(eng.memset(prev_last[:, 0:1], -1.0))
                t.did(eng.tensor_scalar(prev_last[:, 1:], dst_col[:, 0:E_TILES - 1], 1.0, is_127[:],
                                        ALU.add, ALU.mult))
                t.settle()
                t.did(eng.tensor_scalar(prev_last[:, 1:], prev_last[:, 1:], -1.0, None, ALU.add))
                t.did(eng.tensor_scalar(weight_col[:], dst_col[:], -float(PAD_DST), None, ALU.add))
                t.settle()
                t.did(eng.tensor_tensor(weight_col[:], weight_col[:], last_col[:], ALU.mult))
                t.settle()
                t.did(eng.tensor_scalar(out_idx[:], weight_col[:], float(PAD_DST), None, ALU.add))
                t.settle()

            @block.scalar
            def _(eng):
                for c in range(8):
                    eng.wait_ge(s_pe, 17 + c)
                    eng.activation(rw_sb[:, c * 512:(c + 1) * 512], p[6 + c % 2][0:N_REL, :], ACT.Copy).then_inc(s_rw, 1)

        RING = 4
        DRING = 8
        with ExitStack() as ctx:
            sb, psum, sem, ring = makers = tools(nc, ctx, "lookup")
            xd = sb("xd", [P, DRING, J * IN])
            xg = sb("xg", [P, RING, J * IN])
            idx = sb("idx", [P, RING, J], I32)
            tile_i = sb("tile_i", [P, 3, E_TILES], I32)
            tile_f = sb("tile_f", [P, 2, E_TILES])
            tile_first = sb("tile_first", [P, E_TILES])
            hit = sb("hit", [P, E_TILES])
            junk = sb("junk", [P, J, E_TILES])
            before = sb("before", [P, P])
            sel_row = sb("sel_row", [P, P])
            ramp = sb("ramp", [P, R_TILES], I32)
            ramp_f = sb("ramp_f", [P, R_TILES])
            hot = sb("hot", [P, N_REL, E_TILES])
            within = sb("within", [P, N_REL, E_TILES])
            count = sb("count", [P, N_REL, E_TILES])
            upto = sb("upto", [P, N_REL, E_TILES])
            rel = sb("rel", [P, 8, N_REL])
            rel_i = sb("rel_i", [P, N_REL], I32)
            part_id = sb("part_id", [P, 2], I32)
            cmp = sb("cmp", [P, R_TILES // 2, N_REL])
            rel_of = sb("rel_of", [P, R_TILES])
            rel_start = sb("rel_start", [P, 2])
            weight_row = sb("weight_row", [P, R_TILES // 2], I32)
            xsum = sb("xsum", [P, IN])
            zero = sb("zero", [P, 256])
            pGram = psum("pGram")
            pSum = psum("pSum")
            pFirst = psum("pFirst")
            pRel = psum("pRel", 4)
            s_const, s_dve = sem("s_const"), sem("s_dve")
            d_free, d_gram = sem("d_free"), sem("d_gram")
            d_loaded = [sem(f"d_loaded{i}") for i in range(DRING)]
            s_first = sem("s_first")
            s_hot, s_rel, s_rel_got = sem("s_hot"), sem("s_rel"), sem("s_rel_got")
            idx_ready, got, kept = sem("idx_ready"), ring("got", RING), ring("kept", RING)
            s_begun, s_count = sem("s_begun"), sem("s_count")
            s_slots, s_homes = sem("s_slots"), sem("s_homes")
            block = ctx.enter_context(nc.Block())
            x_dense = x[0:D_GROUPS * GROUP].rearrange("(g p q) f -> g p (q f)", p=P, q=J)
            x_tail = x[D_GROUPS * GROUP:N_NODES].rearrange("(p q) f -> p (q f)", q=J)
            hot_flat, within_flat, count_flat = (a[:].rearrange("p r t -> p (r t)") for a in (hot, within, count))
            WIDTH = N_REL * E_TILES
            CHUNKS = [(c, min(512, WIDTH - c)) for c in range(0, WIDTH, 512)]

            @block.sync
            def _(eng):
                def load(g, slot, turn):
                    eng.wait_ge(d_free, g + 1)
                    eng.dma_start(xd[:, slot, :], at(x_dense, g)).then_inc(d_loaded[slot], 16)
                loop(eng, D_GROUPS, DRING, load)
                eng.wait_ge(d_free, D_GROUPS + 1)
                slot = D_GROUPS % DRING
                eng.dma_start(xd[0:TAIL_P, slot, :], x_tail).then_inc(d_loaded[slot], 16)
                eng.dma_start(out_home, out_idx[:]).then_inc(s_homes, 16)
                eng.wait_ge(s_slots, 1)
                eng.dma_start(rel_home, rel_pos[:]).then_inc(s_homes, 16)
                eng.dma_start(weight_home, weight_row[:]).then_inc(s_homes, 16)
                eng.wait_ge(s_homes, 48)

            @block.gpsimd
            def _(eng):
                eng.iota(ramp[:], [[1, R_TILES]], base=0, channel_multiplier=0).then_inc(s_const, 1)
                eng.memset(before[:], 0.0).then_inc(s_const, 1)
                for h in range(2):
                    eng.iota(part_id[:, h:h + 1], [[0, 1]], base=-IN * h, channel_multiplier=1).then_inc(s_const, 1)
                eng.wait_ge(s_const, 4)
                eng.affine_select(out=before[:], in_=before[:], compare_op=ALU.is_ge, fill=1.0,
                                  base=0, pattern=[[-1, P]], channel_multiplier=1).then_inc(s_const, 1)

                def gather_x(g, slot, turn):
                    eng.wait_ge(idx_ready, g + 1)
                    eng.sem_inc(s_begun, 1)
                    for j in range(J):
                        eng.indirect_dma_start(xg[:, slot, j * IN:(j + 1) * IN], None, x,
                                               bass.IndirectOffsetOnAxis(ap=idx[:, slot, j:j + 1], axis=0))\
                            .then_inc(got[slot], 16)
                loop(eng, E_GROUPS, RING, gather_x)

            @block.scalar
            def _(eng):
                for slot in range(RING):
                    eng.sem_inc(kept[slot], 16)

                def stage(g, slot):
                    eng.activation(idx[:, slot, :], cols(src_col, g * J, J), ACT.Copy).then_inc(idx_ready, 1)

                def store(g, slot, turn):
                    eng.wait_ge(got[slot], 16 * J * turn + 16 * J)
                    eng.dma_start(at(x_src, g), xg[:, slot, :]).then_inc(kept[slot], 16)

                def both(g, slot, turn):
                    store(g, slot, turn)
                    ahead = (slot + 2) % RING
                    eng.wait_ge(kept[ahead], 16 * (turn + (slot + 2) // RING) + 16)
                    stage(g + 2, ahead)
                stage(0, 0)
                stage(1, 1)
                loop(eng, E_GROUPS - 2, RING, both)
                for g in range(E_GROUPS - 2, E_GROUPS):
                    store(g, g % RING, g // RING)
                for slot in range(RING):
                    eng.wait_ge(kept[slot], 16 * len(range(slot, E_GROUPS, RING)) + 16)

            @block.tensor
            def _(eng):
                eng.wait_ge(s_dve, 3)
                eng.matmul(pFirst[:, 0:E_TILES], sel_row[:], dst_col[:], start=True, stop=True).then_inc(s_first, 1)
                eng.matmul(pGram[0:IN, 0:IN], zero[:, 0:IN], zero[:, 0:IN], start=True, stop=False)
                eng.matmul(pSum[:, 0:J * IN], zero[:, 0:P], zero[:], start=True, stop=False)
                eng.sem_inc(d_free, DRING)

                def add(g, slot, turn, p=P, last=False):
                    eng.wait_ge(d_loaded[slot], 16 * turn + 16)
                    for q in range(J):
                        rows = xd[0:p, slot, q * IN:(q + 1) * IN]
                        eng.matmul(pGram[0:IN, 0:IN], rows, rows, start=False, stop=last and q == J - 1)
                    eng.matmul(pSum[:, 0:J * IN], ones[0:p, :], xd[0:p, slot, :], start=False,
                               stop=last).then_inc(d_free, 1)
                FIRST_PART = D_GROUPS // (2 * DRING) * DRING
                loop(eng, FIRST_PART, DRING, add)
                eng.wait_ge(s_hot, 1)
                eng.wait_ge(s_const, 5)
                for n, (c, w) in enumerate(CHUNKS):
                    if n >= 2:
                        eng.wait_ge(s_rel_got, 2 * (n - 1))
                    eng.matmul(pRel[:, n % 2, 0:w], before[:], hot_flat[:, c:c + w], start=True, stop=True).then_inc(s_rel, 1)
                    eng.matmul(pRel[:, 2 + n % 2, 0:w], ones[:], hot_flat[:, c:c + w], start=True, stop=True).then_inc(s_rel, 1)
                loop_from(eng, FIRST_PART, D_GROUPS, DRING, add)
                add(D_GROUPS, D_GROUPS % DRING, D_GROUPS // DRING, TAIL_P, True)

            @block.vector
            def _(eng):
                t = Steps(eng, s_dve)
                t.did(eng.memset(zero[:], 0.0))
                t.did(eng.memset(sel_row[:], 1.0))
                t.settle()
                t.did(eng.tensor_scalar(sel_row[:], sel_row[:], ident[:, 0:1], None, ALU.mult))
                t.did(eng.tensor_scalar(dst_in[:], dst_col[:], float(N_NODES - 1), None, ALU.min))
                eng.wait_ge(s_const, 5)
                t.did(eng.tensor_copy(ramp_f[:], ramp[:]))
                t.settle()
                t.did(eng.tensor_scalar(number[:], ramp_f[:, 0:P], 1.0, None, ALU.add))
                relid = ramp_f[:, 0:N_REL].unsqueeze(2).to_broadcast([P, N_REL, E_TILES])
                eng.tensor_tensor(hot[:], typ_col[:].unsqueeze(1).to_broadcast([P, N_REL, E_TILES]), relid,
                                  ALU.is_equal).then_inc(s_hot, 1)
                eng.wait_ge(s_first, 1)
                t.did(eng.tensor_copy(tile_first[:], pFirst[:, 0:E_TILES]))
                t.settle()

                def below(g, slot, turn):
                    for j in range(J):
                        eng.wait_ge(s_count, g * J + j + 1)
                        eng.tensor_scalar(junk[:, j, :], tile_first[:], cols(src_col, g * J + j, 1), 0.0,
                                          ALU.is_le, ALU.add, accum_out=cols(tile_of, g * J + j, 1)).then_inc(s_count, 1)
                eng.sem_inc(s_count, J)
                loop(eng, E_GROUPS, 1, below)
                eng.wait_ge(s_count, J + E_TILES)
                t.did(eng.tensor_scalar(tile_of[:], tile_of[:], -1.0, 0.0, ALU.add, ALU.max))
                t.settle()
                t.did(eng.tensor_copy(tile_i[:, 2, :], tile_of[:]))
                t.settle()
                t.did(eng.tensor_scalar(tile_i[:, 1, :], tile_i[:, 2, :], J - 1, None, ALU.bitwise_and))
                t.did(eng.tensor_scalar(tile_i[:, 0, :], tile_i[:, 2, :], 2, 9, ALU.arith_shift_right, ALU.logical_shift_left))
                t.settle()
                t.did(eng.tensor_copy(tile_f[:], tile_i[:, 0:2, :]))
                t.settle()
                t.did(eng.scalar_tensor_tensor(slot_base[:], tile_f[:, 0, :], -float(J + ZERO_ROW), tile_f[:, 1, :],
                                               ALU.add, ALU.add))
                for n, (c, w) in enumerate(CHUNKS):
                    eng.wait_ge(s_rel, 2 * n + 1)
                    eng.tensor_copy(within_flat[:, c:c + w], pRel[:, n % 2, 0:w]).then_inc(s_rel_got, 1)
                    eng.wait_ge(s_rel, 2 * n + 2)
                    eng.tensor_copy(count_flat[:, c:c + w], pRel[:, 2 + n % 2, 0:w]).then_inc(s_rel_got, 1)
                eng.wait_ge(s_rel_got, 2 * len(CHUNKS))
                upto_flat = upto[:].rearrange("p r t -> p (r t)")
                t.did(eng.tensor_tensor_scan(upto_flat, ones[:, 0:1].to_broadcast([P, WIDTH]), count_flat, 0.0,
                                             ALU.mult, ALU.add))
                t.settle()
                ends, starts, size, pends, pstarts, shift = (rel[:, i, :] for i in range(6))
                t.did(eng.tensor_copy(ends, upto[:, :, E_TILES - 1]))
                t.did(eng.memset(starts[:, 0:1], 0.0))
                t.did(eng.memset(pstarts[:, 0:1], 0.0))
                t.settle()
                t.did(eng.tensor_copy(starts[:, 1:], ends[:, 0:N_REL - 1]))
                t.settle()
                t.did(eng.tensor_tensor(size, ends, starts, ALU.subtract))
                t.settle()
                t.did(eng.tensor_scalar(rel_i[:], size, float(P - 1), None, ALU.add))
                t.settle()
                t.did(eng.tensor_scalar(rel_i[:], rel_i[:], 7, 7, ALU.arith_shift_right, ALU.logical_shift_left))
                t.settle()
                t.did(eng.tensor_copy(size, rel_i[:]))
                t.settle()
                t.did(eng.tensor_tensor_scan(pends, ones[:, 0:N_REL], size, 0.0, ALU.mult, ALU.add))
                t.settle()
                t.did(eng.tensor_copy(pstarts[:, 1:], pends[:, 0:N_REL - 1]))
                t.settle()
                t.did(eng.tensor_tensor(shift, pstarts, starts, ALU.subtract))
                t.did(eng.tensor_tensor(upto[:], upto[:], count[:], ALU.subtract))
                t.settle()
                t.did(eng.tensor_tensor(within[:], within[:], upto[:], ALU.add))
                t.settle()
                t.did(eng.tensor_tensor(within[:], within[:], shift.unsqueeze(2).to_broadcast([P, N_REL, E_TILES]), ALU.add))
                t.settle()
                t.did(eng.tensor_tensor(within[:], within[:], hot[:], ALU.mult))
                t.settle()
                t.did(eng.tensor_reduce(hit[:], within[:].rearrange("p r t -> p t r"), AX.X, ALU.add))
                t.settle()
                t.did(eng.tensor_copy(rel_pos[:], hit[:]))
                t.did(eng.tensor_scalar(ramp_f[:], ramp_f[:], float(P), None, ALU.mult))
                t.settle()
                for h in range(2):
                    part = slice(h * R_TILES // 2, (h + 1) * R_TILES // 2)
                    shape = [P, R_TILES // 2, N_REL]
                    t.did(eng.tensor_tensor(cmp[:], pends.unsqueeze(1).to_broadcast(shape),
                                            ramp_f[:, part].unsqueeze(2).to_broadcast(shape), ALU.is_le))
                    t.settle()
                    t.did(eng.tensor_reduce(rel_of[:, part], cmp[:], AX.X, ALU.add))
                    t.settle()
                t.did(eng.tensor_scalar(rel_of[:], rel_of[:], float(N_REL - 1), float(IN), ALU.min, ALU.mult))
                t.did(eng.tensor_copy(rel_start[:], part_id[:]))
                t.settle()
                for h in range(2):
                    q = slice(h * IN, (h + 1) * IN)
                    t.did(eng.tensor_scalar(weight_row[q], rel_of[q].rearrange("p (m h) -> p m h", h=2)[:, :, h],
                                            rel_start[q, h:h + 1], None, ALU.add))
                t.settle()
                eng.sem_inc(s_slots, 1)
                eng.wait_ge(d_free, DRING + D_GROUPS + 1)
                t.did(eng.tensor_copy(gram[0:IN, 0:IN], pGram[0:IN, 0:IN]))
                t.did(eng.tensor_reduce(xsum[:], pSum[:, 0:J * IN].rearrange("p (q f) -> p f q", q=J), AX.X, ALU.add))
                t.settle()
                t.did(eng.tensor_tensor(xsum[0:IN], xsum[0:IN], ident[0:IN, 0:IN], ALU.mult))
                t.settle()
                t.did(eng.tensor_reduce(zsum[0:IN], xsum[0:IN], AX.X, ALU.add))
                t.settle()

        dst_rows = dst_flat[0:E_ROWS].rearrange("(g c) -> g c", c=GROUP)
        with ExitStack() as ctx:
            sb, psum, sem, ring = makers = tools(nc, ctx, "agg0")
            runs = GroupSums(makers, dst_rows, dst_col, prev_last, IN + 1)
            xs = sb("xs", [P, RING, J, IN + 1])
            Z = sb("Z", [P, RING, J, P + 1])
            wy = sb("wy", [P, HID + 1])
            recip = sb("recip", [P, J])
            st = sb("st", [P, 8])
            idx = sb("idx", [P, RING, J], I32)
            pZ = psum("pZ")
            pBN = psum("pBN")
            m_loaded, z_got, z_stored = (ring(n, RING) for n in ("m_loaded", "z_got", "z_stored"))
            s_ones, s_weighed, s_gram = sem("s_ones"), sem("s_weighed"), sem("s_gram")
            s_dve, s_pe, s_recip = sem("s_dve"), sem("s_pe"), sem("s_recip")
            s_var, s_std = sem("s_var"), sem("s_std")
            s_idx, s_idx_seen = sem("s_idx"), sem("s_idx_seen")
            block = ctx.enter_context(nc.Block())

            @block.sync
            def _(eng):
                def load(g, slot):
                    eng.dma_start(xs[:, slot, :, 0:IN], at(x_src, g).rearrange("p (j f) -> p j f", j=J))\
                        .then_inc(m_loaded[slot], 16)

                def group(g, slot, turn):
                    if not isinstance(g, int) or g + 2 < E_GROUPS:
                        eng.wait_ge(runs.selected, (J + 1) * g + J + 1)
                        runs.load(eng, g + 2, slot % 2)
                    eng.wait_ge(z_got[slot], 16 * J * turn + 16 * J)
                    eng.dma_start(at(x_dst, g).rearrange("p (j f) -> p j f", j=J), Z[:, slot, :, 0:IN])\
                        .then_inc(z_stored[slot], 16)
                    eng.wait_ge(runs.read, g + 2)
                    eng.dma_start(at(agg0_g, g).rearrange("p (j f) -> p j f", j=J), Z[:, slot, :, IN:P])\
                        .then_inc(z_stored[slot], 16)
                    if not isinstance(g, int) or 0 < g < E_GROUPS - 3:
                        eng.wait_ge(s_gram, g)
                        load(g + 3, (slot + 3) % RING)
                for h in range(RING):
                    if h < 2:
                        runs.load(eng, h, h)
                    load(h, h)
                for g in range(RING):
                    group(g, g, 0)
                loop_from(eng, RING, E_GROUPS - 3, RING, group)
                for g in range(E_GROUPS - 3, E_GROUPS):
                    group(g, g % RING, g // RING)
                for slot in range(RING):
                    eng.wait_ge(z_stored[slot], 32 * len(range(slot, E_GROUPS, RING)) + 16)

            @block.gpsimd
            def _(eng):
                def gather(h, slot, turn):
                    if not isinstance(h, int) or h >= RING:
                        eng.wait_ge(z_stored[slot], 32 * turn + 16)
                        eng.wait_ge(s_gram, h - RING + 1)
                    eng.tensor_copy(idx[:, slot, :], cols(dst_in, h * J, J)).then_inc(s_idx, 1)
                    eng.wait_ge(s_idx, h + 1)
                    eng.sem_inc(s_idx_seen, 1)
                    for j in range(J):
                        eng.indirect_dma_start(Z[:, slot, j, 0:IN], None, x,
                                               bass.IndirectOffsetOnAxis(ap=idx[:, slot, j:j + 1], axis=0))\
                            .then_inc(z_got[slot], 16)
                for h in range(RING):
                    gather(h, h, 0)
                loop_from(eng, RING, E_GROUPS, RING, gather)

            @block.tensor
            def _(eng):
                eng.wait_ge(s_ones, 3)
                eng.matmul(pZ[:, 0:P + 1], wy[:, 0:P], wy[:], start=True, stop=False)

                def gram_of(g, slot, turn, last=False):
                    eng.wait_ge(runs.read, g + 2)
                    eng.wait_ge(z_got[slot], 16 * J * turn + 16 * J)
                    for j in range(J):
                        rows = Z[:, slot, j, :]
                        ins = eng.matmul(pZ[:, 0:P + 1], rows[:, 0:P], rows, start=False, stop=last and j == J - 1)
                    ins.then_inc(s_gram, 1)

                def group(g, slot, turn):
                    eng.wait_ge(m_loaded[slot], 16 * turn + 16)
                    runs.add(eng, g, slot % 2, lambda i: xs[:, slot, i, :])
                    runs.carry(eng, g, slot % 2)
                    if not isinstance(g, int) or g > 0:
                        gram_of(g - 1, (slot + 3) % RING, turn if slot else turn - 1)
                for g in range(RING):
                    group(g, g, 0)
                loop_from(eng, RING, E_GROUPS, RING, group)
                gram_of(E_GROUPS - 1, (E_GROUPS - 1) % RING, (E_GROUPS - 1) // RING, True)
                t = Steps(eng, s_pe)
                eng.wait_ge(s_dve, 4)
                t.did(eng.matmul(pBN[:, 0:HID], gram[:], W0[:], start=True, stop=True))
                t.did(eng.matmul(pBN[:, HID:HID + 1], W0[:], zsum[:], start=True, stop=True))
                t.did(eng.matmul(pBN[:, HID + 1:HID + 2], W0_top[:], b2_pair[:], start=True, stop=True))
                eng.wait_ge(s_dve, 5)
                t.did(eng.matmul(pBN[:, HID + 2:HID + 3], wy[:, 0:HID], ones[:, 0:1], start=True, stop=True))

            @block.scalar
            def _(eng):
                eng.wait_ge(s_var, 1)
                eng.activation(st[:, 4:5], st[:, 2:3], ACT.Sqrt).then_inc(s_std, 1)

            @block.vector
            def _(eng):
                eng.memset(xs[:, :, :, IN:], 1.0).then_inc(s_ones, 1)
                eng.memset(Z[:, :, :, P:], 1.0).then_inc(s_ones, 1)
                eng.memset(wy[:], 0.0).then_inc(s_ones, 1)
                for slot in range(RING):
                    eng.sem_inc(z_stored[slot], 16)
                runs.start_vector(eng)

                def group(g, slot, turn):
                    two = slot % 2
                    if not isinstance(g, int) or g + 1 < E_GROUPS:
                        runs.select(eng, g + 1, 1 - two, turn * 2 + (slot + 1) // 2)
                    runs.keep(eng, g, two)
                    degree = runs.sums[:, two, 0:J * (IN + 1)].rearrange("p (j f) -> p j f", j=J)[:, :, IN]
                    eng.reciprocal(recip[:], degree).then_inc(s_recip, 1)
                    eng.wait_ge(s_recip, g + 1)
                    eng.tensor_tensor(cols(weight_col, g * J, J), cols(last_col, g * J, J), recip[:],
                                      ALU.mult).then_inc(s_weighed, 1)
                    eng.wait_ge(s_weighed, g + 1)
                    eng.wait_ge(z_stored[slot], 32 * turn + 16)
                    runs.means(eng, two, Z[:, slot, :, IN:P], weight_col, g)
                runs.select(eng, 0, 0, 0)
                loop(eng, E_GROUPS - 1, RING, group)
                group(E_GROUPS - 1, (E_GROUPS - 1) % RING, (E_GROUPS - 1) // RING)
                t = Steps(eng, s_dve)
                eng.wait_ge(s_gram, E_GROUPS)
                t.did(eng.tensor_copy(gram[0:IN, IN:P], pZ[0:IN, IN:P]))
                t.did(eng.tensor_copy(gram[IN:P, :], pZ[IN:P, 0:P]))
                t.did(eng.tensor_copy(zsum[IN:P], pZ[IN:P, P:P + 1]))
                t.settle()
                t.did(eng.memset(st[:], 0.0))
                eng.wait_ge(s_pe, 3)
                t.did(eng.tensor_tensor(wy[:, 0:HID], W0[:], pBN[:, 0:HID], ALU.mult))
                mean, ex2, var, tmp = (st[:, i:i + 1] for i in range(4))
                eng.wait_ge(s_pe, 4)
                t.settle()
                t.did(eng.tensor_scalar(mean, pBN[:, HID:HID + 1], 1.0 / N_NODES, None, ALU.mult))
                t.did(eng.tensor_scalar(ex2, pBN[:, HID + 2:HID + 3], 1.0 / N_NODES, None, ALU.mult))
                t.settle()
                t.did(eng.tensor_tensor(var, mean, mean, ALU.mult))
                t.settle()
                t.did(eng.tensor_tensor(var, ex2, var, ALU.subtract))
                t.settle()
                eng.tensor_scalar(var, var, 0.0, BN_EPS, ALU.max, ALU.add).then_inc(s_var, 1)
                eng.wait_ge(s_std, 1)
                t.did(eng.reciprocal(var, st[:, 4:5]))
                t.settle()
                t.did(eng.tensor_tensor(SC0, G0, var, ALU.mult))
                t.did(eng.tensor_tensor(tmp, mean, B0, ALU.add))
                t.settle()
                t.did(eng.tensor_tensor(tmp, B0, tmp, ALU.subtract))
                t.settle()
                t.did(eng.tensor_tensor(tmp, tmp, SC0, ALU.mult))
                t.settle()
                t.did(eng.tensor_tensor(SH0, BE0, tmp, ALU.add))
                t.settle()
                t.did(eng.tensor_tensor(tmp, SC0, pBN[:, HID + 1:HID + 2], ALU.mult))
                t.settle()
                t.did(eng.tensor_tensor(SH0D, SH0, tmp, ALU.subtract))
                t.settle()

        statD = keep("statD", [P, (D_GROUPS + 1) * 6])
        with ExitStack() as ctx:
            sb, psum, sem, ring = makers = tools(nc, ctx, "layer1")
            runs = RunSums(makers, dst_rows, dst_col, prev_last, HID)
            xd = sb("xd", [P, DRING, J * IN])
            xT = sb("xT", [P, 2, GROUP // 2])
            h0d = sb("h0d", [P, 2, GROUP])
            Z = sb("Z", [P, 2, J, P])
            idx = sb("idx", [P, 2, J], I32)
            tab = sb("tab", [P, 2, J, P], I32)
            tile_idx = sb("tile_idx", [P, 2, J], I32)
            match = sb("match", [P, 2, J, P])
            hit = sb("hit", [P, 2, 3, J])
            zT = sb("zT", [P, GROUP])
            h0e = sb("h0e", [P, 2, GROUP])
            msg = sb("msg", [P, 2, J, HID])
            agg_out = sb("agg_out", [P, 2, J * HID])
            pXT, pH0, pH1, pZT, pHE, pM = (psum(n) for n in ("pXT", "pH0", "pH1", "pZT", "pHE", "pM"))
            d_loaded = ring("d_loaded", DRING)
            d_transposed, d_xT, d_h0, d_relu, d_h1, d_stats = (
                sem(n) for n in ("d_transposed", "d_xT", "d_h0", "d_relu", "d_h1", "d_stats"))
            x_loaded, tab_got, gathered = ring("x_loaded"), ring("tab_got"), ring("gathered")
            s_tile_idx, s_matched, s_hit, s_place, s_base, s_slot, s_home = (
                sem(n) for n in ("s_tile_idx", "s_matched", "s_hit", "s_place", "s_base", "s_slot", "s_home"))
            h0_stored, agg_stored = ring("h0_stored"), ring("agg_stored")
            e_transposed, e_zT, e_h0, e_relu, e_msgT, e_msg = (
                sem(n) for n in ("e_transposed", "e_zT", "e_h0", "e_relu", "e_msgT", "e_msg"))
            s_begun = sem("s_begun")
            block = ctx.enter_context(nc.Block())
            LAST = E_GROUPS - 1
            assert E_GROUPS * J == D_GROUPS + 1

            def rows_of(d):
                return TAIL_P if isinstance(d, int) and d == D_GROUPS else P

            @block.sync
            def _(eng):
                def load_rows(h, slot):
                    eng.dma_start(Z[:, slot, :, 0:IN], at(x_src, h).rearrange("p (j f) -> p j f", j=J))\
                        .then_inc(x_loaded[slot], 16)

                def load_dense(d, slot):
                    if isinstance(d, int) and d > D_GROUPS:
                        return
                    p = rows_of(d)
                    eng.dma_start(xd[0:p, slot, :], at(x_dense, d) if p == P else x_tail).then_inc(d_loaded[slot], 16)

                def store_h0(h, slot):
                    eng.wait_ge(e_relu, h + 2)
                    eng.dma_start(at(h0_src, h), h0e[:, slot, :]).then_inc(h0_stored[slot], 16)

                def group(g, slot, turn):
                    for j in range(J):
                        if not isinstance(g, int) or g * J + j + DRING <= D_GROUPS:
                            eng.wait_ge(d_transposed, g * J + j + 1)
                            load_dense(g * J + j + DRING, (slot * J + j) % DRING)
                    if not isinstance(g, int) or g + 3 < E_GROUPS:
                        eng.wait_ge(e_transposed, g + 2)
                        load_rows(g + 3, (slot + 1) % 2)
                    eng.wait_ge(runs.scaled, J * g + J + 2)
                    eng.dma_start(at(agg1_g, g), agg_out[:, slot, :]).then_inc(agg_stored[slot], 16)
                    if not isinstance(g, int) or g + 2 < E_GROUPS:
                        runs.load(eng, g + 2, slot)
                    if not isinstance(g, int) or g + 1 < E_GROUPS:
                        store_h0(g + 1, (slot + 1) % 2)
                for h in range(2):
                    load_rows(h, h)
                    runs.load(eng, h, h)
                for d in range(DRING):
                    load_dense(d, d)
                eng.wait_ge(e_transposed, 1)
                load_rows(2, 0)
                store_h0(0, 0)
                loop(eng, E_GROUPS - 3, 2, group)
                for g in range(E_GROUPS - 3, E_GROUPS):
                    group(g, g % 2, g // 2)
                eng.wait_ge(s_slot, 2 * E_GROUPS)
                eng.dma_start(slot_home, slot_idx[:]).then_inc(s_home, 16)
                eng.wait_ge(s_home, 16)
                for slot in range(2):
                    eng.wait_ge(h0_stored[slot], 16 * len(range(slot, E_GROUPS, 2)) + 16)
                    eng.wait_ge(agg_stored[slot], 16 * len(range(slot, E_GROUPS, 2)) + 16)

            @block.gpsimd
            def _(eng):
                def gather_dst(h, slot):
                    if not isinstance(h, int) or h > 0:
                        eng.wait_ge(s_matched, h)
                    eng.tensor_copy(tile_idx[:, slot, :], cols(tile_of, h * J, J)).then_inc(s_tile_idx, 1)
                    eng.wait_ge(s_tile_idx, h + 1)
                    eng.sem_inc(s_begun, 1)
                    for j in range(J):
                        eng.indirect_dma_start(tab[:, slot, j, :], None, dst_table,
                                               bass.IndirectOffsetOnAxis(ap=tile_idx[:, slot, j:j + 1], axis=0))\
                            .then_inc(tab_got[slot], 16)

                def gather(h, slot, turn):
                    eng.wait_ge(s_slot, 2 * h + 2)
                    eng.sem_inc(s_begun, 1)
                    eng.wait_ge(x_loaded[slot], 16 * turn + 16)
                    eng.sem_inc(s_begun, 1)
                    for j in range(J):
                        eng.indirect_dma_start(Z[:, slot, j, IN:P], None, agg0,
                                               bass.IndirectOffsetOnAxis(ap=idx[:, slot, j:j + 1], axis=0))\
                            .then_inc(gathered[slot], 16)

                def both(h, slot, turn):
                    gather_dst(h + 1, (slot + 1) % 2)
                    gather(h, slot, turn)
                gather_dst(0, 0)
                loop(eng, E_GROUPS - 1, 2, both)
                gather(E_GROUPS - 1, (E_GROUPS - 1) % 2, (E_GROUPS - 1) // 2)

            @block.tensor
            def _(eng):
                def transpose_dense(d, slot, turn):
                    p = rows_of(d)
                    eng.wait_ge(d_loaded[slot], 16 * turn + 16)
                    eng.wait_ge(d_xT, d + 1)
                    for h in range(2):
                        ins = eng.transpose(pXT[:, h * p:(h + 1) * p], xd[0:p, slot, h * P:(h + 1) * P], ident[0:p, 0:p])
                    ins.then_inc(d_transposed, 1)

                def first_dense(d, slot):
                    w = 2 * rows_of(d)
                    eng.wait_ge(d_xT, d + 2)
                    eng.wait_ge(d_relu, d + 1)
                    eng.matmul(pH0[:, 0:w], W0_top[:], xT[:, slot % 2, 0:w], start=True, stop=True)
                    eng.matmul(pH0[:, w:2 * w], W0_bot[:], xT[:, slot % 2, 0:w], start=True, stop=True).then_inc(d_h0, 1)

                def second_dense(d, slot):
                    w = 4 * rows_of(d)
                    eng.wait_ge(d_relu, d + 2)
                    eng.wait_ge(d_stats, d + 1)
                    eng.matmul(pH1[:, 0:w], Wr1T[:], h0d[:, slot % 2, 0:w], start=True, stop=True).then_inc(d_h1, 1)

                def transpose_rows(g, slot, turn):
                    eng.wait_ge(x_loaded[slot], 16 * turn + 16)
                    eng.wait_ge(gathered[slot], 16 * J * turn + 16 * J)
                    eng.wait_ge(e_zT, g + 1)
                    for j in range(J):
                        ins = eng.transpose(pZT[:, j * P:(j + 1) * P], Z[:, slot, j, :], ident[:])
                    ins.then_inc(e_transposed, 1)

                def first_rows(g):
                    eng.wait_ge(e_zT, g + 2)
                    eng.wait_ge(e_relu, g + 1)
                    eng.matmul(pHE[:], W0[:], zT[:], start=True, stop=True).then_inc(e_h0, 1)

                def message(g, slot):
                    eng.wait_ge(e_relu, g + 2)
                    eng.wait_ge(e_msg, g + 1)
                    for j in range(J):
                        ins = eng.transpose(pM[:, j * P:(j + 1) * P], h0e[:, slot, j * P:(j + 1) * P], ident[:])
                    ins.then_inc(e_msgT, 1)

                def group(g, slot, turn):
                    more = not isinstance(g, int) or g + 1 < E_GROUPS
                    s1, t1 = later(slot, turn, 1, 2)
                    eng.wait_ge(e_msg, g + 2)
                    for j in range(J):
                        runs.add(eng, g, slot, j, msg[:, slot, j, :])
                        d = g * J + j
                        if not isinstance(d, int) or d + 2 <= D_GROUPS:
                            transpose_dense(d + 2, *later(slot * J + j, turn, 2, DRING))
                        if not isinstance(d, int) or d + 1 <= D_GROUPS:
                            first_dense(d + 1, slot * J + j + 1)
                        second_dense(d, slot * J + j)
                        if more and j == 0:
                            transpose_rows(g + 1, s1, t1)
                        if more and j == 1:
                            first_rows(g + 1)
                        if more and j == 3:
                            message(g + 1, s1)
                transpose_rows(0, 0, 0)
                transpose_dense(0, 0, 0)
                first_rows(0)
                transpose_dense(1, 1, 0)
                first_dense(0, 0)
                message(0, 0)
                loop(eng, E_GROUPS - 1, 2, group)
                group(LAST, LAST % 2, LAST // 2)

            @block.scalar
            def _(eng):
                eng.sem_inc(runs.scaled, 2)
                eng.sem_inc(e_zT, 1)
                eng.sem_inc(e_relu, 1)
                eng.sem_inc(d_relu, 1)
                for slot in range(2):
                    eng.sem_inc(agg_stored[slot], 16)
                    eng.sem_inc(h0_stored[slot], 16)

                def relu_dense(d, slot):
                    w = 4 * rows_of(d)
                    eng.wait_ge(d_h0, d + 1)
                    eng.activation(h0d[:, slot % 2, 0:w], pH0[:, 0:w], ACT.Relu, bias=SH0D, scale=SC0).then_inc(d_relu, 1)

                def copy_rows(g):
                    eng.wait_ge(e_transposed, g + 1)
                    eng.activation(zT[:], pZT[:], ACT.Copy).then_inc(e_zT, 1)

                def relu_rows(g, slot, turn):
                    eng.wait_ge(e_h0, g + 1)
                    eng.wait_ge(h0_stored[slot], 16 * turn + 16)
                    eng.activation(h0e[:, slot, :], pHE[:], ACT.Relu, bias=SH0, scale=SC0).then_inc(e_relu, 1)

                def group(g, slot, turn):
                    more = not isinstance(g, int) or g + 1 < E_GROUPS
                    eng.wait_ge(agg_stored[slot], 16 * turn + 16)
                    for j in range(J):
                        runs.scale(eng, g, j, agg_out[:, slot, j * HID:(j + 1) * HID], weight_col)
                        d = g * J + j
                        if not isinstance(d, int) or d + 1 <= D_GROUPS:
                            relu_dense(d + 1, slot * J + j + 1)
                        if more and j == 0:
                            copy_rows(g + 1)
                        if more and j == 1:
                            relu_rows(g + 1, *later(slot, turn, 1, 2))
                copy_rows(0)
                relu_rows(0, 0, 0)
                relu_dense(0, 0)
                loop(eng, E_GROUPS - 1, 2, group)
                group(LAST, LAST % 2, LAST // 2)

            @block.vector
            def _(eng):
                eng.sem_inc(e_msg, 1)
                eng.sem_inc(s_matched, 1)
                eng.sem_inc(d_xT, 1)
                eng.sem_inc(d_stats, 1)
                runs.start_vector(eng)

                def copy_dense(d, slot):
                    w = 2 * rows_of(d)
                    eng.wait_ge(d_transposed, d + 1)
                    eng.tensor_scalar(xT[:, slot % 2, 0:w], pXT[:, 0:w], b2_pair[:], None, ALU.add).then_inc(d_xT, 1)

                def stats_dense(d):
                    w = 4 * rows_of(d)
                    eng.wait_ge(d_h1, d + 1)
                    eng.bn_stats(cols(statD, d * 6, 6), pH1[:, 0:w]).then_inc(d_stats, 1)

                def copy_message(g, slot):
                    eng.wait_ge(e_msgT, g + 1)
                    eng.tensor_copy(msg[:, slot], pM[:].rearrange("p (j f) -> p j f", j=J)).then_inc(e_msg, 1)

                def match_rows(h, slot, turn):
                    eng.wait_ge(tab_got[slot], 16 * J * turn + 16 * J)
                    for j in range(J):
                        ins = eng.scalar_tensor_tensor(match[:, slot, j, :], tab[:, slot, j, :],
                                                       cols(src_col, h * J + j, 1), number[:], ALU.is_equal, ALU.mult)
                    ins.then_inc(s_matched, 1)

                def place_of(h, slot):
                    eng.wait_ge(s_matched, h + 2)
                    eng.tensor_reduce(hit[:, slot, 0, :], match[:, slot, :, :], AX.X, ALU.max).then_inc(s_hit, 1)

                def row_of(h, slot):
                    place, row, found = (hit[:, slot, i, :] for i in range(3))
                    eng.wait_ge(s_hit, h + 1)
                    eng.scalar_tensor_tensor(row, place, float(J), cols(slot_base, h * J, J), ALU.mult, ALU.add)\
                        .then_inc(s_place, 1)
                    eng.wait_ge(s_place, h + 1)
                    eng.scalar_tensor_tensor(found, place, 0.0, row, ALU.is_gt, ALU.mult).then_inc(s_base, 1)

                def give_row(h, slot, turn):
                    found = hit[:, slot, 2, :]
                    eng.wait_ge(s_base, h + 1)
                    if not isinstance(h, int) or h > 1:
                        eng.wait_ge(gathered[slot], 16 * J * turn)
                    for to in (idx[:, slot, :], cols(slot_idx, h * J, J)):
                        eng.tensor_scalar(to, found, float(ZERO_ROW), None, ALU.add).then_inc(s_slot, 1)

                def group(g, slot, turn):
                    more = not isinstance(g, int) or g + 1 < E_GROUPS
                    for j in range(J):
                        runs.keep(eng, g, j)
                        d = g * J + j
                        if not isinstance(d, int) or d + 2 <= D_GROUPS:
                            copy_dense(d + 2, slot * J + j + 2)
                        stats_dense(d)
                        if more and j == 0:
                            runs.select(eng, g + 1, *later(slot, turn, 1, 2))
                        if not isinstance(g, int) or g + 3 < E_GROUPS:
                            s3, t3 = later(slot, turn, 3, 2)
                            (lambda: match_rows(g + 3, s3, t3), lambda: place_of(g + 3, s3),
                             lambda: row_of(g + 3, s3), lambda: give_row(g + 3, s3, t3))[j]()
                        if more and j == 3:
                            copy_message(g + 1, (slot + 1) % 2)
                for h in range(3):
                    match_rows(h, h % 2, h // 2)
                    place_of(h, h % 2)
                    row_of(h, h % 2)
                    give_row(h, h % 2, h // 2)
                runs.select(eng, 0, 0, 0)
                copy_dense(0, 0)
                copy_dense(1, 1)
                copy_message(0, 0)
                loop(eng, E_GROUPS - 3, 2, group)
                for g in range(E_GROUPS - 3, E_GROUPS):
                    group(g, g % 2, g // 2)

        with ExitStack() as ctx:
            sb, psum, sem, ring = makers = tools(nc, ctx, "bn1")
            Z = sb("Z", [P, 2, J, P])
            A = sb("A", [P, 2, J, HID])
            zT = sb("zT", [P, GROUP])
            aT = sb("aT", [P, 2, GROUP])
            h0 = sb("h0", [P, 2, GROUP])
            h0v = sb("h0v", [P, 2, GROUP])
            h1 = sb("h1", [P, 2, GROUP])
            statT = sb("statT", [P, E_GROUPS * 6])
            statV = sb("statV", [P, E_GROUPS * 6])
            st = sb("st", [P, 16])
            pZ, pA, pH0, pV0, pH1, pV1 = (psum(n) for n in ("pZ", "pA", "pH0", "pV0", "pH1", "pV1"))
            loaded, h0_stored, h1_stored = ring("loaded"), ring("h0_stored"), ring("h1_stored")
            s_Z, s_A, s_H0, s_V0, s_H1, s_V1 = (sem(f"s_{n}") for n in ("Z", "A", "H0", "V0", "H1", "V1"))
            c_z, c_a, c_h0, c_v0 = (sem(f"c_{n}") for n in ("z", "a", "h0", "v0"))
            c_h1, c_v1, s_copy = sem("c_h1"), sem("c_v1"), sem("s_copy")
            s_dve, s_var, s_std = sem("s_dve"), sem("s_var"), sem("s_std")
            block = ctx.enter_context(nc.Block())
            LAST = E_GROUPS - 1

            @block.sync
            def _(eng):
                def load(h, slot):
                    for to, of in ((Z[:, slot, :, 0:IN], x_dst), (Z[:, slot, :, IN:P], agg0_g), (A[:, slot], agg1_g)):
                        eng.dma_start(to, at(of, h).rearrange("p (j f) -> p j f", j=J)).then_inc(loaded[slot], 16)

                def store_h0(h, slot):
                    eng.wait_ge(c_h0, h + 2)
                    eng.dma_start(at(h0_dst, h), h0[:, slot, :]).then_inc(h0_stored[slot], 16)

                def group(g, slot, turn):
                    if not isinstance(g, int) or g + 1 < E_GROUPS:
                        store_h0(g + 1, (slot + 1) % 2)
                    if not isinstance(g, int) or g + 3 < E_GROUPS:
                        eng.wait_ge(s_A, g + 2)
                        load(g + 3, (slot + 1) % 2)
                    eng.wait_ge(s_copy, g + 1)
                    eng.dma_start(at(h1_dst, g), h1[:, slot, :]).then_inc(h1_stored[slot], 16)
                load(0, 0)
                load(1, 1)
                eng.wait_ge(s_A, 1)
                load(2, 0)
                store_h0(0, 0)
                loop(eng, E_GROUPS - 3, 2, group)
                for g in range(E_GROUPS - 3, E_GROUPS):
                    group(g, g % 2, g // 2)
                for slot in range(2):
                    eng.wait_ge(h0_stored[slot], 16 * len(range(slot, E_GROUPS, 2)) + 16)
                    eng.wait_ge(h1_stored[slot], 16 * len(range(slot, E_GROUPS, 2)) + 16)

            @block.tensor
            def _(eng):
                def turn_rows(g, slot, turn):
                    eng.wait_ge(loaded[slot], 48 * turn + 48)
                    eng.wait_ge(c_z, g + 1)
                    for j in range(J):
                        ins = eng.transpose(pZ[:, j * P:(j + 1) * P], Z[:, slot, j, :], ident[:])
                    ins.then_inc(s_Z, 1)
                    eng.wait_ge(c_a, g + 1)
                    for j in range(J):
                        ins = eng.transpose(pA[:, j * P:(j + 1) * P], A[:, slot, j, :], ident[:])
                    ins.then_inc(s_A, 1)

                def first(g):
                    eng.wait_ge(c_z, g + 2)
                    eng.wait_ge(c_h0, g + 1)
                    eng.matmul(pH0[:], W0[:], zT[:], start=True, stop=True).then_inc(s_H0, 1)
                    eng.wait_ge(c_v0, g + 1)
                    eng.matmul(pV0[:], W0_top[:], zT[:], start=True, stop=True).then_inc(s_V0, 1)

                def second(g, slot):
                    eng.wait_ge(c_h0, g + 2)
                    eng.wait_ge(c_a, g + 2)
                    eng.wait_ge(c_h1, g + 1)
                    eng.matmul(pH1[:], Wr1T[:], h0[:, slot, :], start=True, stop=False)
                    eng.matmul(pH1[:], Wl1T[:], aT[:, slot, :], start=False, stop=True).then_inc(s_H1, 1)
                    eng.wait_ge(c_v0, g + 2)
                    eng.wait_ge(c_v1, g + 1)
                    eng.matmul(pV1[:], Wr1T[:], h0v[:, slot, :], start=True, stop=True).then_inc(s_V1, 1)

                def group(g, slot, turn):
                    if not isinstance(g, int) or g + 1 < E_GROUPS:
                        turn_rows(g + 1, *later(slot, turn, 1, 2))
                        first(g + 1)
                    second(g, slot)
                turn_rows(0, 0, 0)
                first(0)
                loop(eng, LAST, 2, group)
                group(LAST, LAST % 2, LAST // 2)

            @block.scalar
            def _(eng):
                for s in (c_z, c_a, c_h0, c_v0):
                    eng.sem_inc(s, 1)
                for slot in range(2):
                    eng.sem_inc(h0_stored[slot], 16)

                def group(g, slot, turn):
                    eng.wait_ge(s_Z, g + 1)
                    eng.activation(zT[:], pZ[:], ACT.Copy).then_inc(c_z, 1)
                    eng.wait_ge(s_A, g + 1)
                    eng.activation(aT[:, slot, :], pA[:], ACT.Copy).then_inc(c_a, 1)
                    eng.wait_ge(s_H0, g + 1)
                    eng.wait_ge(h0_stored[slot], 16 * turn + 16)
                    eng.activation(h0[:, slot, :], pH0[:], ACT.Relu, bias=SH0, scale=SC0).then_inc(c_h0, 1)
                    eng.wait_ge(s_V0, g + 1)
                    eng.activation(h0v[:, slot, :], pV0[:], ACT.Relu, bias=SH0, scale=SC0).then_inc(c_v0, 1)
                loop(eng, E_GROUPS, 2, group)
                eng.wait_ge(s_var, 1)
                eng.activation(st[:, 11:12], st[:, 10:11], ACT.Sqrt).then_inc(s_std, 1)

            @block.vector
            def _(eng):
                for s in (c_h1, c_v1):
                    eng.sem_inc(s, 1)
                for slot in range(2):
                    eng.sem_inc(h1_stored[slot], 16)

                def group(g, slot, turn):
                    eng.wait_ge(s_H1, g + 1)
                    eng.wait_ge(h1_stored[slot], 16 * turn + 16)
                    eng.tensor_copy(h1[:, slot, :], pH1[:]).then_inc(s_copy, 1)
                    eng.bn_stats(cols(statT, g * 6, 6), pH1[:]).then_inc(c_h1, 1)
                    eng.wait_ge(s_V1, g + 1)
                    eng.bn_stats(cols(statV, g * 6, 6), pV1[:]).then_inc(c_v1, 1)
                loop(eng, E_GROUPS, 2, group)
                t = Steps(eng, s_dve)
                eng.wait_ge(c_h1, E_GROUPS + 1)
                eng.wait_ge(c_v1, E_GROUPS + 1)
                mD, vD, mT, vT, mV, vV, a, b, c, delta, var, std = (st[:, i:i + 1] for i in range(12))
                t.did(eng.bn_aggr(st[:, 0:2], statD[:]))
                t.did(eng.bn_aggr(st[:, 2:4], statT[:]))
                t.did(eng.bn_aggr(st[:, 4:6], statV[:]))
                t.settle()
                SHARE = E_ROWS / N_NODES
                t.did(eng.tensor_tensor(a, mT, mD, ALU.subtract))
                t.did(eng.tensor_tensor(b, mV, mD, ALU.subtract))
                t.did(eng.tensor_tensor(delta, mT, mV, ALU.subtract))
                t.did(eng.tensor_tensor(c, vT, vV, ALU.subtract))
                t.settle()
                t.did(eng.tensor_scalar(delta, delta, SHARE, None, ALU.mult))
                t.did(eng.tensor_tensor(a, a, a, ALU.mult))
                t.did(eng.tensor_tensor(b, b, b, ALU.mult))
                t.settle()
                t.did(eng.tensor_tensor(c, c, a, ALU.add))
                t.settle()
                t.did(eng.tensor_tensor(c, c, b, ALU.subtract))
                t.did(eng.tensor_tensor(a, delta, delta, ALU.mult))
                t.settle()
                t.did(eng.scalar_tensor_tensor(var, c, SHARE, vD, ALU.mult, ALU.add))
                t.settle()
                t.did(eng.tensor_tensor(var, var, a, ALU.subtract))
                t.did(eng.tensor_tensor(mD, mD, delta, ALU.add))
                t.settle()
                eng.tensor_scalar(var, var, 0.0, BN_EPS, ALU.max, ALU.add).then_inc(s_var, 1)
                eng.wait_ge(s_std, 1)
                t.did(eng.reciprocal(var, std))
                t.did(eng.tensor_tensor(a, mD, B1, ALU.add))
                t.settle()
                t.did(eng.tensor_tensor(SC1, G1, var, ALU.mult))
                t.did(eng.tensor_tensor(b, B1, a, ALU.subtract))
                t.settle()
                t.did(eng.tensor_tensor(b, b, SC1, ALU.mult))
                t.settle()
                t.did(eng.tensor_tensor(SH1, BE1, b, ALU.add))
                t.settle()

        with ExitStack() as ctx:
            sb, psum, sem, ring = makers = tools(nc, ctx, "layer2")
            runs = GroupSums(makers, dst_rows, dst_col, prev_last, OUT)
            idx = sb("idx", [P, 2, J], I32)
            A = sb("A", [P, 2, J, HID])
            aT = sb("aT", [P, GROUP])
            h0 = sb("h0", [P, 2, GROUP])
            h2 = sb("h2", [P, 2, GROUP])
            xe = sb("xe", [P, 2, J * IN])
            h0t = sb("h0t", [P, 2, GROUP])
            h1t = sb("h1t", [P, 2, GROUP])
            h2t = sb("h2t", [P, 2, GROUP])
            xt = sb("xt", [P, 2, J * IN])
            msg = sb("msg", [P, 2, J, OUT])
            ue = sb("ue", [P, 2, J, OUT])
            ut = sb("ut", [P, 2, J, OUT])
            agg_out = sb("agg_out", [P, 2, J * OUT])
            pA, pH1, pO, pOT = (psum(n) for n in ("pA", "pH1", "pO", "pOT"))
            i_loaded, gathered = ring("i_loaded"), ring("gathered")
            e_loaded, t_loaded = ring("e_loaded"), ring("t_loaded")
            e_stored, t_stored, agg_stored = ring("e_stored"), ring("t_stored"), ring("agg_stored")
            s_A, s_H1, s_O, s_OT = (sem(f"s_{n}") for n in ("A", "H1", "O", "OT"))
            c_A, c_relu, c_h2, c_O = (sem(f"c_{n}") for n in ("A", "relu", "h2", "O"))
            c_relut, c_h2t, c_OT = (sem(f"c_{n}") for n in ("relut", "h2t", "OT"))
            s_ux, s_uxt, s_u, s_ut, s_begun = (sem(n) for n in ("s_ux", "s_uxt", "s_u", "s_ut", "s_begun"))
            block = ctx.enter_context(nc.Block())
            LAST = E_GROUPS - 1

            @block.sync
            def _(eng):
                def load_e(h, slot):
                    eng.dma_start(h0[:, slot, :], at(h0_src, h)).then_inc(e_loaded[slot], 16)
                    eng.dma_start(xe[:, slot, :], at(x_src, h)).then_inc(e_loaded[slot], 16)

                def load_idx(h, slot):
                    eng.dma_start(idx[:, slot, :], cols(slot_home, h * J, J)).then_inc(i_loaded[slot], 16)

                def load_t(h, slot):
                    eng.dma_start(h0t[:, slot, :], at(h0_dst, h)).then_inc(t_loaded[slot], 16)
                    eng.dma_start(h1t[:, slot, :], at(h1_dst, h)).then_inc(t_loaded[slot], 16)
                    eng.dma_start(xt[:, slot, :], at(x_dst, h)).then_inc(t_loaded[slot], 16)

                def store_u(h, slot):
                    eng.wait_ge(s_u, h + 1)
                    eng.dma_start(at(u_src, h), ue[:, slot].rearrange("p j f -> p (j f)")).then_inc(e_stored[slot], 16)
                    eng.wait_ge(s_ut, h + 1)
                    eng.dma_start(at(u_dst, h), ut[:, slot].rearrange("p j f -> p (j f)")).then_inc(t_stored[slot], 16)

                def group(g, slot, turn):
                    if not isinstance(g, int) or g + 3 < E_GROUPS:
                        eng.wait_ge(s_A, g + 2)
                        load_idx(g + 3, (slot + 1) % 2)
                    if not isinstance(g, int) or g + 2 < E_GROUPS:
                        eng.wait_ge(runs.selected, (J + 1) * g + J + 1)
                        runs.load(eng, g + 2, slot)
                    eng.wait_ge(runs.read, g + 2)
                    eng.dma_start(at(agg2_g, g), agg_out[:, slot, :]).then_inc(agg_stored[slot], 16)
                    if not isinstance(g, int) or g + 1 < E_GROUPS:
                        store_u(g + 1, (slot + 1) % 2)
                    if not isinstance(g, int) or g + 3 < E_GROUPS:
                        load_e(g + 3, (slot + 1) % 2)
                        load_t(g + 3, (slot + 1) % 2)
                for h in range(2):
                    load_idx(h, h)
                    load_e(h, h)
                    load_t(h, h)
                    runs.load(eng, h, h)
                eng.wait_ge(s_A, 1)
                load_idx(2, 0)
                store_u(0, 0)
                load_e(2, 0)
                load_t(2, 0)
                loop(eng, E_GROUPS - 3, 2, group)
                for g in range(E_GROUPS - 3, E_GROUPS):
                    group(g, g % 2, g // 2)
                for slot in range(2):
                    n = 16 * len(range(slot, E_GROUPS, 2)) + 16
                    eng.wait_ge(e_stored[slot], n)
                    eng.wait_ge(t_stored[slot], n)
                    eng.wait_ge(agg_stored[slot], n)

            @block.gpsimd
            def _(eng):
                def gather(h, slot, turn):
                    eng.wait_ge(i_loaded[slot], 16 * turn + 16)
                    eng.sem_inc(s_begun, 1)
                    for j in range(J):
                        eng.indirect_dma_start(A[:, slot, j, :], None, agg1,
                                               bass.IndirectOffsetOnAxis(ap=idx[:, slot, j:j + 1], axis=0))\
                            .then_inc(gathered[slot], 16)
                loop(eng, E_GROUPS, 2, gather)

            @block.tensor
            def _(eng):
                def turn_rows(g, slot, turn):
                    eng.wait_ge(gathered[slot], 16 * J * turn + 16 * J)
                    eng.wait_ge(c_A, g + 1)
                    for j in range(J):
                        ins = eng.transpose(pA[:, j * P:(j + 1) * P], A[:, slot, j, :], ident[:])
                    ins.then_inc(s_A, 1)

                def second(g, slot, turn):
                    eng.wait_ge(e_loaded[slot], 32 * turn + 32)
                    eng.wait_ge(c_A, g + 2)
                    eng.wait_ge(c_relu, g + 1)
                    eng.matmul(pH1[:], Wr1T[:], h0[:, slot, :], start=True, stop=False)
                    eng.matmul(pH1[:], Wl1T[:], aT[:], start=False, stop=True).then_inc(s_H1, 1)

                def third_t(g, slot):
                    eng.wait_ge(c_h2t, g + 1)
                    eng.wait_ge(c_OT, g + 1)
                    for j in range(J):
                        ins = eng.matmul(pOT[:, j * OUT:(j + 1) * OUT], h2t[:, slot, j * P:(j + 1) * P],
                                         W2_msg[:, OUT:], start=True, stop=True)
                    ins.then_inc(s_OT, 1)

                def third(g, slot):
                    eng.wait_ge(c_h2, g + 1)
                    eng.wait_ge(c_O, g + 1)
                    eng.wait_ge(s_ux, g + 1)
                    for j in range(J):
                        ins = eng.matmul(pO[:, j * P:(j + 1) * P], h2[:, slot, j * P:(j + 1) * P],
                                         W2_msg[:], start=True, stop=True)
                    ins.then_inc(s_O, 1)

                def group(g, slot, turn):
                    more = not isinstance(g, int) or g + 1 < E_GROUPS
                    s1, t1 = later(slot, turn, 1, 2)
                    eng.wait_ge(c_O, g + 2)
                    if more:
                        turn_rows(g + 1, s1, t1)
                    runs.add(eng, g, slot, lambda i: msg[:, slot, i, :])
                    if more:
                        second(g + 1, s1, t1)
                    runs.carry(eng, g, slot)
                    if more:
                        third_t(g + 1, s1)
                        third(g + 1, s1)
                turn_rows(0, 0, 0)
                second(0, 0, 0)
                third_t(0, 0)
                third(0, 0)
                loop(eng, LAST, 2, group)
                group(LAST, LAST % 2, LAST // 2)

            @block.scalar
            def _(eng):
                eng.sem_inc(c_A, 1)
                eng.sem_inc(c_relu, 1)

                def relu_t(g, slot, turn):
                    eng.wait_ge(t_loaded[slot], 48 * turn + 48)
                    eng.activation(h2t[:, slot, :], h1t[:, slot, :], ACT.Relu, bias=SH1, scale=SC1).then_inc(c_relut, 1)

                def copy(g):
                    eng.wait_ge(s_A, g + 1)
                    eng.activation(aT[:], pA[:], ACT.Copy).then_inc(c_A, 1)

                def relu(g, slot):
                    eng.wait_ge(s_H1, g + 1)
                    eng.activation(h2[:, slot, :], pH1[:], ACT.Relu, bias=SH1, scale=SC1).then_inc(c_relu, 1)

                def group(g, slot, turn):
                    copy(g)
                    relu_t(g, slot, turn)
                    relu(g, slot)
                loop(eng, E_GROUPS, 2, group)

            @block.vector
            def _(eng):
                eng.sem_inc(c_O, 1)
                eng.sem_inc(c_OT, 1)
                eng.sem_inc(s_ux, 1)
                for slot in range(2):
                    eng.sem_inc(agg_stored[slot], 16)
                    eng.sem_inc(e_stored[slot], 16)
                    eng.sem_inc(t_stored[slot], 16)
                runs.start_vector(eng)
                b2_all = b2_row[:].unsqueeze(1).to_broadcast([P, J, OUT])

                def residual_t(g, slot):
                    eng.wait_ge(c_relut, g + 1)
                    eng.tensor_tensor(h2t[:, slot, :], h2t[:, slot, :], h0t[:, slot, :], ALU.add).then_inc(c_h2t, 1)

                def residual(g, slot):
                    eng.wait_ge(c_relu, g + 2)
                    eng.tensor_tensor(h2[:, slot, :], h2[:, slot, :], h0[:, slot, :], ALU.add).then_inc(c_h2, 1)

                def sum_t(g, slot, turn):
                    eng.wait_ge(s_OT, g + 1)
                    eng.wait_ge(t_stored[slot], 16 * turn + 16)
                    eng.tensor_tensor(ut[:, slot], pOT[:, 0:J * OUT].rearrange("p (j f) -> p j f", j=J),
                                      xt[:, slot, :].rearrange("p (j f) -> p j f", j=J), ALU.add).then_inc(c_OT, 1)
                    eng.wait_ge(c_OT, g + 2)
                    eng.tensor_tensor(ut[:, slot], ut[:, slot], b2_all, ALU.add).then_inc(s_ut, 1)

                def sum_e(g, slot, turn):
                    eng.wait_ge(s_O, g + 1)
                    eng.wait_ge(e_stored[slot], 16 * turn + 16)
                    both = pO[:].rearrange("p (j f) -> p j f", j=J)
                    eng.tensor_copy(msg[:, slot], both[:, :, 0:OUT]).then_inc(c_O, 1)
                    eng.tensor_tensor(ue[:, slot], both[:, :, OUT:], xe[:, slot, :].rearrange("p (j f) -> p j f", j=J),
                                      ALU.add).then_inc(s_ux, 1)
                    eng.wait_ge(s_ux, g + 2)
                    eng.tensor_tensor(ue[:, slot], ue[:, slot], b2_all, ALU.add).then_inc(s_u, 1)

                def group(g, slot, turn):
                    more = not isinstance(g, int) or g + 1 < E_GROUPS
                    s1, t1 = later(slot, turn, 1, 2)
                    if more:
                        residual_t(g + 1, s1)
                        runs.select(eng, g + 1, s1, t1)
                        residual(g + 1, s1)
                    runs.keep(eng, g, slot)
                    eng.wait_ge(agg_stored[slot], 16 * turn + 16)
                    runs.means(eng, slot, agg_out[:, slot, :].rearrange("p (j f) -> p j f", j=J), weight_col, g)
                    if more:
                        sum_t(g + 1, s1, t1)
                        sum_e(g + 1, s1, t1)
                runs.select(eng, 0, 0, 0)
                residual_t(0, 0)
                residual(0, 0)
                sum_t(0, 0, 0)
                sum_e(0, 0, 0)
                loop(eng, LAST, 2, group)
                group(LAST, LAST % 2, LAST // 2)

        out_dense = out[0:D_GROUPS * GROUP].rearrange("(g p q) f -> g p (q f)", p=P, q=J)
        out_tail = out[D_GROUPS * GROUP:N_NODES].rearrange("(p q) f -> p (q f)", q=J)
        with ExitStack() as ctx:
            sb, psum, sem, ring = makers = tools(nc, ctx, "dense")
            xd = sb("xd", [P, DRING, J * IN])
            xT = sb("xT", [P, 4, GROUP // 2])
            h0 = sb("h0", [P, 4, GROUP])
            h2 = sb("h2", [P, 2, GROUP])
            sq1 = sb("sq1", [P, 2, J, OUT])
            sq2 = sb("sq2", [P, 2, J, OUT])
            y = sb("y", [P, 4, J, OUT])
            o = sb("o", [P, 4, J, OUT])
            small = sb("small", [P, 8, 2, J])
            mean1, var1, std1, r1, mean2, var2, std2, r2 = (small[:, i] for i in range(8))
            pXT, pH0, pH1, pU = psum("pXT"), psum("pH0"), psum("pH1"), psum("pU", 2)
            d_loaded, d_stored = ring("d_loaded", DRING), ring("d_stored", 4)
            d_T, d_X, d_H0, d_R0, d_H1, d_R1, d_h2, d_U = (
                sem(f"d_{n}") for n in ("T", "X", "H0", "R0", "H1", "R1", "h2", "U"))
            d_q1, d_m1, d_v1, d_s1, d_r1, d_y, d_yb = (
                sem(f"d_{n}") for n in ("q1", "m1", "v1", "s1", "r1", "y", "yb"))
            d_q2, d_m2, d_v2, d_s2, d_r2, d_out = (sem(f"d_{n}") for n in ("q2", "m2", "v2", "s2", "r2", "out"))
            idx = sb("idx", [P, 2, 2, J], I32)
            ue = sb("ue", [P, 2, J, OUT])
            A = sb("A", [P, 2, J, OUT])
            x1 = sb("x1", [P, 2, J, OUT])
            stats = sb("stats", [P, 2, J, 6])
            mv = sb("mv", [P, 2, J, 2])
            rstd = sb("rstd", [P, 2, 2, J])
            e_idx, e_loaded, gathered, scattered = ring("e_idx"), ring("e_loaded"), ring("gathered"), ring("scattered")
            e_sum, e_st, e_mv, e_var, e_std, e_r, e_x1, e_begun, s_begun = (
                sem(n) for n in ("e_sum", "e_st", "e_mv", "e_var", "e_std", "e_r", "e_x1", "e_begun", "s_begun"))
            block = ctx.enter_context(nc.Block())
            N_TILES = D_GROUPS + 1

            def exists(d):
                return not isinstance(d, int) or 0 <= d < N_TILES

            @block.sync
            def _(eng):
                def load_e(h, slot):
                    eng.dma_start(idx[:, slot, 0, :], cols(slot_home, h * J, J)).then_inc(e_idx[slot], 16)
                    eng.dma_start(idx[:, slot, 1, :], cols(rel_home, h * J, J)).then_inc(e_idx[slot], 16)
                    eng.dma_start(ue[:, slot].rearrange("p j f -> p (j f)"), at(u_src, h)).then_inc(e_loaded[slot], 16)

                def load_d(d, slot):
                    p = rows_of(d)
                    eng.dma_start(xd[0:p, slot, :], at(x_dense, d) if p == P else x_tail).then_inc(d_loaded[slot], 16)

                def group(g, slot, turn):
                    for j in range(J):
                        d = g * J + j
                        if exists(d + DRING):
                            eng.wait_ge(d_T, d + 1)
                            load_d(d + DRING, (slot * J + j) % DRING)
                        eng.wait_ge(d_out, d + 1)
                        p = rows_of(d)
                        eng.dma_start(at(out_dense, d) if p == P else out_tail,
                                      o[0:p, j].rearrange("p q f -> p (q f)")).then_inc(d_stored[j], 16)
                        if j == 2 and (not isinstance(g, int) or g + 2 < E_GROUPS):
                            eng.wait_ge(scattered[slot], 16 * J * turn + 16 * J)
                            load_e(g + 2, slot)
                for h in range(2):
                    load_e(h, h)
                for d in range(DRING):
                    load_d(d, d)
                loop(eng, E_GROUPS - 3, 2, group)
                for g in range(E_GROUPS - 3, E_GROUPS):
                    group(g, g % 2, g // 2)
                for j in range(4):
                    eng.wait_ge(d_stored[j], 16 * E_GROUPS + 16)

            @block.gpsimd
            def _(eng):
                def gather(h, slot, turn):
                    eng.wait_ge(e_idx[slot], 32 * turn + 32)
                    eng.sem_inc(s_begun, 1)
                    for j in range(J):
                        eng.indirect_dma_start(A[:, slot, j, :], None, agg2,
                                               bass.IndirectOffsetOnAxis(ap=idx[:, slot, 0, j:j + 1], axis=0))\
                            .then_inc(gathered[slot], 16)

                def scatter(h, slot):
                    eng.wait_ge(e_x1, h + 1)
                    eng.sem_inc(s_begun, 1)
                    for j in range(J):
                        eng.indirect_dma_start(x1_by_rel, bass.IndirectOffsetOnAxis(ap=idx[:, slot, 1, j:j + 1], axis=0),
                                               x1[:, slot, j, :], None).then_inc(scattered[slot], 16)

                def group(g, slot, turn):
                    if not isinstance(g, int) or g + 1 < E_GROUPS:
                        gather(g + 1, *later(slot, turn, 1, 2))
                    scatter(g, slot)
                gather(0, 0, 0)
                loop(eng, E_GROUPS - 1, 2, group)
                group(E_GROUPS - 1, (E_GROUPS - 1) % 2, (E_GROUPS - 1) // 2)
                for slot in range(2):
                    eng.wait_ge(scattered[slot], 16 * J * len(range(slot, E_GROUPS, 2)))

            @block.tensor
            def _(eng):
                def turn_rows(d, slot, turn):
                    p = rows_of(d)
                    eng.wait_ge(d_loaded[slot], 16 * turn + 16)
                    eng.wait_ge(d_X, d + 1)
                    for h in range(2):
                        ins = eng.transpose(pXT[:, h * p:(h + 1) * p], xd[0:p, slot, h * P:(h + 1) * P], ident[0:p, 0:p])
                    ins.then_inc(d_T, 1)

                def first(d, slot):
                    w = 2 * rows_of(d)
                    eng.wait_ge(d_X, d + 2)
                    eng.wait_ge(d_R0, d + 1)
                    eng.matmul(pH0[:, 0:w], W0_top[:], xT[:, slot % 4, 0:w], start=True, stop=True)
                    eng.matmul(pH0[:, w:2 * w], W0_bot[:], xT[:, slot % 4, 0:w], start=True, stop=True).then_inc(d_H0, 1)

                def second(d, slot):
                    w = 4 * rows_of(d)
                    eng.wait_ge(d_R0, d + 2)
                    eng.wait_ge(d_R1, d + 1)
                    eng.matmul(pH1[:, 0:w], Wr1T[:], h0[:, slot % 4, 0:w], start=True, stop=True).then_inc(d_H1, 1)

                def third(d, slot):
                    p = rows_of(d)
                    eng.wait_ge(d_h2, d + 1)
                    eng.wait_ge(d_y, d + 1)
                    for h in range(2):
                        eng.matmul(pU[0:p, slot % 2, h * 256:(h + 1) * 256], xT[:, slot % 4, h * p:(h + 1) * p],
                                   U_x[:], start=True, stop=False)
                        for k in range(2):
                            q = 2 * h + k
                            ins = eng.matmul(pU[0:p, slot % 2, q * P:(q + 1) * P],
                                             h2[:, slot % 2, (2 * k + h) * p:(2 * k + h + 1) * p],
                                             U_h[:], start=False, stop=k == 1)
                    ins.then_inc(d_U, 1)

                def group(g, slot, turn):
                    for j in range(J):
                        d, s = g * J + j, slot * J + j
                        if exists(d + 1):
                            second(d + 1, s + 1)
                        if exists(d + 2):
                            first(d + 2, s + 2)
                        third(d, s)
                        if exists(d + 3):
                            turn_rows(d + 3, *later(s, turn, 3, DRING))
                for d in range(3):
                    turn_rows(d, d, 0)
                    if d >= 1:
                        first(d - 1, d - 1)
                second(0, 0)
                loop(eng, E_GROUPS - 1, 2, group)
                group(E_GROUPS - 1, (E_GROUPS - 1) % 2, (E_GROUPS - 1) // 2)

            @block.scalar
            def _(eng):
                eng.sem_inc(d_R0, 1)
                eng.sem_inc(d_R1, 1)

                def relu0(d, slot):
                    w = 4 * rows_of(d)
                    eng.wait_ge(d_H0, d + 1)
                    eng.activation(h0[:, slot % 4, 0:w], pH0[:, 0:w], ACT.Relu, bias=SH0D, scale=SC0).then_inc(d_R0, 1)

                def relu1(d, slot):
                    w = 4 * rows_of(d)
                    eng.wait_ge(d_H1, d + 1)
                    eng.activation(h2[:, slot % 2, 0:w], pH1[:, 0:w], ACT.Relu, bias=SH1, scale=SC1).then_inc(d_R1, 1)

                def square_u(d, slot):
                    p = rows_of(d)
                    eng.wait_ge(d_U, d + 1)
                    u = pU[0:p, slot % 2].rearrange("p (q f) -> p q f", q=J)[:, :, 0:OUT]
                    eng.activation(sq1[0:p, slot % 2], u, ACT.Square).then_inc(d_q1, 1)

                def square_y(d, slot):
                    p = rows_of(d)
                    eng.wait_ge(d_yb, d + 1)
                    eng.activation(sq2[0:p, slot % 2], y[0:p, slot % 4], ACT.Square).then_inc(d_q2, 1)

                def root(d, slot, known, var, std, done):
                    p = rows_of(d)
                    eng.wait_ge(known, d + 1)
                    eng.activation(std[0:p, slot % 2], var[0:p, slot % 2], ACT.Sqrt).then_inc(done, 1)

                def step(d, s):
                    if exists(d - 1):
                        square_u(d - 1, s + 7)
                    if exists(d + 1):
                        relu1(d + 1, s + 1)
                    if exists(d - 1):
                        root(d - 1, s + 7, d_v1, var1, std1, d_s1)
                    if exists(d + 2):
                        relu0(d + 2, s + 2)
                    if exists(d - 2):
                        square_y(d - 2, s + 6)
                        root(d - 2, s + 6, d_v2, var2, std2, d_s2)

                def group(g, slot, turn):
                    for j in range(J):
                        step(g * J + j, slot * J + j)
                        if j == 2:
                            eng.wait_ge(e_var, g + 1)
                            eng.activation(rstd[:, slot, 0, :], mv[:, slot, :, 1], ACT.Sqrt).then_inc(e_std, 1)
                relu0(0, 0)
                relu0(1, 1)
                relu1(0, 0)
                group(0, 0, 0)
                group(1, 1, 0)
                loop_from(eng, 2, E_GROUPS - 1, 2, group)
                group(E_GROUPS - 1, (E_GROUPS - 1) % 2, (E_GROUPS - 1) // 2)
                for d in (N_TILES, N_TILES + 1):
                    step(d, d % 8)

            @block.vector
            def _(eng):
                eng.sem_inc(d_X, 1)
                eng.sem_inc(d_y, 2)
                for j in range(4):
                    eng.sem_inc(d_stored[j], 16)

                def copy(d, slot):
                    w = 2 * rows_of(d)
                    eng.wait_ge(d_T, d + 1)
                    eng.tensor_scalar(xT[:, slot % 4, 0:w], pXT[:, 0:w], b2_pair[:], None, ALU.add).then_inc(d_X, 1)

                def residual(d, slot):
                    w = 4 * rows_of(d)
                    eng.wait_ge(d_R1, d + 2)
                    eng.tensor_tensor(h2[:, slot % 2, 0:w], h2[:, slot % 2, 0:w], h0[:, slot % 4, 0:w], ALU.add).then_inc(d_h2, 1)

                def variance(d, slot, squared, sq, mean, var, s_mean, s_var):
                    p = rows_of(d)
                    eng.wait_ge(squared, d + 1)
                    eng.tensor_reduce(mean[0:p, slot % 2], sq[0:p, slot % 2], AX.X, ALU.add).then_inc(s_mean, 1)
                    eng.wait_ge(s_mean, d + 1)
                    eng.tensor_scalar(var[0:p, slot % 2], mean[0:p, slot % 2], 1.0 / OUT, LN_EPS, ALU.mult, ALU.add).then_inc(s_var, 1)

                def first_norm(d, slot):
                    p = rows_of(d)
                    eng.wait_ge(d_s1, d + 1)
                    eng.reciprocal(r1[0:p, slot % 2], std1[0:p, slot % 2]).then_inc(d_r1, 1)
                    um = pU[0:p, slot % 2].rearrange("p (q f) -> p q f", q=J)[:, :, OUT:]
                    eng.wait_ge(d_r1, d + 1)
                    eng.tensor_tensor(y[0:p, slot % 4], um, r1[0:p, slot % 2].unsqueeze(2).to_broadcast([p, J, OUT]),
                                      ALU.mult).then_inc(d_y, 1)
                    eng.wait_ge(d_y, d + 3)
                    eng.tensor_tensor(y[0:p, slot % 4], y[0:p, slot % 4],
                                      biasC_row[0:p].unsqueeze(1).to_broadcast([p, J, OUT]), ALU.add).then_inc(d_yb, 1)

                def second_norm(d, slot, turn):
                    p = rows_of(d)
                    eng.wait_ge(d_s2, d + 1)
                    eng.reciprocal(r2[0:p, slot % 2], std2[0:p, slot % 2]).then_inc(d_r2, 1)
                    eng.wait_ge(d_r2, d + 1)
                    eng.wait_ge(d_stored[slot % 4], 16 * (turn * 2 + slot // 4) + 16)
                    eng.tensor_tensor(o[0:p, slot % 4], y[0:p, slot % 4],
                                      r2[0:p, slot % 2].unsqueeze(2).to_broadcast([p, J, OUT]), ALU.mult).then_inc(d_out, 1)

                def rows(g, slot, turn, part):
                    if part == 0:
                        eng.wait_ge(e_loaded[slot], 16 * turn + 16)
                        eng.wait_ge(gathered[slot], 16 * J * turn + 16 * J)
                        eng.tensor_tensor(ue[:, slot], ue[:, slot], A[:, slot], ALU.add).then_inc(e_sum, 1)
                        eng.wait_ge(e_sum, g + 1)
                        for q in range(J):
                            ins = eng.bn_stats(stats[:, slot, q, :], ue[:, slot, q, :])
                        ins.then_inc(e_st, 1)
                    if part == 1:
                        eng.wait_ge(e_st, g + 1)
                        eng.sem_inc(e_begun, 1)
                        for q in range(J):
                            ins = eng.bn_aggr(mv[:, slot, q, :], stats[:, slot, q, :])
                        ins.then_inc(e_mv, 1)
                    if part == 2:
                        eng.wait_ge(e_mv, g + 1)
                        eng.tensor_scalar(mv[:, slot, :, 1], mv[:, slot, :, 1], LN_EPS, None, ALU.add).then_inc(e_var, 1)
                    if part == 3:
                        eng.wait_ge(e_std, g + 1)
                        eng.reciprocal(rstd[:, slot, 1, :], rstd[:, slot, 0, :]).then_inc(e_r, 1)
                        eng.wait_ge(e_r, g + 1)
                        for q in range(J):
                            ins = eng.tensor_scalar(x1[:, slot, q, :], ue[:, slot, q, :], mv[:, slot, q, 0:1],
                                                    rstd[:, slot, 1, q:q + 1], ALU.subtract, ALU.mult)
                        ins.then_inc(e_x1, 1)

                def step(d, s, turn):
                    if exists(d + 2):
                        copy(d + 2, s + 2)
                    if exists(d - 1):
                        variance(d - 1, s + 7, d_q1, sq1, mean1, var1, d_m1, d_v1)
                    if exists(d + 1):
                        residual(d + 1, s + 1)
                    if exists(d - 1):
                        first_norm(d - 1, s + 7)
                    if exists(d - 2):
                        variance(d - 2, s + 6, d_q2, sq2, mean2, var2, d_m2, d_v2)
                    if exists(d - 3):
                        second_norm(d - 3, (s + 5) % 8, turn - 1 if s < 3 else turn)

                def group(g, slot, turn):
                    for j in range(J):
                        step(g * J + j, slot * J + j, turn)
                        rows(g, slot, turn, j)
                for d in range(2):
                    copy(d, d)
                residual(0, 0)
                group(0, 0, 0)
                group(1, 1, 0)
                loop_from(eng, 2, E_GROUPS - 1, 2, group)
                group(E_GROUPS - 1, (E_GROUPS - 1) % 2, (E_GROUPS - 1) // 2)
                for d in range(N_TILES, N_TILES + 3):
                    step(d, d % 8, d // 8)

        with ExitStack() as ctx:
            sb, psum, sem, ring = makers = tools(nc, ctx, "relations")
            idx = sb("idx", [P, RING, 2], I32)
            W = sb("W", [P, RING, 2, OUT])
            xr = sb("xr", [P, RING, J, IN])
            xrT = sb("xrT", [P, 2, 2 * P])
            msg = sb("msg", [P, RING, J, OUT])
            pT, pM = psum("pT", 2), psum("pM", 4)
            i_loaded, x_loaded, w_got, m_stored = (ring(n, RING) for n in ("i_loaded", "x_loaded", "w_got", "m_stored"))
            s_T, c_T, s_M, c_M, s_begun = (sem(n) for n in ("s_T", "c_T", "s_M", "c_M", "s_begun"))
            block = ctx.enter_context(nc.Block())
            x_tiles = x1_by_rel.rearrange("(m q p) f -> m p q f", q=J, p=P)
            msg_tiles = msg_by_rel.rearrange("(m q p) f -> m p q f", q=J, p=P)
            weight_rows = rel_weights.rearrange("r i o -> (r i) o")

            @block.sync
            def _(eng):
                def load(m, slot):
                    eng.dma_start(idx[:, slot, :], cols(weight_home, m * 2, 2)).then_inc(i_loaded[slot], 16)
                    eng.dma_start(xr[:, slot], at(x_tiles, m)).then_inc(x_loaded[slot], 16)

                def group(m, slot, turn):
                    if not isinstance(m, int) or 0 < m < R_GROUPS - 3:
                        eng.wait_ge(s_M, m)
                        load(m + 3, (slot + 3) % RING)
                    eng.wait_ge(c_M, m + 3)
                    eng.dma_start(at(msg_tiles, m), msg[:, slot]).then_inc(m_stored[slot], 16)
                for m in range(RING):
                    load(m, m)
                for m in range(RING):
                    group(m, m, 0)
                loop_from(eng, RING, R_GROUPS - 3, RING, group)
                for m in range(R_GROUPS - 3, R_GROUPS):
                    group(m, m % RING, m // RING)
                for slot in range(RING):
                    eng.wait_ge(m_stored[slot], 16 * len(range(slot, R_GROUPS, RING)) + 16)

            @block.gpsimd
            def _(eng):
                def gather(m, slot, turn):
                    eng.wait_ge(i_loaded[slot], 16 * turn + 16)
                    eng.sem_inc(s_begun, 1)
                    for h in range(2):
                        eng.indirect_dma_start(W[:, slot, h, :], None, weight_rows,
                                               bass.IndirectOffsetOnAxis(ap=idx[:, slot, h:h + 1], axis=0))\
                            .then_inc(w_got[slot], 16)
                loop(eng, R_GROUPS, RING, gather)

            @block.tensor
            def _(eng):
                def turn_rows(m, slot, turn):
                    eng.wait_ge(x_loaded[slot], 16 * turn + 16)
                    eng.wait_ge(c_T, m + 1)
                    for h in range(2):
                        ins = eng.transpose(pT[:, slot % 2, h * P:(h + 1) * P], xr[:, slot, 2 * h:2 * h + 2, :], ident[:])
                    ins.then_inc(s_T, 1)

                def products(m, slot, turn):
                    eng.wait_ge(w_got[slot], 32 * turn + 32)
                    eng.wait_ge(c_T, m + 3)
                    eng.wait_ge(c_M, m + 2)
                    for h in range(2):
                        for k in range(2):
                            half = slice(k * IN, (k + 1) * IN)
                            ins = eng.matmul(pM[:, 2 * (slot % 2) + k, h * OUT:(h + 1) * OUT], xrT[half, slot % 2, h * P:(h + 1) * P],
                                             W[half, slot, h, :], start=True, stop=True)
                    ins.then_inc(s_M, 1)

                def group(m, slot, turn):
                    if not isinstance(m, int) or m + 1 < R_GROUPS:
                        turn_rows(m + 1, *later(slot, turn, 1, RING))
                    products(m, slot, turn)
                turn_rows(0, 0, 0)
                loop(eng, R_GROUPS - 1, RING, group)
                m = R_GROUPS - 1
                group(m, m % RING, m // RING)

            @block.scalar
            def _(eng):
                eng.sem_inc(c_T, 2)

                def copy(m, slot, turn):
                    eng.wait_ge(s_T, m + 1)
                    eng.wait_ge(c_M, m + 1)
                    eng.activation(xrT[:, slot % 2, :], pT[:, slot % 2, 0:2 * P], ACT.Copy).then_inc(c_T, 1)
                loop(eng, R_GROUPS, RING, copy)

            @block.vector
            def _(eng):
                eng.sem_inc(c_M, 2)
                for slot in range(RING):
                    eng.sem_inc(m_stored[slot], 16)

                def copy(m, slot, turn):
                    eng.wait_ge(s_M, m + 1)
                    eng.wait_ge(m_stored[slot], 16 * turn + 16)
                    eng.tensor_copy(msg[:, slot].rearrange("p (h k) f -> p k h f", k=2),
                                    pM[:, 2 * (slot % 2):2 * (slot % 2) + 2, 0:P].rearrange("p k (h f) -> p k h f", h=2))\
                        .then_inc(c_M, 1)
                loop(eng, R_GROUPS, RING, copy)

        RING = 4
        with ExitStack() as ctx:
            sb, psum, sem, ring = makers = tools(nc, ctx, "final")
            runs = GroupSums(makers, dst_rows, dst_col, prev_last, OUT)
            idx = sb("idx", [P, RING, 2, J], I32)
            M = sb("M", [P, RING, J, OUT])
            v = sb("v", [P, RING, J, OUT])
            A2 = sb("A2", [P, RING, J, OUT])
            A3 = sb("A3", [P, RING, J, OUT])
            x1 = sb("x1", [P, RING, J, OUT])
            x1T = sb("x1T", [P, 2, 2 * P])
            y = sb("y", [P, RING, J, OUT])
            o = sb("o", [P, RING, J, OUT])
            stats = sb("stats", [P, 2, RING, J, 6])
            mv = sb("mv", [P, 2, RING, J, 2])
            std = sb("std", [P, 2, RING, 2, J])
            pT, pY = psum("pT"), psum("pY")
            i_loaded, t_loaded, gathered, scattered = (ring(n, RING) for n in ("i_loaded", "t_loaded", "gathered", "scattered"))
            s_v, s_x1, s_T, c_T, s_Y, c_Y, s_yb, s_y, s_o, s_begun, s_wait = (
                sem(n) for n in ("s_v", "s_x1", "s_T", "c_T", "s_Y", "c_Y", "s_yb", "s_y", "s_o", "s_begun", "s_wait"))
            n_stats, n_mv, n_var, n_std, n_r = ([sem(f"{n}{i}") for i in range(2)]
                                                for n in ("n_stats", "n_mv", "n_var", "n_std", "n_r"))
            block = ctx.enter_context(nc.Block())

            def has(h):
                return not isinstance(h, int) or 0 <= h < E_GROUPS

            @block.sync
            def _(eng):
                def load(h, slot):
                    eng.dma_start(idx[:, slot, 0, :], cols(rel_home, h * J, J)).then_inc(i_loaded[slot], 16)
                    eng.dma_start(idx[:, slot, 1, :], cols(out_home, h * J, J)).then_inc(i_loaded[slot], 16)
                    eng.dma_start(v[:, slot].rearrange("p j f -> p (j f)"), at(u_dst, h)).then_inc(t_loaded[slot], 16)
                    eng.dma_start(A2[:, slot].rearrange("p j f -> p (j f)"), at(agg2_g, h)).then_inc(t_loaded[slot], 16)

                def group(g, slot, turn):
                    if has(g + 2):
                        eng.wait_ge(runs.selected, (J + 1) * g + J + 1)
                        runs.load(eng, g + 2, slot % 2)
                    if has(g + 3) and (not isinstance(g, int) or g > 0):
                        s3, t3 = later(slot, turn, 3, RING)
                        eng.wait_ge(scattered[s3], 16 * J * t3)
                        load(g + 3, s3)
                for h in range(RING):
                    load(h, h)
                for h in range(2):
                    runs.load(eng, h, h)
                for g in range(RING):
                    group(g, g, 0)
                loop_from(eng, RING, E_GROUPS - 3, RING, group)
                for g in range(E_GROUPS - 3, E_GROUPS):
                    group(g, g % RING, g // RING)

            @block.gpsimd
            def _(eng):
                def gather(h, slot, turn):
                    eng.wait_ge(i_loaded[slot], 32 * turn + 32)
                    eng.sem_inc(s_begun, 1)
                    for j in range(J):
                        eng.indirect_dma_start(M[:, slot, j, :], None, msg_by_rel,
                                               bass.IndirectOffsetOnAxis(ap=idx[:, slot, 0, j:j + 1], axis=0))\
                            .then_inc(gathered[slot], 16)

                def scatter(h, slot):
                    eng.wait_ge(s_o, h + 1)
                    eng.sem_inc(s_begun, 1)
                    for j in range(J):
                        eng.indirect_dma_start(out, bass.IndirectOffsetOnAxis(ap=idx[:, slot, 1, j:j + 1], axis=0),
                                               o[:, slot, j, :], None, bounds_check=N_NODES - 1, oob_is_err=False)\
                            .then_inc(scattered[slot], 16)

                def group(g, slot, turn):
                    if has(g + 2):
                        gather(g + 2, *later(slot, turn, 2, RING))
                    scatter(g, slot)
                gather(0, 0, 0)
                gather(1, 1, 0)
                loop(eng, E_GROUPS - 2, RING, group)
                for g in range(E_GROUPS - 2, E_GROUPS):
                    group(g, g % RING, g // RING)
                for slot in range(RING):
                    eng.wait_ge(scattered[slot], 16 * J * len(range(slot, E_GROUPS, RING)))

            @block.tensor
            def _(eng):
                def turn_rows(h, slot):
                    eng.wait_ge(s_x1, h + 1)
                    eng.wait_ge(c_T, h + 1)
                    for i in range(2):
                        ins = eng.transpose(pT[:, i * P:(i + 1) * P], x1[:, slot, 2 * i:2 * i + 2, :], ident[:])
                    ins.then_inc(s_T, 1)

                def own(h, slot):
                    eng.wait_ge(c_T, h + 2)
                    eng.wait_ge(c_Y, h + 1)
                    for i in range(2):
                        ins = eng.matmul(pY[:, i * P:(i + 1) * P], x1T[:, slot % 2, i * P:(i + 1) * P], Ws2[:],
                                         start=True, stop=True)
                    ins.then_inc(s_Y, 1)

                def group(g, slot, turn):
                    eng.wait_ge(gathered[slot], 16 * J * turn + 16 * J)
                    runs.add(eng, g, slot % 2, lambda i: M[:, slot, i, :])
                    if has(g + 1):
                        turn_rows(g + 1, (slot + 1) % RING)
                    runs.carry(eng, g, slot % 2)
                    if has(g + 1):
                        own(g + 1, (slot + 1) % RING)
                turn_rows(0, 0)
                own(0, 0)
                loop(eng, E_GROUPS - 1, RING, group)
                g = E_GROUPS - 1
                group(g, g % RING, g // RING)

            @block.scalar
            def _(eng):
                eng.sem_inc(c_T, 1)

                def copy(h, slot):
                    eng.wait_ge(s_T, h + 1)
                    eng.wait_ge(c_Y, h + 1)
                    eng.activation(x1T[:, slot % 2, :], pT[:, 0:2 * P], ACT.Copy).then_inc(c_T, 1)

                def root(n, h, slot):
                    eng.wait_ge(n_var[n], h + 1)
                    eng.activation(std[:, n, slot, 0, :], mv[:, n, slot, :, 1], ACT.Sqrt).then_inc(n_std[n], 1)

                def group(g, slot, turn):
                    if has(g + 1):
                        copy(g + 1, (slot + 1) % RING)
                    if has(g + 2):
                        root(0, g + 2, (slot + 2) % RING)
                    root(1, g, slot)
                root(0, 0, 0)
                copy(0, 0)
                root(0, 1, 1)
                loop(eng, E_GROUPS - 2, RING, group)
                for g in range(E_GROUPS - 2, E_GROUPS):
                    group(g, g % RING, g // RING)

            @block.vector
            def _(eng):
                eng.sem_inc(c_Y, 1)
                runs.start_vector(eng)
                bias_all = bias_row[:].unsqueeze(1).to_broadcast([P, J, OUT])

                def moments(n, h, slot, rows, ready):
                    eng.wait_ge(ready, h + 1)
                    for q in range(J):
                        ins = eng.bn_stats(stats[:, n, slot, q, :], rows[:, slot, q, :])
                    ins.then_inc(n_stats[n], 1)

                def aggregate(n, h, slot):
                    eng.wait_ge(n_stats[n], h + 1)
                    eng.sem_inc(s_wait, 1)
                    for q in range(J):
                        ins = eng.bn_aggr(mv[:, n, slot, q, :], stats[:, n, slot, q, :])
                    ins.then_inc(n_mv[n], 1)
                    eng.wait_ge(n_mv[n], h + 1)
                    eng.tensor_scalar(mv[:, n, slot, :, 1], mv[:, n, slot, :, 1], LN_EPS, None, ALU.add)\
                        .then_inc(n_var[n], 1)

                def normalize(n, h, slot, rows, to, done):
                    eng.wait_ge(n_std[n], h + 1)
                    eng.reciprocal(std[:, n, slot, 1, :], std[:, n, slot, 0, :]).then_inc(n_r[n], 1)
                    eng.wait_ge(n_r[n], h + 1)
                    for q in range(J):
                        ins = eng.tensor_scalar(to[:, slot, q, :], rows[:, slot, q, :], mv[:, n, slot, q, 0:1],
                                                std[:, n, slot, 1, q:q + 1], ALU.subtract, ALU.mult)
                    ins.then_inc(done, 1)

                def first_sum(h, slot, turn):
                    eng.wait_ge(t_loaded[slot], 32 * turn + 32)
                    eng.tensor_tensor(v[:, slot], v[:, slot], A2[:, slot], ALU.add).then_inc(s_v, 1)
                    moments(0, h, slot, v, s_v)

                def own_sum(h, slot):
                    eng.wait_ge(s_Y, h + 1)
                    eng.tensor_tensor(y[:, slot], pY[:, 0:J * OUT].rearrange("p (j f) -> p j f", j=J), x1[:, slot],
                                      ALU.add).then_inc(c_Y, 1)
                    eng.wait_ge(c_Y, h + 2)
                    eng.tensor_tensor(y[:, slot], y[:, slot], bias_all, ALU.add).then_inc(s_yb, 1)

                def second_sum(h, slot):
                    eng.wait_ge(s_yb, h + 1)
                    eng.wait_ge(runs.read, h + 2)
                    eng.tensor_tensor(y[:, slot], y[:, slot], A3[:, slot], ALU.add).then_inc(s_y, 1)
                    moments(1, h, slot, y, s_y)

                def group(g, slot, turn):
                    nxt, ahead = (slot + 1) % RING, (slot + 2) % RING
                    if has(g + 1):
                        runs.select(eng, g + 1, nxt % 2, later(slot, turn, 1, RING)[1] * 2 + nxt // 2)
                    runs.keep(eng, g, slot % 2)
                    runs.means(eng, slot % 2, A3[:, slot], weight_col, g)
                    second_sum(g, slot)
                    if has(g + 2):
                        first_sum(g + 2, *later(slot, turn, 2, RING))
                        aggregate(0, g + 2, ahead)
                    aggregate(1, g, slot)
                    if has(g + 1):
                        own_sum(g + 1, nxt)
                    if has(g + 2):
                        normalize(0, g + 2, ahead, v, x1, s_x1)
                    normalize(1, g, slot, y, o, s_o)
                for h in range(2):
                    first_sum(h, h, 0)
                    aggregate(0, h, h)
                    normalize(0, h, h, v, x1, s_x1)
                runs.select(eng, 0, 0, 0)
                own_sum(0, 0)
                loop(eng, E_GROUPS - 2, RING, group)
                for g in range(E_GROUPS - 2, E_GROUPS):
                    group(g, g % RING, g // RING)


_INS = ['x', 'src', 'dst', 'edge_type_32', 'L0_gnn_Wl0', 'L0_gnn_Wr0', 'L0_gnn_b0', 'L0_gnn_Wl1', 'L0_gnn_Wr1',
        'L0_gnn_b1', 'L0_gnn_Wl2', 'L0_gnn_Wr2', 'L0_gnn_b2', 'L0_gnn_g0', 'L0_gnn_be0', 'L0_gnn_g1', 'L0_gnn_be1',
        'L1_gnn_basis', 'L1_gnn_coeff', 'L1_gnn_self_weight', 'L1_gnn_bias']


def kernel(**inputs):
    import numpy as _np
    import concourse.bacc as _bacc
    from concourse import mybir as _mybir
    from concourse.bass_utils import run_bass_kernel_spmd as _run

    nc = _bacc.Bacc("TRN2", target_bir_lowering=False, num_devices=1)
    arrays, args = {}, []
    for name in _INS:
        a = _np.ascontiguousarray(inputs[name])
        arrays[f"in_{name}"] = a
        args.append(nc.dram_tensor(f"in_{name}", a.shape, _mybir.dt.from_np(a.dtype), kind="ExternalInput").ap())
    args.append(nc.dram_tensor("out_0", (N_NODES, OUT), F32, kind="ExternalOutput").ap())
    gnn_program(nc, *args)
    return _run(nc, [arrays], core_ids=[0]).results[0]["out_0"]
```

```python
from contextlib import ExitStack

import concourse.bass as bass
import concourse.mybir as mybir

ALU = mybir.AluOpType
ACT = mybir.ActivationFunctionType
AX = mybir.AxisListType
F32 = mybir.dt.float32
I32 = mybir.dt.int32

P = 128
N_NODES = 100000
N_EDGES = 25000
IN = 64
HID = 128
OUT = 64
N_REL = 32
N_BASES = 30
J = 4
GROUP = J * P
E_GROUPS = -(-N_EDGES // GROUP)
E_TILES = E_GROUPS * J
E_ROWS = E_TILES * P
ZERO_ROW = E_ROWS
HALF = E_TILES // 2
D_GROUPS = N_NODES // GROUP
TAIL = N_NODES - D_GROUPS * GROUP
TAIL_P = TAIL // J
R_GROUPS = -(-(E_TILES + N_REL - 1) // J)
R_TILES = R_GROUPS * J
PAD_DST = 1 << 23
BN_EPS = 1e-5
LN_EPS = 1e-5
assert TAIL_P * J == TAIL and 2 * IN == P and HID == P


def at(ap, g):
    if isinstance(g, int):
        return ap[g]
    names = "abcdefg"[: len(ap.shape) - 1]
    spaced = " ".join(names)
    rest = " ".join(names[1:])
    return ap[bass.ds(g, 1)].rearrange(f"z {spaced} -> (z {names[0]}) {rest}")


def cols(ap, start, n):
    return ap[:, bass.ds(start, n)] if not isinstance(start, int) else ap[:, start:start + n]


def later(slot, turn, k, ring):
    return (slot + k) % ring, turn + (slot + k) // ring


def loop(eng, n, unroll, body):
    turns = n // unroll
    if turns > 1:
        with eng.Fori(0, turns) as turn:
            for slot in range(unroll):
                body(turn * unroll + slot, slot, turn)
        first = turns * unroll
    else:
        first = 0
    for g in range(first, n):
        body(g, g % unroll, g // unroll)


def tools(nc, ctx, block):
    sems = []

    def clear():
        nc.clear_and_free_semaphores(sems)
        nc.all_engine_barrier()
    ctx.callback(clear)

    def sb(name, shape, dt=F32):
        return ctx.enter_context(nc.sbuf_tensor(f"{block}_{name}", shape, dt))

    def psum(name, banks=1):
        return ctx.enter_context(nc.psum_tensor(f"{block}_{name}", [P, 512] if banks == 1 else [P, banks, 512], F32))

    def sem(name):
        sems.append(nc.alloc_semaphore(f"{block}_{name}"))
        return sems[-1]

    def ring(name, n=2):
        return [sem(f"{name}{i}") for i in range(n)]

    return sb, psum, sem, ring


def loop_from(eng, first, n, unroll, body):
    turns = (n - first) // unroll
    with eng.Fori(0, turns) as k:
        turn = k + first // unroll
        for slot in range(unroll):
            body(turn * unroll + slot, slot, turn)
    for g in range(first + turns * unroll, n):
        body(g, g % unroll, g // unroll)


class Steps:

    def __init__(self, eng, sem, base=0):
        self.eng, self.sem, self.base, self.n = eng, sem, base, 0

    def did(self, instruction):
        instruction.then_inc(self.sem, 1)
        self.n += 1
        return self.base + self.n

    def settle(self):
        self.eng.wait_ge(self.sem, self.base + self.n)


class RunSums:

    def __init__(self, makers, dst_rows, dst_col, prev_last, width):
        sb, psum, sem, ring = makers
        self.dst_rows, self.dst_col, self.prev_last, self.width = dst_rows, dst_col, prev_last, width
        self.dst_tile = sb("run_dst_tile", [P, 2, GROUP], I32)
        self.S = sb("run_S", [P, 2, J, P])
        self.Q = sb("run_Q", [P, 2, J, P])
        self.kept = sb("run_kept", [P, 2, width])
        self.sums = psum("run_sums", 2)
        self.loaded = [sem(f"run_loaded{i}") for i in range(2)]
        self.selected = sem("run_selected")
        self.summed = sem("run_summed")
        self.copied = sem("run_copied")
        self.scaled = sem("run_scaled")

    def load(self, eng, g, slot):
        row = self.dst_rows[g:g + 1] if isinstance(g, int) else self.dst_rows[bass.ds(g, 1)]
        eng.dma_start(self.dst_tile[:, slot, :], row.rearrange("a c -> (a c)").partition_broadcast(P))\
            .then_inc(self.loaded[slot], 16)

    def start_vector(self, eng):
        eng.memset(self.kept[:, 1, :], 0.0).then_inc(self.copied, 1)

    def select(self, eng, g, slot, turn, which=(0, 1)):
        eng.wait_ge(self.loaded[slot], 16 * turn + 16)
        tile = self.dst_tile[:, slot, :].rearrange("p (j c) -> p j c", j=J)
        for i in which:
            to, col = ((self.S, self.dst_col), (self.Q, self.prev_last))[i]
            eng.tensor_tensor(to[:, slot], tile, cols(col, g * J, J).unsqueeze(2).to_broadcast([P, J, P]),
                              ALU.is_equal).then_inc(self.selected, 1)

    def add(self, eng, g, slot, j, message):
        t = g * J + j
        if j == 0:
            eng.wait_ge(self.selected, 2 * g + 2)
        to = self.sums[:, j % 2, 0:self.width]
        eng.matmul(to, self.S[:, slot, j, :], message, start=True, stop=False)
        eng.wait_ge(self.copied, t + 1)
        eng.matmul(to, self.Q[:, slot, j, :], self.kept[:, (j + 1) % 2, :], start=False, stop=True)\
            .then_inc(self.summed, 1)

    def keep(self, eng, g, j):
        eng.wait_ge(self.summed, g * J + j + 1)
        eng.wait_ge(self.scaled, g * J + j + 1)
        eng.tensor_copy(self.kept[:, j % 2, :], self.sums[:, j % 2, 0:self.width]).then_inc(self.copied, 1)

    def scale(self, eng, g, j, to, weight_col):
        eng.wait_ge(self.copied, g * J + j + 2)
        eng.activation(to, self.kept[:, j % 2, 0:to.shape[-1]], ACT.Copy,
                       scale=cols(weight_col, g * J + j, 1)).then_inc(self.scaled, 1)


class GroupSums:

    FIRST = [0, J, 2 * J - 1, 3 * J - 3]

    def __init__(self, makers, dst_rows, dst_col, prev_last, width, banks=2):
        sb, psum, sem, ring = makers
        self.dst_rows, self.dst_col, self.prev_last, self.width = dst_rows, dst_col, prev_last, width
        self.dst_tile = sb("run_dst_tile", [P, 2, GROUP], I32)
        self.R = sb("run_R", [P, 2, J * (J + 1) // 2, P])
        self.Q = sb("run_Q", [P, 2, J, P])
        self.kept = sb("run_kept", [P, 2, width])
        self.banks = banks
        self.sums = psum("run_sums", banks) if banks > 1 else psum("run_sums")[:].unsqueeze(1)
        self.loaded = [sem(f"run_loaded{i}") for i in range(2)]
        self.selected = sem("run_selected")
        self.summed = sem("run_summed")
        self.copied = sem("run_copied")
        self.read = sem("run_read")

    def load(self, eng, g, slot):
        row = self.dst_rows[g:g + 1] if isinstance(g, int) else self.dst_rows[bass.ds(g, 1)]
        eng.dma_start(self.dst_tile[:, slot, :], row.rearrange("a c -> (a c)").partition_broadcast(P))\
            .then_inc(self.loaded[slot], 16)

    def start_vector(self, eng):
        eng.memset(self.kept[:, 1, :], 0.0).then_inc(self.copied, 1)
        eng.sem_inc(self.read, 2)

    def select(self, eng, g, slot, turn):
        eng.wait_ge(self.loaded[slot], 16 * turn + 16)
        for i in range(J):
            to = self.R[:, slot, self.FIRST[i]:self.FIRST[i] + J - i, :].rearrange("p j c -> p (j c)")
            eng.tensor_scalar(to, self.dst_tile[:, slot, i * P:], cols(self.dst_col, g * J + i, 1), None,
                              ALU.is_equal).then_inc(self.selected, 1)
        eng.tensor_scalar(self.Q[:, slot].rearrange("p j c -> p (j c)"), self.dst_tile[:, slot, :],
                          cols(self.prev_last, g * J, 1), None, ALU.is_equal).then_inc(self.selected, 1)

    def place(self, slot, j):
        return self.sums[:, slot % self.banks, j * self.width:(j + 1) * self.width]

    def add(self, eng, g, slot, message):
        eng.wait_ge(self.selected, (J + 1) * g + J + 1)
        eng.wait_ge(self.read, g + 3 - self.banks)
        for j in range(J):
            for i in range(j + 1):
                eng.matmul(self.place(slot, j), self.R[:, slot, self.FIRST[i] + j - i, :], message(i),
                           start=j == 0 and i == 0, stop=False)

    def carry(self, eng, g, slot):
        eng.wait_ge(self.copied, g + 1)
        for j in range(J):
            ins = eng.matmul(self.place(slot, j), self.Q[:, slot, j, :], self.kept[:, (slot + 1) % 2, :],
                             start=False, stop=j == J - 1)
        ins.then_inc(self.summed, 1)

    def keep(self, eng, g, slot):
        eng.wait_ge(self.summed, g + 1)
        eng.tensor_copy(self.kept[:, slot, :], self.place(slot, J - 1)).then_inc(self.copied, 1)

    def means(self, eng, slot, to, weight_col, g):
        n = to.shape[-1]
        rows = self.sums[:, slot % self.banks, 0:J * self.width].rearrange("p (j f) -> p j f", j=J)[:, :, 0:n]
        eng.tensor_tensor(to, rows, cols(weight_col, g * J, J).unsqueeze(2).to_broadcast([P, J, n]), ALU.mult)\
            .then_inc(self.read, 1)


def gnn_program(nc, x, src, dst, edge_type_32, Wl0, Wr0, b0, Wl1, Wr1, b1, Wl2, Wr2, b2,
                g0, be0, g1, be1, basis, coeff, self_weight, bias, out):
    persistent = ExitStack()

    def scratch(name, shape, dt=F32):
        return nc.dram_tensor(name, shape, dt).ap()

    src_flat = scratch("src_flat", [E_ROWS], I32)
    dst_flat = scratch("dst_flat", [E_ROWS + P], I32)
    typ_flat = scratch("typ_flat", [E_ROWS], I32)
    edge_sorted = scratch("edge_sorted", [E_ROWS, 3], I32)
    x_src = scratch("x_src", [E_GROUPS, P, J * IN])
    x_dst = scratch("x_dst", [E_GROUPS, P, J * IN])
    agg0 = scratch("agg0", [E_ROWS + 1, IN])
    agg1 = scratch("agg1", [E_ROWS + 1, HID])
    agg2 = scratch("agg2", [E_ROWS + 1, OUT])
    h0_src = scratch("h0_src", [E_GROUPS, P, GROUP])
    h0_dst = scratch("h0_dst", [E_GROUPS, P, GROUP])
    h1_dst = scratch("h1_dst", [E_GROUPS, P, GROUP])
    u_src = scratch("u_src", [E_GROUPS, P, J * OUT])
    u_dst = scratch("u_dst", [E_GROUPS, P, J * OUT])
    xT_dense = scratch("xT_dense", [D_GROUPS + 1, P, GROUP // 2])
    x1_by_rel = scratch("x1_by_rel", [R_TILES * P, OUT])
    msg_by_rel = scratch("msg_by_rel", [R_TILES * P, OUT])
    rel_weights = scratch("rel_weights", [N_REL, IN, OUT])

    def grouped(a, width):
        return a[0:E_ROWS].rearrange("(g p j) f -> g p (j f)", p=P, j=J)

    slot_home = scratch("slot_home", [P, E_TILES], I32)
    rel_home = scratch("rel_home", [P, E_TILES], I32)
    weight_home = scratch("weight_home", [P, R_TILES // 2], I32)
    out_home = scratch("out_home", [P, E_TILES], I32)

    agg0_g, agg1_g, agg2_g = grouped(agg0, IN), grouped(agg1, HID), grouped(agg2, OUT)
    src_table = src_flat.rearrange("(t c) -> t c", c=P)
    dst_table = dst_flat[0:E_ROWS].rearrange("(t c) -> t c", c=P)
    typ_table = typ_flat.rearrange("(t c) -> t c", c=P)
    dst_next = dst_flat[1:E_ROWS + 1].rearrange("(t c) -> t c", c=P)

    with ExitStack() as ctx:
        sb, psum, sem, ring = makers = tools(nc, ctx, "order")
        rows_i = sb("rows_i", [HALF, 4, 2, P], I32)
        falls = sb("falls", [HALF, 2, P])
        n_falls = sb("n_falls", [HALF, 2])
        any_fall = sb("any_fall", [1, 1], I32)
        col_i = sb("col_i", [P, 3, E_TILES], I32)
        dst_f = sb("dst_f", [P, E_TILES])
        every = sb("every", [P, E_ROWS], I32)
        SEG = E_ROWS // 8
        junk = sb("junk", [P, SEG])
        lower = sb("lower", [P, P])
        tie = sb("tie", [P, P])
        counts = sb("counts", [P, 9])
        rank = sb("rank", [P, 1])
        rank_i = sb("rank_i", [P, 2, 1], I32)
        edge = sb("edge", [P, 2, 3], I32)
        pF = psum("pF")
        s_edges, s_loaded, s_out, s_next = sem("s_edges"), sem("s_loaded"), sem("s_out"), sem("s_next")
        s_falls, s_summed, s_flag = sem("s_falls"), sem("s_summed"), sem("s_flag")
        s_cols, s_lower, s_float, s_count = sem("s_cols"), sem("s_lower"), sem("s_float"), sem("s_count")
        s_staged, s_gone, s_free, s_back = sem("s_staged"), ring("s_gone"), sem("s_free"), sem("s_back")
        block = ctx.enter_context(nc.Block())
        FULL = N_EDGES // P
        REST = N_EDGES - FULL * P
        tables = (src_table, dst_table, typ_table)
        flats = (src_flat, dst_flat[0:E_ROWS], typ_flat)

        @block.sync
        def _(eng):
            eng.wait_ge(s_edges, 2)
            for n, a in enumerate((src, dst, edge_type_32)):
                eng.dma_start(rows_i[:, n, 0, :], a[0:HALF * P].rearrange("(t c) -> t c", c=P)).then_inc(s_loaded, 16)
                eng.dma_start(rows_i[0:FULL - HALF, n, 1, :],
                              a[HALF * P:FULL * P].rearrange("(t c) -> t c", c=P)).then_inc(s_loaded, 16)
                eng.dma_start(rows_i[FULL - HALF:FULL - HALF + 1, n, 1, 0:REST],
                              a[FULL * P:N_EDGES].rearrange("(t c) -> t c", t=1)).then_inc(s_loaded, 16)
            eng.wait_ge(s_loaded, 16 * 9)
            for n in range(3):
                for h in range(2):
                    eng.dma_start(tables[n][h * HALF:(h + 1) * HALF], rows_i[:, n, h, :]).then_inc(s_out, 16)
            eng.dma_start(dst_flat[E_ROWS:E_ROWS + P].rearrange("(t c) -> t c", t=1),
                          rows_i[HALF - 1:HALF, 3, 0, :]).then_inc(s_out, 16)
            eng.wait_ge(s_out, 16 * 7)
            for h in range(2):
                eng.dma_start(rows_i[:, 3, h, :], dst_next[h * HALF:(h + 1) * HALF]).then_inc(s_next, 16)
            eng.wait_ge(s_flag, 1)
            with eng.If(eng.value_load(any_fall[0:1, 0:1]) != 0), \
                    nc.allow_non_contiguous_dma(reason="only where edges come out of order"):
                for n in range(3):
                    for c in range(0, E_TILES, 28):
                        eng.dma_start(col_i[:, n, c:c + 28], flats[n][c * P:(c + 28) * P].rearrange("(t p) -> p t", p=P))\
                            .then_inc(s_cols, 16)
                eng.dma_start(every[:], flats[1].partition_broadcast(P)).then_inc(s_cols, 16)
                eng.wait_ge(s_free, 2 + E_TILES)
                for n in range(3):
                    for c in range(0, E_TILES, 28):
                        rows = slice(c * P, (c + 28) * P)
                        eng.dma_start(flats[n][rows].rearrange("(e a) -> e a", a=1), edge_sorted[rows, n:n + 1])\
                            .then_inc(s_back, 16)
                eng.wait_ge(s_back, 16 * 3 * (E_TILES // 28))

        @block.tensor
        def _(eng):
            eng.wait_ge(s_falls, 2)
            eng.matmul(pF[0:1, 0:1], n_falls[:, 0:1], n_falls[:, 1:2], start=True, stop=True).then_inc(s_summed, 1)

        @block.gpsimd
        def _(eng):
            eng.wait_ge(s_flag, 1)
            with eng.If(eng.value_load(any_fall[0:1, 0:1]) != 0):
                eng.memset(lower[:], 1.0).then_inc(s_lower, 1)
                eng.wait_ge(s_lower, 1)
                eng.affine_select(out=lower[:], in_=lower[:], compare_op=ALU.is_gt, fill=0.0,
                                  base=0, pattern=[[-1, P]], channel_multiplier=1).then_inc(s_lower, 1)

                def scatter(t, slot, turn):
                    eng.wait_ge(s_staged, 2 * t + 2)
                    eng.sem_inc(s_lower, 1)
                    eng.indirect_dma_start(edge_sorted, bass.IndirectOffsetOnAxis(ap=rank_i[:, slot, :], axis=0),
                                           edge[:, slot, :], None).then_inc(s_gone[slot], 16)
                    eng.wait_ge(s_gone[slot], 16 * turn + 16)
                    eng.sem_inc(s_free, 1)
                loop(eng, E_TILES, 2, scatter)

        @block.vector
        def _(eng):
            eng.memset(rows_i[:], 0).then_inc(s_edges, 1)
            eng.wait_ge(s_edges, 1)
            eng.memset(rows_i[:, 1:4:2, :, :], PAD_DST).then_inc(s_edges, 1)
            eng.memset(n_falls[:, 1:2], 1.0).then_inc(s_falls, 1)
            eng.wait_ge(s_loaded, 16 * 9)
            eng.wait_ge(s_next, 32)
            eng.tensor_tensor(falls[:], rows_i[:, 1], rows_i[:, 3], ALU.is_gt).then_inc(s_count, 1)
            eng.wait_ge(s_count, 1)
            eng.tensor_reduce(n_falls[:, 0:1], falls[:], AX.XY, ALU.add).then_inc(s_falls, 1)
            eng.wait_ge(s_summed, 1)
            eng.tensor_copy(any_fall[:], pF[0:1, 0:1]).then_inc(s_flag, 1)
            eng.wait_ge(s_flag, 1)
            with eng.If(eng.value_load(any_fall[0:1, 0:1]) != 0):
                eng.wait_ge(s_cols, 16 * (3 * (E_TILES // 28) + 1))
                eng.wait_ge(s_lower, 2)
                eng.tensor_copy(dst_f[:], col_i[:, 1, :]).then_inc(s_float, 1)
                every_f = every[:].bitcast(F32)
                eng.tensor_copy(every_f, every[:]).then_inc(s_float, 1)
                eng.wait_ge(s_float, 2)
                eng.sem_inc(s_free, 2)
                STEPS = 12

                def count(t, slot, turn):
                    own = cols(every_f, t * P, P)
                    mine = cols(dst_f, t, 1)
                    n = t * STEPS + 1
                    for i in range(8):
                        eng.tensor_scalar(junk[:], every_f[:, i * SEG:(i + 1) * SEG], mine, 0.0, ALU.is_lt, ALU.add,
                                          accum_out=counts[:, i:i + 1]).then_inc(s_count, 1)
                        eng.wait_ge(s_count, n + i + 1)
                    eng.scalar_tensor_tensor(tie[:], own, mine, lower[:], ALU.is_equal, ALU.mult).then_inc(s_count, 1)
                    eng.wait_ge(s_count, n + 9)
                    eng.tensor_reduce(counts[:, 8:9], tie[:], AX.X, ALU.add).then_inc(s_count, 1)
                    eng.tensor_scalar(own, own, -0.5, None, ALU.add).then_inc(s_count, 1)
                    eng.wait_ge(s_count, n + 11)
                    eng.tensor_reduce(rank[:], counts[:], AX.X, ALU.add).then_inc(s_count, 1)
                    eng.wait_ge(s_count, n + 12)
                    eng.wait_ge(s_free, t + 1)
                    eng.tensor_copy(rank_i[:, slot, :], rank[:]).then_inc(s_staged, 1)
                    eng.tensor_copy(edge[:, slot, :].unsqueeze(2), col_i[:, :, bass.ds(t, 1)]).then_inc(s_staged, 1)
                    eng.wait_ge(s_staged, 2 * t + 2)
                loop(eng, E_TILES, 2, count)

    def keep(name, shape, dt=F32):
        return persistent.enter_context(nc.sbuf_tensor(name, shape, dt))

    with persistent:
        ident = keep("ident", [P, P])
        ones = keep("ones", [P, P])
        src_col = keep("src_col", [P, E_TILES])
        dst_col = keep("dst_col", [P, E_TILES])
        typ_col = keep("typ_col", [P, E_TILES])
        prev_last = keep("prev_last", [P, E_TILES])
        last_col = keep("last_col", [P, E_TILES])
        weight_col = keep("weight_col", [P, E_TILES])
        slot_idx = keep("slot_idx", [P, E_TILES], I32)
        rel_pos = keep("rel_pos", [P, E_TILES], I32)
        out_idx = keep("out_idx", [P, E_TILES], I32)
        W0 = keep("W0", [P, HID])
        W0_top = keep("W0_top", [P, HID])
        W0_bot = keep("W0_bot", [P, HID])
        Wr1T = keep("Wr1T", [P, HID])
        Wl1T = keep("Wl1T", [P, HID])
        W2_msg = keep("W2_msg", [P, 2 * OUT])
        U_h = keep("U_h", [P, 2 * OUT])
        U_x = keep("U_x", [P, 4 * OUT])
        Ws2 = keep("Ws2", [P, 2 * OUT])
        b2_pair = keep("b2_pair", [P, 1])
        b2_row = keep("b2_row", [P, OUT])
        bias_row = keep("bias_row", [P, OUT])
        biasC_row = keep("biasC_row", [P, OUT])
        bn = keep("bn", [P, 16])
        G0, BE0, B0, G1, BE1, B1 = (bn[:, i:i + 1] for i in range(6))
        SC0, SH0, SH0D, SC1, SH1 = (bn[:, i:i + 1] for i in range(6, 11))
        gram = keep("gram", [P, P])
        zsum = keep("zsum", [P, 1])
        is_127 = keep("is_127", [P, 1])
        eps_col = keep("eps_col", [P, 1])
        number = keep("number", [P, P])
        tile_of = keep("tile_of", [P, E_TILES])
        slot_base = keep("slot_base", [P, E_TILES])
        dst_in = keep("dst_in", [P, E_TILES])

        with ExitStack() as ctx:
            sb, psum, sem, ring = makers = tools(nc, ctx, "layout")
            rows_i = sb("rows_i", [HALF, 4, 2, P], I32)
            rows_f = sb("rows_f", [HALF, 4, 2, P])
            wraw = sb("wraw", [P, 7, P])
            w2raw = sb("w2raw", [OUT, 2, HID])
            ws_sb = sb("ws_sb", [IN, OUT])
            coeff_sb = sb("coeff_sb", [N_REL, N_BASES])
            coeffT = sb("coeffT", [N_BASES, N_REL])
            basis_sb = sb("basis_sb", [N_BASES, IN * OUT])
            rw_sb = sb("rw_sb", [N_REL, IN * OUT])
            zeros = sb("zeros", [P, 2048])
            rsel = sb("rsel", [P, 4])
            idT = sb("idT", [IN, P])
            r2cT = sb("r2cT", [OUT, P])
            mean_c = sb("mean_c", [P, 4])
            p = [psum(f"p{i}") for i in range(8)]
            s_loaded, s_weights = sem("s_loaded"), sem("s_weights")
            s_set = sem("s_set")
            s_const, s_zero, s_zeroed, s_pool = sem("s_const"), sem("s_zero"), sem("s_zeroed"), sem("s_pool")
            s_dve, s_pe, s_rw, s_rw_out = sem("s_dve"), sem("s_pe"), sem("s_rw"), sem("s_rw_out")
            block = ctx.enter_context(nc.Block())

            @block.gpsimd
            def _(eng):
                eng.memset(ident[:], 0.0).then_inc(s_pool, 1)
                eng.iota(rsel[:, 0:1].bitcast(I32), [[0, 1]], base=0, channel_multiplier=1).then_inc(s_pool, 1)
                eng.wait_ge(s_pool, 2)
                eng.affine_select(out=ident[:], in_=ident[:], compare_op=ALU.not_equal, fill=1.0,
                                  base=0, pattern=[[-1, P]], channel_multiplier=1).then_inc(s_const, 1)

            @block.sync
            def _(eng):
                for n, table in enumerate((src_table, dst_table, typ_table, dst_next)):
                    for h in range(2):
                        eng.dma_start(rows_i[:, n, h, :], table[h * HALF:(h + 1) * HALF]).then_inc(s_loaded, 16)
                eng.wait_ge(s_zero, 5)
                for d, s in ((wraw[:, 0, 0:IN], Wr0), (wraw[:, 0, IN:], Wl0), (wraw[:, 1, 0:IN], Wr0),
                             (wraw[:, 2, IN:], Wr0), (wraw[:, 3, :], Wr1), (wraw[:, 4, :], Wl1),
                             (w2raw[:, 0, :], Wl2), (w2raw[:, 1, :], Wr2), (ws_sb[:], self_weight),
                             (coeff_sb[:], coeff), (basis_sb[:], basis.rearrange("b i o -> b (i o)")),
                             (Ws2[0:IN, 0:OUT], self_weight), (Ws2[IN:P, OUT:], self_weight),
                             (b2_pair[0:IN], b2.rearrange("(p a) -> p a", a=1)),
                             (b2_pair[IN:P], b2.rearrange("(p a) -> p a", a=1)),
                             (b2_row[:], b2.partition_broadcast(P)), (bias_row[:], bias.partition_broadcast(P)),
                             (G0, g0.rearrange("(p a) -> p a", a=1)), (BE0, be0.rearrange("(p a) -> p a", a=1)),
                             (B0, b0.rearrange("(p a) -> p a", a=1)), (G1, g1.rearrange("(p a) -> p a", a=1)),
                             (BE1, be1.rearrange("(p a) -> p a", a=1)), (B1, b1.rearrange("(p a) -> p a", a=1))):
                    eng.dma_start(d, s).then_inc(s_weights, 16)
                for a in (agg0, agg1, agg2):
                    eng.dma_start(a[E_ROWS:E_ROWS + 1], zeros[0:1, 0:a.shape[1]]).then_inc(s_zeroed, 16)
                flat = x1_by_rel.rearrange("(p q) f -> p (q f)", p=P)
                width, n = flat.shape[1], 0
                for c in range(0, width, 2048):
                    w = min(2048, width - c)
                    eng.dma_start(flat[:, c:c + w], zeros[:, 0:w]).then_inc(s_zeroed, 16)
                    n += 1
                eng.wait_ge(s_rw, 8)
                eng.dma_start(rel_weights.rearrange("r i o -> r (i o)"), rw_sb[:]).then_inc(s_rw_out, 16)
                eng.wait_ge(s_zeroed, 16 * (3 + n))
                eng.wait_ge(s_rw_out, 16)

            @block.tensor
            def _(eng):
                t = Steps(eng, s_pe)
                eng.wait_ge(s_const, 1)
                eng.wait_ge(s_weights, 16 * 23)
                for n in range(4):
                    t.did(eng.transpose(p[0][:, n * P:(n + 1) * P], wraw[:, n, :], ident[:]))
                t.did(eng.transpose(p[1][:, 0:P], wraw[:, 4, :], ident[:]))
                for n in range(2):
                    t.did(eng.transpose(p[1][:, P + n * OUT:P + (n + 1) * OUT], w2raw[:, n, :], ident[0:OUT, 0:OUT]))
                t.did(eng.transpose(p[1][0:N_BASES, 256:256 + N_REL], coeff_sb[:], ident[0:N_REL, 0:N_REL]))
                eng.wait_ge(s_set, 1)
                for n in range(4):
                    for h in range(2):
                        t.did(eng.transpose(p[2 + n][:, h * HALF:(h + 1) * HALF], rows_f[:, n, h, :],
                                            ident[0:HALF, 0:HALF]))
                eng.wait_ge(s_dve, 8)
                for c in range(8):
                    if c >= 2:
                        eng.wait_ge(s_rw, c - 1)
                    t.did(eng.matmul(p[6 + c % 2][0:N_REL, :], coeffT[:], basis_sb[:, c * 512:(c + 1) * 512],
                                     start=True, stop=True))
                eng.wait_ge(s_dve, 13)
                t.did(eng.matmul(p[0][:, 0:OUT], idT[:], ws_sb[:], start=True, stop=True))
                t.did(eng.transpose(p[1][0:OUT, 0:P], U_h[:, 0:OUT], ident[:]))
                eng.wait_ge(s_dve, 14)
                t.did(eng.matmul(p[0][:, OUT:2 * OUT], r2cT[:], ws_sb[:], start=True, stop=True))

            @block.vector
            def _(eng):
                eng.memset(wraw[:], 0.0).then_inc(s_zero, 1)
                eng.memset(Ws2[:], 0.0).then_inc(s_zero, 1)
                eng.memset(zeros[:], 0.0).then_inc(s_zero, 1)
                eng.memset(ones[:], 1.0).then_inc(s_zero, 1)
                eng.memset(eps_col[:], LN_EPS).then_inc(s_zero, 1)
                eng.wait_ge(s_loaded, 16 * 8)
                eng.tensor_copy(rows_f[:], rows_i[:]).then_inc(s_set, 1)
                t = Steps(eng, s_dve)
                eng.wait_ge(s_pe, 8)
                for n, w in enumerate((W0, W0_top, W0_bot, Wr1T)):
                    t.did(eng.tensor_copy(w[:], p[0][:, n * P:(n + 1) * P]))
                t.did(eng.tensor_copy(Wl1T[:], p[1][:, 0:P]))
                t.did(eng.tensor_copy(W2_msg[:], p[1][:, P:2 * P]))
                t.did(eng.tensor_copy(coeffT[:], p[1][0:N_BASES, 256:256 + N_REL]))
                t.did(eng.tensor_reduce(mean_c[:, 0:1], p[1][:, P + OUT:2 * P], AX.X, ALU.add))
                t.settle()
                t.did(eng.tensor_scalar(mean_c[:, 0:1], mean_c[:, 0:1], -1.0 / OUT, None, ALU.mult))
                t.settle()
                t.did(eng.tensor_scalar(U_h[:, 0:OUT], W2_msg[:, OUT:], mean_c[:, 0:1], None, ALU.add))
                for h in range(2):
                    t.did(eng.tensor_scalar(idT[:, h * OUT:(h + 1) * OUT], ident[0:OUT, 0:OUT], -1.0 / OUT, None, ALU.add))
                t.did(eng.memset(U_x[:], 0.0))
                eng.wait_ge(s_pe, 26)
                t.did(eng.tensor_copy(r2cT[:], p[1][0:OUT, 0:P]))
                t.settle()
                for h in range(2):
                    q = slice(h * IN, (h + 1) * IN)
                    t.did(eng.tensor_scalar(U_x[q, h * P:h * P + OUT], ident[q, q], -1.0 / OUT, None, ALU.add))
                eng.wait_ge(s_pe, 27)
                t.settle()
                t.did(eng.tensor_tensor(U_h[:, OUT:], U_h[:, 0:OUT], p[0][:, OUT:2 * OUT], ALU.add))
                for h in range(2):
                    q = slice(h * IN, (h + 1) * IN)
                    t.did(eng.tensor_tensor(U_x[q, h * P + OUT:(h + 1) * P], U_x[q, h * P:h * P + OUT],
                                            p[0][q, 0:OUT], ALU.add))
                t.settle()
                t.did(eng.tensor_reduce(mean_c[:, 1:2], U_h[:, OUT:], AX.X, ALU.add))
                for h in range(2):
                    q = slice(h * IN, (h + 1) * IN)
                    t.did(eng.tensor_reduce(mean_c[q, 2:3], U_x[q, h * P + OUT:(h + 1) * P], AX.X, ALU.add))
                t.did(eng.tensor_reduce(mean_c[:, 3:4], bias_row[:], AX.X, ALU.add))
                t.settle()
                t.did(eng.tensor_scalar(mean_c[:], mean_c[:], -1.0 / OUT, None, ALU.mult))
                t.settle()
                t.did(eng.tensor_scalar(U_h[:, OUT:], U_h[:, OUT:], mean_c[:, 1:2], None, ALU.add))
                for h in range(2):
                    q = slice(h * IN, (h + 1) * IN)
                    ux = U_x[q, h * P + OUT:(h + 1) * P]
                    t.did(eng.tensor_scalar(ux, ux, mean_c[q, 2:3], None, ALU.add))
                t.did(eng.tensor_scalar(biasC_row[:], bias_row[:], mean_c[:, 3:4], None, ALU.add))
                eng.wait_ge(s_pe, 16)
                t.did(eng.tensor_copy(src_col[:], p[2][:, 0:E_TILES]))
                t.did(eng.tensor_copy(dst_col[:], p[3][:, 0:E_TILES]))
                t.did(eng.tensor_copy(typ_col[:], p[4][:, 0:E_TILES]))
                t.did(eng.tensor_copy(rsel[:, 1:2], rsel[:, 0:1].bitcast(I32)))
                t.settle()
                t.did(eng.tensor_tensor(last_col[:], dst_col[:], p[5][:, 0:E_TILES], ALU.not_equal))
                t.did(eng.tensor_scalar(prev_last[:], dst_col[:], float(N_NODES), None, ALU.is_lt))
                t.did(eng.tensor_scalar(is_127[:], rsel[:, 1:2], float(P - 1), None, ALU.is_equal))
                t.settle()
                t.did(eng.tensor_tensor(last_col[:], last_col[:], prev_last[:], ALU.mult))
                t.settle()
                t.did(eng.memset(prev_last[:, 0:1], -1.0))
                t.did(eng.tensor_scalar(prev_last[:, 1:], dst_col[:, 0:E_TILES - 1], 1.0, is_127[:],
                                        ALU.add, ALU.mult))
                t.settle()
                t.did(eng.tensor_scalar(prev_last[:, 1:], prev_last[:, 1:], -1.0, None, ALU.add))
                t.did(eng.tensor_scalar(weight_col[:], dst_col[:], -float(PAD_DST), None, ALU.add))
                t.settle()
                t.did(eng.tensor_tensor(weight_col[:], weight_col[:], last_col[:], ALU.mult))
                t.settle()
                t.did(eng.tensor_scalar(out_idx[:], weight_col[:], float(PAD_DST), None, ALU.add))
                t.settle()

            @block.scalar
            def _(eng):
                for c in range(8):
                    eng.wait_ge(s_pe, 17 + c)
                    eng.activation(rw_sb[:, c * 512:(c + 1) * 512], p[6 + c % 2][0:N_REL, :], ACT.Copy).then_inc(s_rw, 1)

        RING = 4
        DRING = 8
        with ExitStack() as ctx:
            sb, psum, sem, ring = makers = tools(nc, ctx, "lookup")
            xd = sb("xd", [P, DRING, J * IN])
            xg = sb("xg", [P, RING, J * IN])
            idx = sb("idx", [P, RING, J], I32)
            tile_i = sb("tile_i", [P, 3, E_TILES], I32)
            pos_i = sb("pos_i", [P, 3, E_TILES], I32)
            tile_f = sb("tile_f", [P, 2, E_TILES])
            tile_first = sb("tile_first", [P, E_TILES])
            hit = sb("hit", [P, E_TILES])
            junk = sb("junk", [P, J, E_TILES])
            before = sb("before", [P, P])
            sel_row = sb("sel_row", [P, P])
            ramp = sb("ramp", [P, R_TILES], I32)
            ramp_f = sb("ramp_f", [P, R_TILES])
            hot = sb("hot", [P, N_REL, E_TILES])
            within = sb("within", [P, N_REL, E_TILES])
            count = sb("count", [P, N_REL, E_TILES])
            upto = sb("upto", [P, N_REL, E_TILES])
            rel = sb("rel", [P, 8, N_REL])
            rel_i = sb("rel_i", [P, N_REL], I32)
            part_id = sb("part_id", [P, 2], I32)
            cmp = sb("cmp", [P, R_TILES // 2, N_REL])
            rel_of = sb("rel_of", [P, R_TILES])
            rel_start = sb("rel_start", [P, 2])
            weight_row = sb("weight_row", [P, R_TILES // 2], I32)
            xsum = sb("xsum", [P, IN])
            zero = sb("zero", [P, 256])
            pGram = psum("pGram")
            pSum = psum("pSum")
            pFirst = psum("pFirst")
            pRel = psum("pRel", 4)
            s_const, s_dve = sem("s_const"), sem("s_dve")
            d_free = sem("d_free")
            d_loaded = [sem(f"d_loaded{i}") for i in range(DRING)]
            s_first = sem("s_first")
            s_hot, s_rel, s_rel_got = sem("s_hot"), sem("s_rel"), sem("s_rel_got")
            idx_ready, got, kept = sem("idx_ready"), ring("got", RING), ring("kept", RING)
            s_begun, s_count = sem("s_begun"), sem("s_count")
            s_slots, s_homes = sem("s_slots"), sem("s_homes")
            block = ctx.enter_context(nc.Block())
            x_dense = x[0:D_GROUPS * GROUP].rearrange("(g p q) f -> g p (q f)", p=P, q=J)
            x_tail = x[D_GROUPS * GROUP:N_NODES].rearrange("(p q) f -> p (q f)", q=J)
            hot_flat, within_flat, count_flat = (a[:].rearrange("p r t -> p (r t)") for a in (hot, within, count))
            WIDTH = N_REL * E_TILES
            CHUNKS = [(c, min(512, WIDTH - c)) for c in range(0, WIDTH, 512)]

            @block.sync
            def _(eng):
                def load(g, slot, turn):
                    eng.wait_ge(d_free, g + 1)
                    eng.dma_start(xd[:, slot, :], at(x_dense, g)).then_inc(d_loaded[slot], 16)
                loop(eng, D_GROUPS, DRING, load)
                eng.wait_ge(d_free, D_GROUPS + 1)
                slot = D_GROUPS % DRING
                eng.dma_start(xd[0:TAIL_P, slot, :], x_tail).then_inc(d_loaded[slot], 16)
                eng.dma_start(out_home, out_idx[:]).then_inc(s_homes, 16)
                eng.wait_ge(s_slots, 1)
                eng.dma_start(rel_home, rel_pos[:]).then_inc(s_homes, 16)
                eng.dma_start(weight_home, weight_row[:]).then_inc(s_homes, 16)
                eng.wait_ge(s_homes, 48)

            @block.gpsimd
            def _(eng):
                eng.iota(ramp[:], [[1, R_TILES]], base=0, channel_multiplier=0).then_inc(s_const, 1)
                eng.memset(before[:], 0.0).then_inc(s_const, 1)
                for h in range(2):
                    eng.iota(part_id[:, h:h + 1], [[0, 1]], base=-IN * h, channel_multiplier=1).then_inc(s_const, 1)
                eng.wait_ge(s_const, 4)
                eng.affine_select(out=before[:], in_=before[:], compare_op=ALU.is_ge, fill=1.0,
                                  base=0, pattern=[[-1, P]], channel_multiplier=1).then_inc(s_const, 1)

                def gather_x(g, slot, turn):
                    eng.wait_ge(idx_ready, g + 1)
                    eng.sem_inc(s_begun, 1)
                    for j in range(J):
                        eng.indirect_dma_start(xg[:, slot, j * IN:(j + 1) * IN], None, x,
                                               bass.IndirectOffsetOnAxis(ap=idx[:, slot, j:j + 1], axis=0))\
                            .then_inc(got[slot], 16)
                loop(eng, E_GROUPS, RING, gather_x)

            @block.scalar
            def _(eng):
                for slot in range(RING):
                    eng.sem_inc(kept[slot], 16)

                def stage(g, slot):
                    eng.activation(idx[:, slot, :], cols(src_col, g * J, J), ACT.Copy).then_inc(idx_ready, 1)

                def store(g, slot, turn):
                    eng.wait_ge(got[slot], 16 * J * turn + 16 * J)
                    eng.dma_start(at(x_src, g), xg[:, slot, :]).then_inc(kept[slot], 16)

                def both(g, slot, turn):
                    store(g, slot, turn)
                    ahead = (slot + 2) % RING
                    eng.wait_ge(kept[ahead], 16 * (turn + (slot + 2) // RING) + 16)
                    stage(g + 2, ahead)
                stage(0, 0)
                stage(1, 1)
                loop(eng, E_GROUPS - 2, RING, both)
                for g in range(E_GROUPS - 2, E_GROUPS):
                    store(g, g % RING, g // RING)
                for slot in range(RING):
                    eng.wait_ge(kept[slot], 16 * len(range(slot, E_GROUPS, RING)) + 16)

            @block.tensor
            def _(eng):
                eng.wait_ge(s_dve, 3)
                eng.matmul(pFirst[:, 0:E_TILES], sel_row[:], dst_col[:], start=True, stop=True).then_inc(s_first, 1)
                eng.matmul(pGram[0:IN, 0:IN], zero[:, 0:IN], zero[:, 0:IN], start=True, stop=False)
                eng.matmul(pSum[:, 0:J * IN], zero[:, 0:P], zero[:], start=True, stop=False)
                eng.sem_inc(d_free, DRING)

                def add(g, slot, turn, p=P, last=False):
                    eng.wait_ge(d_loaded[slot], 16 * turn + 16)
                    for q in range(J):
                        rows = xd[0:p, slot, q * IN:(q + 1) * IN]
                        eng.matmul(pGram[0:IN, 0:IN], rows, rows, start=False, stop=last and q == J - 1)
                    eng.matmul(pSum[:, 0:J * IN], ones[0:p, :], xd[0:p, slot, :], start=False,
                               stop=last).then_inc(d_free, 1)
                FIRST_PART = D_GROUPS // (2 * DRING) * DRING
                loop(eng, FIRST_PART, DRING, add)
                eng.wait_ge(s_hot, 1)
                eng.wait_ge(s_const, 5)
                for n, (c, w) in enumerate(CHUNKS):
                    if n >= 2:
                        eng.wait_ge(s_rel_got, 2 * (n - 1))
                    eng.matmul(pRel[:, n % 2, 0:w], before[:], hot_flat[:, c:c + w], start=True, stop=True).then_inc(s_rel, 1)
                    eng.matmul(pRel[:, 2 + n % 2, 0:w], ones[:], hot_flat[:, c:c + w], start=True, stop=True).then_inc(s_rel, 1)
                loop_from(eng, FIRST_PART, D_GROUPS, DRING, add)
                add(D_GROUPS, D_GROUPS % DRING, D_GROUPS // DRING, TAIL_P, True)

            @block.vector
            def _(eng):
                t = Steps(eng, s_dve)
                t.did(eng.memset(zero[:], 0.0))
                t.did(eng.memset(sel_row[:], 1.0))
                t.settle()
                t.did(eng.tensor_scalar(sel_row[:], sel_row[:], ident[:, 0:1], None, ALU.mult))
                t.did(eng.tensor_scalar(dst_in[:], dst_col[:], float(N_NODES - 1), None, ALU.min))
                eng.wait_ge(s_const, 5)
                t.did(eng.tensor_copy(ramp_f[:], ramp[:]))
                t.settle()
                t.did(eng.tensor_scalar(number[:], ramp_f[:, 0:P], 1.0, None, ALU.add))
                relid = ramp_f[:, 0:N_REL].unsqueeze(2).to_broadcast([P, N_REL, E_TILES])
                eng.tensor_tensor(hot[:], typ_col[:].unsqueeze(1).to_broadcast([P, N_REL, E_TILES]), relid,
                                  ALU.is_equal).then_inc(s_hot, 1)
                eng.wait_ge(s_first, 1)
                t.did(eng.tensor_copy(tile_first[:], pFirst[:, 0:E_TILES]))
                t.settle()

                def below(g, slot, turn):
                    for j in range(J):
                        eng.wait_ge(s_count, g * J + j + 1)
                        eng.tensor_scalar(junk[:, j, :], tile_first[:], cols(src_col, g * J + j, 1), 0.0,
                                          ALU.is_le, ALU.add, accum_out=cols(tile_of, g * J + j, 1)).then_inc(s_count, 1)
                eng.sem_inc(s_count, J)
                loop(eng, E_GROUPS, 1, below)
                eng.wait_ge(s_count, J + E_TILES)
                t.did(eng.tensor_scalar(tile_of[:], tile_of[:], -1.0, 0.0, ALU.add, ALU.max))
                t.settle()
                t.did(eng.tensor_copy(tile_i[:, 2, :], tile_of[:]))
                t.settle()
                t.did(eng.tensor_scalar(tile_i[:, 1, :], tile_i[:, 2, :], J - 1, None, ALU.bitwise_and))
                t.did(eng.tensor_scalar(tile_i[:, 0, :], tile_i[:, 2, :], 2, 9, ALU.arith_shift_right, ALU.logical_shift_left))
                t.settle()
                t.did(eng.tensor_copy(tile_f[:], tile_i[:, 0:2, :]))
                t.settle()
                t.did(eng.scalar_tensor_tensor(slot_base[:], tile_f[:, 0, :], -float(J + ZERO_ROW), tile_f[:, 1, :],
                                               ALU.add, ALU.add))
                for n, (c, w) in enumerate(CHUNKS):
                    eng.wait_ge(s_rel, 2 * n + 1)
                    eng.tensor_copy(within_flat[:, c:c + w], pRel[:, n % 2, 0:w]).then_inc(s_rel_got, 1)
                    eng.wait_ge(s_rel, 2 * n + 2)
                    eng.tensor_copy(count_flat[:, c:c + w], pRel[:, 2 + n % 2, 0:w]).then_inc(s_rel_got, 1)
                eng.wait_ge(s_rel_got, 2 * len(CHUNKS))
                upto_flat = upto[:].rearrange("p r t -> p (r t)")
                t.did(eng.tensor_tensor_scan(upto_flat, ones[:, 0:1].to_broadcast([P, WIDTH]), count_flat, 0.0,
                                             ALU.mult, ALU.add))
                t.settle()
                ends, starts, size, pends, pstarts, shift = (rel[:, i, :] for i in range(6))
                t.did(eng.tensor_copy(ends, upto[:, :, E_TILES - 1]))
                t.did(eng.memset(starts[:, 0:1], 0.0))
                t.did(eng.memset(pstarts[:, 0:1], 0.0))
                t.settle()
                t.did(eng.tensor_copy(starts[:, 1:], ends[:, 0:N_REL - 1]))
                t.settle()
                t.did(eng.tensor_tensor(size, ends, starts, ALU.subtract))
                t.settle()
                t.did(eng.tensor_scalar(rel_i[:], size, float(P - 1), None, ALU.add))
                t.settle()
                t.did(eng.tensor_scalar(rel_i[:], rel_i[:], 7, 7, ALU.arith_shift_right, ALU.logical_shift_left))
                t.settle()
                t.did(eng.tensor_copy(size, rel_i[:]))
                t.settle()
                t.did(eng.tensor_tensor_scan(pends, ones[:, 0:N_REL], size, 0.0, ALU.mult, ALU.add))
                t.settle()
                t.did(eng.tensor_copy(pstarts[:, 1:], pends[:, 0:N_REL - 1]))
                t.settle()
                t.did(eng.tensor_tensor(shift, pstarts, starts, ALU.subtract))
                t.did(eng.tensor_tensor(upto[:], upto[:], count[:], ALU.subtract))
                t.settle()
                t.did(eng.tensor_tensor(within[:], within[:], upto[:], ALU.add))
                t.settle()
                t.did(eng.tensor_tensor(within[:], within[:], shift.unsqueeze(2).to_broadcast([P, N_REL, E_TILES]), ALU.add))
                t.settle()
                t.did(eng.tensor_tensor(within[:], within[:], hot[:], ALU.mult))
                t.settle()
                t.did(eng.tensor_reduce(hit[:], within[:].rearrange("p r t -> p t r"), AX.X, ALU.add))
                t.settle()
                t.did(eng.tensor_copy(pos_i[:, 0, :], hit[:]))
                t.settle()
                t.did(eng.tensor_scalar(pos_i[:, 1, :], pos_i[:, 0, :], P - 1, 2, ALU.bitwise_and, ALU.logical_shift_left))
                t.did(eng.tensor_scalar(pos_i[:, 2, :], pos_i[:, 0, :], 9, 9, ALU.arith_shift_right, ALU.logical_shift_left))
                t.did(eng.tensor_scalar(pos_i[:, 0, :], pos_i[:, 0, :], 7, J - 1, ALU.arith_shift_right, ALU.bitwise_and))
                t.settle()
                t.did(eng.tensor_tensor(pos_i[:, 1, :], pos_i[:, 1, :], pos_i[:, 2, :], ALU.add))
                t.settle()
                t.did(eng.tensor_tensor(rel_pos[:], pos_i[:, 1, :], pos_i[:, 0, :], ALU.add))
                t.did(eng.tensor_scalar(ramp_f[:], ramp_f[:], float(P), None, ALU.mult))
                t.settle()
                for h in range(2):
                    part = slice(h * R_TILES // 2, (h + 1) * R_TILES // 2)
                    shape = [P, R_TILES // 2, N_REL]
                    t.did(eng.tensor_tensor(cmp[:], pends.unsqueeze(1).to_broadcast(shape),
                                            ramp_f[:, part].unsqueeze(2).to_broadcast(shape), ALU.is_le))
                    t.settle()
                    t.did(eng.tensor_reduce(rel_of[:, part], cmp[:], AX.X, ALU.add))
                    t.settle()
                t.did(eng.tensor_scalar(rel_of[:], rel_of[:], float(N_REL - 1), float(IN), ALU.min, ALU.mult))
                t.did(eng.tensor_copy(rel_start[:], part_id[:]))
                t.settle()
                for h in range(2):
                    q = slice(h * IN, (h + 1) * IN)
                    t.did(eng.tensor_scalar(weight_row[q], rel_of[q].rearrange("p (m h) -> p m h", h=2)[:, :, h],
                                            rel_start[q, h:h + 1], None, ALU.add))
                t.settle()
                eng.sem_inc(s_slots, 1)
                eng.wait_ge(d_free, DRING + D_GROUPS + 1)
                t.did(eng.tensor_copy(gram[0:IN, 0:IN], pGram[0:IN, 0:IN]))
                t.did(eng.tensor_reduce(xsum[:], pSum[:, 0:J * IN].rearrange("p (q f) -> p f q", q=J), AX.X, ALU.add))
                t.settle()
                t.did(eng.tensor_tensor(xsum[0:IN], xsum[0:IN], ident[0:IN, 0:IN], ALU.mult))
                t.settle()
                t.did(eng.tensor_reduce(zsum[0:IN], xsum[0:IN], AX.X, ALU.add))
                t.settle()

        dst_rows = dst_flat[0:E_ROWS].rearrange("(g c) -> g c", c=GROUP)
        with ExitStack() as ctx:
            sb, psum, sem, ring = makers = tools(nc, ctx, "agg0")
            runs = GroupSums(makers, dst_rows, dst_col, prev_last, IN + 1)
            xs = sb("xs", [P, RING, J, IN + 1])
            Z = sb("Z", [P, RING, J, P + 1])
            wy = sb("wy", [P, HID + 1])
            recip = sb("recip", [P, J])
            st = sb("st", [P, 8])
            idx = sb("idx", [P, RING, J], I32)
            pZ = psum("pZ")
            pBN = psum("pBN")
            m_loaded, z_got, z_stored = (ring(n, RING) for n in ("m_loaded", "z_got", "z_stored"))
            s_ones, s_weighed, s_gram = sem("s_ones"), sem("s_weighed"), sem("s_gram")
            s_dve, s_pe, s_recip = sem("s_dve"), sem("s_pe"), sem("s_recip")
            s_var, s_std = sem("s_var"), sem("s_std")
            s_idx, s_idx_seen = sem("s_idx"), sem("s_idx_seen")
            block = ctx.enter_context(nc.Block())

            @block.sync
            def _(eng):
                def load(g, slot):
                    eng.dma_start(xs[:, slot, :, 0:IN], at(x_src, g).rearrange("p (j f) -> p j f", j=J))\
                        .then_inc(m_loaded[slot], 16)

                def group(g, slot, turn):
                    if not isinstance(g, int) or g + 2 < E_GROUPS:
                        eng.wait_ge(runs.selected, (J + 1) * g + J + 1)
                        runs.load(eng, g + 2, slot % 2)
                    eng.wait_ge(z_got[slot], 16 * J * turn + 16 * J)
                    eng.dma_start(at(x_dst, g).rearrange("p (j f) -> p j f", j=J), Z[:, slot, :, 0:IN])\
                        .then_inc(z_stored[slot], 16)
                    eng.wait_ge(runs.read, g + 3)
                    eng.dma_start(at(agg0_g, g).rearrange("p (j f) -> p j f", j=J), Z[:, slot, :, IN:P])\
                        .then_inc(z_stored[slot], 16)
                    if not isinstance(g, int) or 0 < g < E_GROUPS - 3:
                        eng.wait_ge(s_gram, g)
                        load(g + 3, (slot + 3) % RING)
                for h in range(RING):
                    if h < 2:
                        runs.load(eng, h, h)
                    load(h, h)
                for g in range(RING):
                    group(g, g, 0)
                loop_from(eng, RING, E_GROUPS - 3, RING, group)
                for g in range(E_GROUPS - 3, E_GROUPS):
                    group(g, g % RING, g // RING)
                for slot in range(RING):
                    eng.wait_ge(z_stored[slot], 32 * len(range(slot, E_GROUPS, RING)) + 16)

            @block.gpsimd
            def _(eng):
                def gather(h, slot, turn):
                    if not isinstance(h, int) or h >= RING:
                        eng.wait_ge(z_stored[slot], 32 * turn + 16)
                        eng.wait_ge(s_gram, h - RING + 1)
                    eng.tensor_copy(idx[:, slot, :], cols(dst_in, h * J, J)).then_inc(s_idx, 1)
                    eng.wait_ge(s_idx, h + 1)
                    eng.sem_inc(s_idx_seen, 1)
                    for j in range(J):
                        eng.indirect_dma_start(Z[:, slot, j, 0:IN], None, x,
                                               bass.IndirectOffsetOnAxis(ap=idx[:, slot, j:j + 1], axis=0))\
                            .then_inc(z_got[slot], 16)
                for h in range(RING):
                    gather(h, h, 0)
                loop_from(eng, RING, E_GROUPS, RING, gather)

            @block.tensor
            def _(eng):
                eng.wait_ge(s_ones, 3)
                eng.matmul(pZ[:, 0:P + 1], wy[:, 0:P], wy[:], start=True, stop=False)

                def gram_of(g, slot, turn, last=False):
                    eng.wait_ge(runs.read, g + 3)
                    eng.wait_ge(z_got[slot], 16 * J * turn + 16 * J)
                    for j in range(J):
                        rows = Z[:, slot, j, :]
                        ins = eng.matmul(pZ[:, 0:P + 1], rows[:, 0:P], rows, start=False, stop=last and j == J - 1)
                    ins.then_inc(s_gram, 1)

                def group(g, slot, turn):
                    eng.wait_ge(m_loaded[slot], 16 * turn + 16)
                    runs.add(eng, g, slot % 2, lambda i: xs[:, slot, i, :])
                    runs.carry(eng, g, slot % 2)
                    if not isinstance(g, int) or g > 0:
                        gram_of(g - 1, (slot + 3) % RING, turn if slot else turn - 1)
                for g in range(RING):
                    group(g, g, 0)
                loop_from(eng, RING, E_GROUPS, RING, group)
                gram_of(E_GROUPS - 1, (E_GROUPS - 1) % RING, (E_GROUPS - 1) // RING, True)
                t = Steps(eng, s_pe)
                eng.wait_ge(s_dve, 4)
                t.did(eng.matmul(pBN[:, 0:HID], gram[:], W0[:], start=True, stop=True))
                t.did(eng.matmul(pBN[:, HID:HID + 1], W0[:], zsum[:], start=True, stop=True))
                t.did(eng.matmul(pBN[:, HID + 1:HID + 2], W0_top[:], b2_pair[:], start=True, stop=True))
                eng.wait_ge(s_dve, 5)
                t.did(eng.matmul(pBN[:, HID + 2:HID + 3], wy[:, 0:HID], ones[:, 0:1], start=True, stop=True))

            @block.scalar
            def _(eng):
                eng.wait_ge(s_var, 1)
                eng.activation(st[:, 4:5], st[:, 2:3], ACT.Sqrt).then_inc(s_std, 1)

            @block.vector
            def _(eng):
                eng.memset(xs[:, :, :, IN:], 1.0).then_inc(s_ones, 1)
                eng.memset(Z[:, :, :, P:], 1.0).then_inc(s_ones, 1)
                eng.memset(wy[:], 0.0).then_inc(s_ones, 1)
                for slot in range(RING):
                    eng.sem_inc(z_stored[slot], 16)
                runs.start_vector(eng)

                def group(g, slot, turn):
                    two = slot % 2
                    if not isinstance(g, int) or g + 1 < E_GROUPS:
                        runs.select(eng, g + 1, 1 - two, turn * 2 + (slot + 1) // 2)
                    runs.keep(eng, g, two)
                    degree = runs.sums[:, two, 0:J * (IN + 1)].rearrange("p (j f) -> p j f", j=J)[:, :, IN]
                    eng.reciprocal(recip[:], degree).then_inc(s_recip, 1)
                    eng.wait_ge(s_recip, g + 1)
                    eng.tensor_tensor(cols(weight_col, g * J, J), cols(last_col, g * J, J), recip[:],
                                      ALU.mult).then_inc(s_weighed, 1)
                    eng.wait_ge(s_weighed, g + 1)
                    eng.wait_ge(z_stored[slot], 32 * turn + 16)
                    runs.means(eng, two, Z[:, slot, :, IN:P], weight_col, g)
                runs.select(eng, 0, 0, 0)
                loop(eng, E_GROUPS - 1, RING, group)
                group(E_GROUPS - 1, (E_GROUPS - 1) % RING, (E_GROUPS - 1) // RING)
                t = Steps(eng, s_dve)
                eng.wait_ge(s_gram, E_GROUPS)
                t.did(eng.tensor_copy(gram[0:IN, IN:P], pZ[0:IN, IN:P]))
                t.did(eng.tensor_copy(gram[IN:P, :], pZ[IN:P, 0:P]))
                t.did(eng.tensor_copy(zsum[IN:P], pZ[IN:P, P:P + 1]))
                t.settle()
                t.did(eng.memset(st[:], 0.0))
                eng.wait_ge(s_pe, 3)
                t.did(eng.tensor_tensor(wy[:, 0:HID], W0[:], pBN[:, 0:HID], ALU.mult))
                mean, ex2, var, tmp = (st[:, i:i + 1] for i in range(4))
                eng.wait_ge(s_pe, 4)
                t.settle()
                t.did(eng.tensor_scalar(mean, pBN[:, HID:HID + 1], 1.0 / N_NODES, None, ALU.mult))
                t.did(eng.tensor_scalar(ex2, pBN[:, HID + 2:HID + 3], 1.0 / N_NODES, None, ALU.mult))
                t.settle()
                t.did(eng.tensor_tensor(var, mean, mean, ALU.mult))
                t.settle()
                t.did(eng.tensor_tensor(var, ex2, var, ALU.subtract))
                t.settle()
                eng.tensor_scalar(var, var, 0.0, BN_EPS, ALU.max, ALU.add).then_inc(s_var, 1)
                eng.wait_ge(s_std, 1)
                t.did(eng.reciprocal(var, st[:, 4:5]))
                t.settle()
                t.did(eng.tensor_tensor(SC0, G0, var, ALU.mult))
                t.did(eng.tensor_tensor(tmp, mean, B0, ALU.add))
                t.settle()
                t.did(eng.tensor_tensor(tmp, B0, tmp, ALU.subtract))
                t.settle()
                t.did(eng.tensor_tensor(tmp, tmp, SC0, ALU.mult))
                t.settle()
                t.did(eng.tensor_tensor(SH0, BE0, tmp, ALU.add))
                t.settle()
                t.did(eng.tensor_tensor(tmp, SC0, pBN[:, HID + 1:HID + 2], ALU.mult))
                t.settle()
                t.did(eng.tensor_tensor(SH0D, SH0, tmp, ALU.subtract))
                t.settle()

        statD = keep("statD", [P, (D_GROUPS + 1) * 6])
        with ExitStack() as ctx:
            sb, psum, sem, ring = makers = tools(nc, ctx, "layer1")
            runs = RunSums(makers, dst_rows, dst_col, prev_last, HID)
            xd = sb("xd", [P, DRING, J * IN])
            xT = sb("xT", [P, 4, GROUP // 2])
            h0d = sb("h0d", [P, 2, GROUP])
            Z = sb("Z", [P, 2, J, P])
            idx = sb("idx", [P, 2, J], I32)
            tab = sb("tab", [P, 2, J, P], I32)
            tile_idx = sb("tile_idx", [P, 2, J], I32)
            match = sb("match", [P, 2, J, P])
            hit = sb("hit", [P, 2, 3, J])
            zT = sb("zT", [P, GROUP])
            h0e = sb("h0e", [P, 2, GROUP])
            msg = sb("msg", [P, 2, J, HID])
            agg_out = sb("agg_out", [P, 2, J * HID])
            pXT, pH0, pH1, pZT, pHE, pM = (psum(n) for n in ("pXT", "pH0", "pH1", "pZT", "pHE", "pM"))
            d_loaded = ring("d_loaded", DRING)
            d_transposed, d_xT, d_h0, d_relu, d_h1, d_stats = (
                sem(n) for n in ("d_transposed", "d_xT", "d_h0", "d_relu", "d_h1", "d_stats"))
            x_loaded, tab_got, gathered = ring("x_loaded"), ring("tab_got"), ring("gathered")
            s_tile_idx, s_matched, s_hit, s_place, s_base, s_slot, s_home = (
                sem(n) for n in ("s_tile_idx", "s_matched", "s_hit", "s_place", "s_base", "s_slot", "s_home"))
            h0_stored, agg_stored, xT_stored = ring("h0_stored"), ring("agg_stored"), ring("xT_stored", 4)
            e_transposed, e_zT, e_h0, e_relu, e_msgT, e_msg = (
                sem(n) for n in ("e_transposed", "e_zT", "e_h0", "e_relu", "e_msgT", "e_msg"))
            s_begun = sem("s_begun")
            block = ctx.enter_context(nc.Block())
            LAST = E_GROUPS - 1
            assert E_GROUPS * J == D_GROUPS + 1

            def rows_of(d):
                return TAIL_P if isinstance(d, int) and d == D_GROUPS else P

            @block.sync
            def _(eng):
                def load_rows(h, slot):
                    eng.dma_start(Z[:, slot, :, 0:IN], at(x_src, h).rearrange("p (j f) -> p j f", j=J))\
                        .then_inc(x_loaded[slot], 16)

                def load_dense(d, slot):
                    if isinstance(d, int) and d > D_GROUPS:
                        return
                    p = rows_of(d)
                    eng.dma_start(xd[0:p, slot, :], at(x_dense, d) if p == P else x_tail).then_inc(d_loaded[slot], 16)

                def store_xT(d, slot):
                    w = 2 * rows_of(d)
                    eng.wait_ge(d_xT, d + 2)
                    eng.dma_start(at(xT_dense, d)[:, 0:w], xT[:, slot, 0:w]).then_inc(xT_stored[slot], 16)

                def store_h0(h, slot):
                    eng.wait_ge(e_relu, h + 2)
                    eng.dma_start(at(h0_src, h), h0e[:, slot, :]).then_inc(h0_stored[slot], 16)

                def group(g, slot, turn):
                    for j in range(J):
                        if not isinstance(g, int) or g * J + j + DRING <= D_GROUPS:
                            eng.wait_ge(d_transposed, g * J + j + 1)
                            load_dense(g * J + j + DRING, (slot * J + j) % DRING)
                        store_xT(g * J + j, j)
                    if not isinstance(g, int) or g + 3 < E_GROUPS:
                        eng.wait_ge(e_transposed, g + 2)
                        load_rows(g + 3, (slot + 1) % 2)
                    eng.wait_ge(runs.scaled, J * g + J + 2)
                    eng.dma_start(at(agg1_g, g), agg_out[:, slot, :]).then_inc(agg_stored[slot], 16)
                    if not isinstance(g, int) or g + 2 < E_GROUPS:
                        runs.load(eng, g + 2, slot)
                    if not isinstance(g, int) or g + 1 < E_GROUPS:
                        store_h0(g + 1, (slot + 1) % 2)
                for h in range(2):
                    load_rows(h, h)
                    runs.load(eng, h, h)
                for d in range(DRING):
                    load_dense(d, d)
                eng.wait_ge(e_transposed, 1)
                load_rows(2, 0)
                store_h0(0, 0)
                loop(eng, E_GROUPS - 3, 2, group)
                for g in range(E_GROUPS - 3, E_GROUPS):
                    group(g, g % 2, g // 2)
                for slot in range(4):
                    eng.wait_ge(xT_stored[slot], 16 * E_GROUPS + 16)
                eng.wait_ge(s_slot, 2 * E_GROUPS)
                eng.dma_start(slot_home, slot_idx[:]).then_inc(s_home, 16)
                eng.wait_ge(s_home, 16)
                for slot in range(2):
                    eng.wait_ge(h0_stored[slot], 16 * len(range(slot, E_GROUPS, 2)) + 16)
                    eng.wait_ge(agg_stored[slot], 16 * len(range(slot, E_GROUPS, 2)) + 16)

            @block.gpsimd
            def _(eng):
                def gather_dst(h, slot):
                    if not isinstance(h, int) or h > 0:
                        eng.wait_ge(s_matched, h)
                    eng.tensor_copy(tile_idx[:, slot, :], cols(tile_of, h * J, J)).then_inc(s_tile_idx, 1)
                    eng.wait_ge(s_tile_idx, h + 1)
                    eng.sem_inc(s_begun, 1)
                    for j in range(J):
                        eng.indirect_dma_start(tab[:, slot, j, :], None, dst_table,
                                               bass.IndirectOffsetOnAxis(ap=tile_idx[:, slot, j:j + 1], axis=0))\
                            .then_inc(tab_got[slot], 16)

                def gather(h, slot, turn):
                    eng.wait_ge(s_slot, 2 * h + 2)
                    eng.sem_inc(s_begun, 1)
                    eng.wait_ge(x_loaded[slot], 16 * turn + 16)
                    eng.sem_inc(s_begun, 1)
                    for j in range(J):
                        eng.indirect_dma_start(Z[:, slot, j, IN:P], None, agg0,
                                               bass.IndirectOffsetOnAxis(ap=idx[:, slot, j:j + 1], axis=0))\
                            .then_inc(gathered[slot], 16)

                def both(h, slot, turn):
                    gather_dst(h + 1, (slot + 1) % 2)
                    gather(h, slot, turn)
                gather_dst(0, 0)
                loop(eng, E_GROUPS - 1, 2, both)
                gather(E_GROUPS - 1, (E_GROUPS - 1) % 2, (E_GROUPS - 1) // 2)

            @block.tensor
            def _(eng):
                def transpose_dense(d, slot, turn):
                    p = rows_of(d)
                    eng.wait_ge(d_loaded[slot], 16 * turn + 16)
                    eng.wait_ge(d_xT, d + 1)
                    for h in range(2):
                        ins = eng.transpose(pXT[:, h * p:(h + 1) * p], xd[0:p, slot, h * P:(h + 1) * P], ident[0:p, 0:p])
                    ins.then_inc(d_transposed, 1)

                def first_dense(d, slot):
                    w = 2 * rows_of(d)
                    eng.wait_ge(d_xT, d + 2)
                    eng.wait_ge(d_relu, d + 1)
                    eng.matmul(pH0[:, 0:w], W0_top[:], xT[:, slot % 4, 0:w], start=True, stop=True)
                    eng.matmul(pH0[:, w:2 * w], W0_bot[:], xT[:, slot % 4, 0:w], start=True, stop=True).then_inc(d_h0, 1)

                def second_dense(d, slot):
                    w = 4 * rows_of(d)
                    eng.wait_ge(d_relu, d + 2)
                    eng.wait_ge(d_stats, d + 1)
                    eng.matmul(pH1[:, 0:w], Wr1T[:], h0d[:, slot % 2, 0:w], start=True, stop=True).then_inc(d_h1, 1)

                def transpose_rows(g, slot, turn):
                    eng.wait_ge(x_loaded[slot], 16 * turn + 16)
                    eng.wait_ge(gathered[slot], 16 * J * turn + 16 * J)
                    eng.wait_ge(e_zT, g + 1)
                    for j in range(J):
                        ins = eng.transpose(pZT[:, j * P:(j + 1) * P], Z[:, slot, j, :], ident[:])
                    ins.then_inc(e_transposed, 1)

                def first_rows(g):
                    eng.wait_ge(e_zT, g + 2)
                    eng.wait_ge(e_relu, g + 1)
                    eng.matmul(pHE[:], W0[:], zT[:], start=True, stop=True).then_inc(e_h0, 1)

                def message(g, slot):
                    eng.wait_ge(e_relu, g + 2)
                    eng.wait_ge(e_msg, g + 1)
                    for j in range(J):
                        ins = eng.transpose(pM[:, j * P:(j + 1) * P], h0e[:, slot, j * P:(j + 1) * P], ident[:])
                    ins.then_inc(e_msgT, 1)

                def group(g, slot, turn):
                    more = not isinstance(g, int) or g + 1 < E_GROUPS
                    s1, t1 = later(slot, turn, 1, 2)
                    eng.wait_ge(e_msg, g + 2)
                    for j in range(J):
                        runs.add(eng, g, slot, j, msg[:, slot, j, :])
                        d = g * J + j
                        if not isinstance(d, int) or d + 2 <= D_GROUPS:
                            transpose_dense(d + 2, *later(slot * J + j, turn, 2, DRING))
                        if not isinstance(d, int) or d + 1 <= D_GROUPS:
                            first_dense(d + 1, slot * J + j + 1)
                        second_dense(d, slot * J + j)
                        if more and j == 0:
                            transpose_rows(g + 1, s1, t1)
                        if more and j == 1:
                            first_rows(g + 1)
                        if more and j == 2:
                            message(g + 1, s1)
                transpose_rows(0, 0, 0)
                transpose_dense(0, 0, 0)
                first_rows(0)
                transpose_dense(1, 1, 0)
                first_dense(0, 0)
                message(0, 0)
                loop(eng, E_GROUPS - 1, 2, group)
                group(LAST, LAST % 2, LAST // 2)

            @block.scalar
            def _(eng):
                eng.sem_inc(runs.scaled, 2)
                eng.sem_inc(e_zT, 1)
                eng.sem_inc(e_relu, 1)
                eng.sem_inc(d_relu, 1)
                for slot in range(2):
                    eng.sem_inc(agg_stored[slot], 16)
                    eng.sem_inc(h0_stored[slot], 16)

                def relu_dense(d, slot):
                    w = 4 * rows_of(d)
                    eng.wait_ge(d_h0, d + 1)
                    eng.activation(h0d[:, slot % 2, 0:w], pH0[:, 0:w], ACT.Relu, bias=SH0D, scale=SC0).then_inc(d_relu, 1)

                def copy_rows(g):
                    eng.wait_ge(e_transposed, g + 1)
                    eng.activation(zT[:], pZT[:], ACT.Copy).then_inc(e_zT, 1)

                def relu_rows(g, slot, turn):
                    eng.wait_ge(e_h0, g + 1)
                    eng.wait_ge(h0_stored[slot], 16 * turn + 16)
                    eng.activation(h0e[:, slot, :], pHE[:], ACT.Relu, bias=SH0, scale=SC0).then_inc(e_relu, 1)

                def group(g, slot, turn):
                    more = not isinstance(g, int) or g + 1 < E_GROUPS
                    eng.wait_ge(agg_stored[slot], 16 * turn + 16)
                    for j in range(J):
                        runs.scale(eng, g, j, agg_out[:, slot, j * HID:(j + 1) * HID], weight_col)
                        d = g * J + j
                        if not isinstance(d, int) or d + 1 <= D_GROUPS:
                            relu_dense(d + 1, slot * J + j + 1)
                        if more and j == 0:
                            copy_rows(g + 1)
                        if more and j == 1:
                            relu_rows(g + 1, *later(slot, turn, 1, 2))
                copy_rows(0)
                relu_rows(0, 0, 0)
                relu_dense(0, 0)
                loop(eng, E_GROUPS - 1, 2, group)
                group(LAST, LAST % 2, LAST // 2)

            @block.vector
            def _(eng):
                eng.sem_inc(e_msg, 1)
                eng.sem_inc(s_matched, 1)
                eng.sem_inc(d_xT, 1)
                eng.sem_inc(d_stats, 1)
                for slot in range(4):
                    eng.sem_inc(xT_stored[slot], 16)
                runs.start_vector(eng)

                def copy_dense(d, slot, turn):
                    w = 2 * rows_of(d)
                    eng.wait_ge(d_transposed, d + 1)
                    eng.wait_ge(xT_stored[slot % 4], 16 * (2 * turn + slot // 4) + 16)
                    eng.tensor_scalar(xT[:, slot % 4, 0:w], pXT[:, 0:w], b2_pair[:], None, ALU.add).then_inc(d_xT, 1)

                def stats_dense(d):
                    w = 4 * rows_of(d)
                    eng.wait_ge(d_h1, d + 1)
                    eng.bn_stats(cols(statD, d * 6, 6), pH1[:, 0:w]).then_inc(d_stats, 1)

                def copy_message(g, slot):
                    eng.wait_ge(e_msgT, g + 1)
                    eng.tensor_copy(msg[:, slot], pM[:].rearrange("p (j f) -> p j f", j=J)).then_inc(e_msg, 1)

                def match_rows(h, slot, turn):
                    eng.wait_ge(tab_got[slot], 16 * J * turn + 16 * J)
                    for j in range(J):
                        ins = eng.scalar_tensor_tensor(match[:, slot, j, :], tab[:, slot, j, :],
                                                       cols(src_col, h * J + j, 1), number[:], ALU.is_equal, ALU.mult)
                    ins.then_inc(s_matched, 1)

                def place_of(h, slot):
                    eng.wait_ge(s_matched, h + 2)
                    eng.tensor_reduce(hit[:, slot, 0, :], match[:, slot, :, :], AX.X, ALU.max).then_inc(s_hit, 1)

                def row_of(h, slot):
                    place, row, found = (hit[:, slot, i, :] for i in range(3))
                    eng.wait_ge(s_hit, h + 1)
                    eng.scalar_tensor_tensor(row, place, float(J), cols(slot_base, h * J, J), ALU.mult, ALU.add)\
                        .then_inc(s_place, 1)
                    eng.wait_ge(s_place, h + 1)
                    eng.scalar_tensor_tensor(found, place, 0.0, row, ALU.is_gt, ALU.mult).then_inc(s_base, 1)

                def give_row(h, slot, turn):
                    found = hit[:, slot, 2, :]
                    eng.wait_ge(s_base, h + 1)
                    if not isinstance(h, int) or h > 1:
                        eng.wait_ge(gathered[slot], 16 * J * turn)
                    for to in (idx[:, slot, :], cols(slot_idx, h * J, J)):
                        eng.tensor_scalar(to, found, float(ZERO_ROW), None, ALU.add).then_inc(s_slot, 1)

                def group(g, slot, turn):
                    more = not isinstance(g, int) or g + 1 < E_GROUPS
                    for j in range(J):
                        runs.keep(eng, g, j)
                        if more and j == 3:
                            copy_message(g + 1, (slot + 1) % 2)
                        d = g * J + j
                        if not isinstance(d, int) or d + 2 <= D_GROUPS:
                            copy_dense(d + 2, slot * J + j + 2, turn)
                        stats_dense(d)
                        if more and j in (1, 2):
                            runs.select(eng, g + 1, *later(slot, turn, 1, 2), which=(j - 1,))
                        if not isinstance(g, int) or g + 3 < E_GROUPS:
                            s3, t3 = later(slot, turn, 3, 2)
                            if j == 0:
                                match_rows(g + 3, s3, t3)
                            if j == 2:
                                place_of(g + 3, s3)
                            if j == 3:
                                row_of(g + 3, s3)
                                give_row(g + 3, s3, t3)
                for h in range(3):
                    match_rows(h, h % 2, h // 2)
                    place_of(h, h % 2)
                    row_of(h, h % 2)
                    give_row(h, h % 2, h // 2)
                runs.select(eng, 0, 0, 0)
                copy_dense(0, 0, 0)
                copy_dense(1, 1, 0)
                copy_message(0, 0)
                loop(eng, E_GROUPS - 3, 2, group)
                for g in range(E_GROUPS - 3, E_GROUPS):
                    group(g, g % 2, g // 2)

        with ExitStack() as ctx:
            sb, psum, sem, ring = makers = tools(nc, ctx, "bn1")
            Z = sb("Z", [P, 2, J, P])
            A = sb("A", [P, 2, J, HID])
            zT = sb("zT", [P, GROUP])
            aT = sb("aT", [P, 2, GROUP])
            h0 = sb("h0", [P, 2, GROUP])
            h0v = sb("h0v", [P, 2, GROUP])
            h1 = sb("h1", [P, 2, GROUP])
            statT = sb("statT", [P, E_GROUPS * 6])
            statV = sb("statV", [P, E_GROUPS * 6])
            st = sb("st", [P, 16])
            pZ, pA, pH0, pV0, pH1, pV1 = (psum(n) for n in ("pZ", "pA", "pH0", "pV0", "pH1", "pV1"))
            loaded, h0_stored, h1_stored = ring("loaded"), ring("h0_stored"), ring("h1_stored")
            s_Z, s_A, s_H0, s_V0, s_H1, s_V1 = (sem(f"s_{n}") for n in ("Z", "A", "H0", "V0", "H1", "V1"))
            c_z, c_a, c_h0, c_v0 = (sem(f"c_{n}") for n in ("z", "a", "h0", "v0"))
            c_h1, c_v1, s_copy = sem("c_h1"), sem("c_v1"), sem("s_copy")
            s_dve, s_var, s_std = sem("s_dve"), sem("s_var"), sem("s_std")
            block = ctx.enter_context(nc.Block())
            LAST = E_GROUPS - 1

            @block.sync
            def _(eng):
                def load(h, slot):
                    for to, of in ((Z[:, slot, :, 0:IN], x_dst), (Z[:, slot, :, IN:P], agg0_g), (A[:, slot], agg1_g)):
                        eng.dma_start(to, at(of, h).rearrange("p (j f) -> p j f", j=J)).then_inc(loaded[slot], 16)

                def store_h0(h, slot):
                    eng.wait_ge(c_h0, h + 2)
                    eng.dma_start(at(h0_dst, h), h0[:, slot, :]).then_inc(h0_stored[slot], 16)

                def group(g, slot, turn):
                    if not isinstance(g, int) or g + 1 < E_GROUPS:
                        store_h0(g + 1, (slot + 1) % 2)
                    if not isinstance(g, int) or g + 3 < E_GROUPS:
                        eng.wait_ge(s_A, g + 2)
                        load(g + 3, (slot + 1) % 2)
                    eng.wait_ge(s_copy, g + 1)
                    eng.dma_start(at(h1_dst, g), h1[:, slot, :]).then_inc(h1_stored[slot], 16)
                load(0, 0)
                load(1, 1)
                eng.wait_ge(s_A, 1)
                load(2, 0)
                store_h0(0, 0)
                loop(eng, E_GROUPS - 3, 2, group)
                for g in range(E_GROUPS - 3, E_GROUPS):
                    group(g, g % 2, g // 2)
                for slot in range(2):
                    eng.wait_ge(h0_stored[slot], 16 * len(range(slot, E_GROUPS, 2)) + 16)
                    eng.wait_ge(h1_stored[slot], 16 * len(range(slot, E_GROUPS, 2)) + 16)

            @block.tensor
            def _(eng):
                def turn_rows(g, slot, turn):
                    eng.wait_ge(loaded[slot], 48 * turn + 48)
                    eng.wait_ge(c_z, g + 1)
                    for j in range(J):
                        ins = eng.transpose(pZ[:, j * P:(j + 1) * P], Z[:, slot, j, :], ident[:])
                    ins.then_inc(s_Z, 1)
                    eng.wait_ge(c_a, g + 1)
                    for j in range(J):
                        ins = eng.transpose(pA[:, j * P:(j + 1) * P], A[:, slot, j, :], ident[:])
                    ins.then_inc(s_A, 1)

                def first(g):
                    eng.wait_ge(c_z, g + 2)
                    eng.wait_ge(c_h0, g + 1)
                    eng.matmul(pH0[:], W0[:], zT[:], start=True, stop=True).then_inc(s_H0, 1)
                    eng.wait_ge(c_v0, g + 1)
                    eng.matmul(pV0[:], W0_top[:], zT[:], start=True, stop=True).then_inc(s_V0, 1)

                def second(g, slot):
                    eng.wait_ge(c_h0, g + 2)
                    eng.wait_ge(c_a, g + 2)
                    eng.wait_ge(c_h1, g + 1)
                    eng.matmul(pH1[:], Wr1T[:], h0[:, slot, :], start=True, stop=False)
                    eng.matmul(pH1[:], Wl1T[:], aT[:, slot, :], start=False, stop=True).then_inc(s_H1, 1)
                    eng.wait_ge(c_v0, g + 2)
                    eng.wait_ge(c_v1, g + 1)
                    eng.matmul(pV1[:], Wr1T[:], h0v[:, slot, :], start=True, stop=True).then_inc(s_V1, 1)

                def group(g, slot, turn):
                    more = not isinstance(g, int) or g + 1 < E_GROUPS
                    if more:
                        turn_rows(g + 1, *later(slot, turn, 1, 2))
                    second(g, slot)
                    if more:
                        first(g + 1)
                turn_rows(0, 0, 0)
                first(0)
                loop(eng, LAST, 2, group)
                group(LAST, LAST % 2, LAST // 2)

            @block.scalar
            def _(eng):
                for s in (c_z, c_a, c_h0, c_v0):
                    eng.sem_inc(s, 1)
                for slot in range(2):
                    eng.sem_inc(h0_stored[slot], 16)

                def group(g, slot, turn):
                    eng.wait_ge(s_Z, g + 1)
                    eng.activation(zT[:], pZ[:], ACT.Copy).then_inc(c_z, 1)
                    eng.wait_ge(s_A, g + 1)
                    eng.activation(aT[:, slot, :], pA[:], ACT.Copy).then_inc(c_a, 1)
                    eng.wait_ge(s_H0, g + 1)
                    eng.wait_ge(h0_stored[slot], 16 * turn + 16)
                    eng.activation(h0[:, slot, :], pH0[:], ACT.Relu, bias=SH0, scale=SC0).then_inc(c_h0, 1)
                    eng.wait_ge(s_V0, g + 1)
                    eng.activation(h0v[:, slot, :], pV0[:], ACT.Relu, bias=SH0, scale=SC0).then_inc(c_v0, 1)
                loop(eng, E_GROUPS, 2, group)
                eng.wait_ge(s_var, 1)
                eng.activation(st[:, 11:12], st[:, 10:11], ACT.Sqrt).then_inc(s_std, 1)

            @block.vector
            def _(eng):
                for s in (c_h1, c_v1):
                    eng.sem_inc(s, 1)
                for slot in range(2):
                    eng.sem_inc(h1_stored[slot], 16)

                def group(g, slot, turn):
                    eng.wait_ge(s_H1, g + 1)
                    eng.wait_ge(h1_stored[slot], 16 * turn + 16)
                    eng.tensor_copy(h1[:, slot, :], pH1[:]).then_inc(s_copy, 1)
                    eng.bn_stats(cols(statT, g * 6, 6), pH1[:]).then_inc(c_h1, 1)
                    eng.wait_ge(s_V1, g + 1)
                    eng.bn_stats(cols(statV, g * 6, 6), pV1[:]).then_inc(c_v1, 1)
                loop(eng, E_GROUPS, 2, group)
                t = Steps(eng, s_dve)
                eng.wait_ge(c_h1, E_GROUPS + 1)
                eng.wait_ge(c_v1, E_GROUPS + 1)
                mD, vD, mT, vT, mV, vV, a, b, c, delta, var, std = (st[:, i:i + 1] for i in range(12))
                t.did(eng.bn_aggr(st[:, 0:2], statD[:]))
                t.did(eng.bn_aggr(st[:, 2:4], statT[:]))
                t.did(eng.bn_aggr(st[:, 4:6], statV[:]))
                t.settle()
                SHARE = E_ROWS / N_NODES
                t.did(eng.tensor_tensor(a, mT, mD, ALU.subtract))
                t.did(eng.tensor_tensor(b, mV, mD, ALU.subtract))
                t.did(eng.tensor_tensor(delta, mT, mV, ALU.subtract))
                t.did(eng.tensor_tensor(c, vT, vV, ALU.subtract))
                t.settle()
                t.did(eng.tensor_scalar(delta, delta, SHARE, None, ALU.mult))
                t.did(eng.tensor_tensor(a, a, a, ALU.mult))
                t.did(eng.tensor_tensor(b, b, b, ALU.mult))
                t.settle()
                t.did(eng.tensor_tensor(c, c, a, ALU.add))
                t.settle()
                t.did(eng.tensor_tensor(c, c, b, ALU.subtract))
                t.did(eng.tensor_tensor(a, delta, delta, ALU.mult))
                t.settle()
                t.did(eng.scalar_tensor_tensor(var, c, SHARE, vD, ALU.mult, ALU.add))
                t.settle()
                t.did(eng.tensor_tensor(var, var, a, ALU.subtract))
                t.did(eng.tensor_tensor(mD, mD, delta, ALU.add))
                t.settle()
                eng.tensor_scalar(var, var, 0.0, BN_EPS, ALU.max, ALU.add).then_inc(s_var, 1)
                eng.wait_ge(s_std, 1)
                t.did(eng.reciprocal(var, std))
                t.did(eng.tensor_tensor(a, mD, B1, ALU.add))
                t.settle()
                t.did(eng.tensor_tensor(SC1, G1, var, ALU.mult))
                t.did(eng.tensor_tensor(b, B1, a, ALU.subtract))
                t.settle()
                t.did(eng.tensor_tensor(b, b, SC1, ALU.mult))
                t.settle()
                t.did(eng.tensor_tensor(SH1, BE1, b, ALU.add))
                t.settle()

        out_dense = out[0:D_GROUPS * GROUP].rearrange("(g p q) f -> g p (q f)", p=P, q=J)
        out_tail = out[D_GROUPS * GROUP:N_NODES].rearrange("(p q) f -> p (q f)", q=J)
        PER = 2

        class DenseRows:

            def __init__(self, makers, first, groups, h1_bank=None):
                sb, psum, sem, ring = makers
                self.SLOTS = groups * PER
                self.first_tile, self.n = first, PER * E_GROUPS
                self.xT = sb("xT", [P, self.SLOTS, GROUP // 2])
                self.h0 = sb("dh0", [P, 4, GROUP])
                self.h2 = sb("dh2", [P, 2, GROUP])
                self.sq1 = sb("sq1", [P, 2, J, OUT])
                self.sq2 = sb("sq2", [P, 2, J, OUT])
                self.y = sb("y", [P, 4, J, OUT])
                self.o = sb("o", [P, 4, J, OUT])
                small = sb("small", [P, 6, 4, J])
                self.sum1, self.std1, self.r1, self.sum2, self.std2, self.r2 = (small[:, i] for i in range(6))
                self.pH0 = psum("dH0")
                self.pH1 = psum("dH1") if h1_bank is None else h1_bank
                self.pU = psum("pU", 2)
                self.loaded, self.stored = ring("d_loaded", self.SLOTS), ring("d_stored", 4)
                self.first_done, self.h0_ready, self.second_done, self.relu_done = (
                    sem(f"d_{n}") for n in ("first", "h0", "second", "relu"))
                self.h2_ready, self.u_done, self.y_done, self.o_done = (sem(f"d_{n}") for n in ("h2", "u", "y", "o"))
                self.n1, self.n2 = ([sem(f"d_{n}{k}") for n in ("square", "root", "recip")]
                                    for k in (1, 2))

            def exists(self, d):
                return not isinstance(d, int) or 0 <= d < self.n

            def rows_of(self, d):
                return TAIL_P if isinstance(d, int) and d + self.first_tile == D_GROUPS else P

            def load(self, eng, d, slot):
                w = 2 * self.rows_of(d)
                eng.dma_start(self.xT[:, slot, 0:w], at(xT_dense, d + self.first_tile)[:, 0:w])\
                    .then_inc(self.loaded[slot], 16)

            def start_sync(self, eng):
                for d in range(self.SLOTS):
                    self.load(eng, d, d)

            def stores(self, eng, g, slot):
                for j in range(PER):
                    d, s = g * PER + j, slot * PER + j
                    if self.exists(d - 4):
                        self.store(eng, d - 4, s)

            def store(self, eng, d, slot):
                p = self.rows_of(d)
                eng.wait_ge(self.o_done, d + 1)
                eng.dma_start(at(out_dense, d + self.first_tile) if p == P else out_tail,
                              self.o[0:p, slot % 4].rearrange("p q f -> p (q f)")).then_inc(self.stored[slot % 4], 16)

            def finish_sync(self, eng):
                for d in range(self.n - 4, self.n):
                    self.store(eng, d, d % 4)
                for i in range(4):
                    eng.wait_ge(self.stored[i], 16 * len(range(i, self.n, 4)) + 16)

            def first(self, eng, d, slot, turn):
                w = 2 * self.rows_of(d)
                eng.wait_ge(self.loaded[slot], 16 * turn + 16)
                eng.wait_ge(self.h0_ready, d + 1)
                eng.matmul(self.pH0[:, 0:w], W0_top[:], self.xT[:, slot, 0:w], start=True, stop=True)
                eng.matmul(self.pH0[:, w:2 * w], W0_bot[:], self.xT[:, slot, 0:w], start=True, stop=True)\
                    .then_inc(self.first_done, 1)

            def second(self, eng, d, slot):
                w = 4 * self.rows_of(d)
                eng.wait_ge(self.h0_ready, d + 2)
                eng.wait_ge(self.relu_done, d + 1)
                eng.matmul(self.pH1[:, 0:w], Wr1T[:], self.h0[:, slot % 4, 0:w], start=True, stop=True)\
                    .then_inc(self.second_done, 1)

            def third(self, eng, d, slot):
                p = self.rows_of(d)
                eng.wait_ge(self.h2_ready, d + 1)
                eng.wait_ge(self.y_done, d + 1)
                bank = self.pU[0:p, slot % 2]
                for h in range(2):
                    eng.matmul(bank[:, h * 256:(h + 1) * 256], self.xT[:, slot, h * p:(h + 1) * p], U_x[:],
                               start=True, stop=False)
                    for k in range(2):
                        q = 2 * h + k
                        ins = eng.matmul(bank[:, q * P:(q + 1) * P],
                                         self.h2[:, slot % 2, (2 * k + h) * p:(2 * k + h + 1) * p], U_h[:],
                                         start=False, stop=k == 1)
                ins.then_inc(self.u_done, 1)

            def start_tensor(self, eng):
                self.first(eng, 0, 0, 0)
                self.first(eng, 1, 1, 0)
                self.second(eng, 0, 0)

            def tensor(self, eng, d, slot, turn, bank_read=None):
                if bank_read and self.exists(d + 2):
                    self.first(eng, d + 2, *later(slot, turn, 2, self.SLOTS))
                if bank_read:
                    bank_read()
                if self.exists(d + 1):
                    self.second(eng, d + 1, slot + 1)
                if not bank_read and self.exists(d + 2):
                    self.first(eng, d + 2, *later(slot, turn, 2, self.SLOTS))
                self.third(eng, d, slot)

            def relu0(self, eng, d, slot):
                w = 4 * self.rows_of(d)
                eng.wait_ge(self.first_done, d + 1)
                eng.activation(self.h0[:, slot % 4, 0:w], self.pH0[:, 0:w], ACT.Relu, bias=SH0D, scale=SC0)\
                    .then_inc(self.h0_ready, 1)

            def relu1(self, eng, d, slot):
                w = 4 * self.rows_of(d)
                eng.wait_ge(self.second_done, d + 1)
                eng.activation(self.h2[:, slot % 2, 0:w], self.pH1[:, 0:w], ACT.Relu, bias=SH1, scale=SC1)\
                    .then_inc(self.relu_done, 1)

            def squares(self, eng, d, slot, norm, rows, junk, sums):
                p = self.rows_of(d)
                for q in range(J):
                    ins = eng.activation(junk[0:p, slot % 2, q, :], rows[:, q, :], ACT.Square,
                                         accum_out=sums[0:p, slot % 4, q:q + 1])
                ins.then_inc(norm[0], 1)

            def root(self, eng, d, slot, norm, sums, std):
                p = self.rows_of(d)
                eng.wait_ge(norm[0], d + 1)
                eng.activation(std[0:p, slot % 4], sums[0:p, slot % 4], ACT.Sqrt, bias=eps_col[0:p], scale=1.0 / OUT)\
                    .then_inc(norm[1], 1)

            def start_scalar(self, eng):
                eng.sem_inc(self.h0_ready, 1)
                eng.sem_inc(self.relu_done, 1)
                self.relu0(eng, 0, 0)
                self.relu0(eng, 1, 1)
                self.relu1(eng, 0, 0)

            def scalar(self, eng, d, slot):
                if self.exists(d - 1):
                    p, s = self.rows_of(d - 1), slot + 3
                    eng.wait_ge(self.u_done, d)
                    if self.exists(d - 1 + self.SLOTS):
                        self.load(eng, d - 1 + self.SLOTS, (slot - 1) % self.SLOTS)
                    u = self.pU[0:p, s % 2].rearrange("p (q f) -> p q f", q=J)[:, :, 0:OUT]
                    self.squares(eng, d - 1, s, self.n1, u, self.sq1, self.sum1)
                if self.exists(d + 1):
                    self.relu1(eng, d + 1, slot + 1)
                if self.exists(d - 1):
                    self.root(eng, d - 1, slot + 3, self.n1, self.sum1, self.std1)
                if self.exists(d - 2):
                    p, s = self.rows_of(d - 2), slot + 2
                    eng.wait_ge(self.y_done, d + 1)
                    self.squares(eng, d - 2, s, self.n2, self.y[0:p, s % 4], self.sq2, self.sum2)
                if self.exists(d + 2):
                    self.relu0(eng, d + 2, slot + 2)
                if self.exists(d - 2):
                    self.root(eng, d - 2, slot + 2, self.n2, self.sum2, self.std2)

            def finish_scalar(self, eng):
                for d in (self.n, self.n + 1):
                    self.scalar(eng, d, d % self.SLOTS)

            def residual(self, eng, d, slot):
                w = 4 * self.rows_of(d)
                eng.wait_ge(self.relu_done, d + 2)
                h2 = self.h2[:, slot % 2, 0:w]
                eng.tensor_tensor(h2, h2, self.h0[:, slot % 4, 0:w], ALU.add).then_inc(self.h2_ready, 1)

            def first_norm(self, eng, d, slot):
                p = self.rows_of(d)
                eng.wait_ge(self.n1[1], d + 1)
                eng.reciprocal(self.r1[0:p, slot % 4], self.std1[0:p, slot % 4]).then_inc(self.n1[2], 1)
                eng.wait_ge(self.n1[2], d + 1)
                for q in range(J):
                    ins = eng.scalar_tensor_tensor(self.y[0:p, slot % 4, q, :], self.pU[0:p, slot % 2, q * P + OUT:(q + 1) * P],
                                                   self.r1[0:p, slot % 4, q:q + 1], biasC_row[0:p], ALU.mult, ALU.add)
                ins.then_inc(self.y_done, 1)

            def second_norm(self, eng, d, slot, turn):
                p = self.rows_of(d)
                eng.wait_ge(self.n2[1], d + 1)
                eng.reciprocal(self.r2[0:p, slot % 4], self.std2[0:p, slot % 4]).then_inc(self.n2[2], 1)
                eng.wait_ge(self.n2[2], d + 1)
                eng.wait_ge(self.stored[slot % 4], 16 * (turn * (self.SLOTS // 4) + slot // 4) + 16)
                eng.tensor_tensor(self.o[0:p, slot % 4], self.y[0:p, slot % 4],
                                  self.r2[0:p, slot % 4].unsqueeze(2).to_broadcast([p, J, OUT]), ALU.mult)\
                    .then_inc(self.o_done, 1)

            def start_vector(self, eng):
                eng.sem_inc(self.y_done, 2)
                for i in range(4):
                    eng.sem_inc(self.stored[i], 16)
                self.residual(eng, 0, 0)

            def vector(self, eng, d, slot, turn):
                if self.exists(d - 1):
                    self.first_norm(eng, d - 1, slot + 3)
                if self.exists(d + 1):
                    self.residual(eng, d + 1, slot + 1)
                if self.exists(d - 3):
                    self.second_norm(eng, d - 3, (slot - 3) % self.SLOTS, turn - 1 if slot < 3 else turn)

            def finish_vector(self, eng):
                for d in range(self.n, self.n + 3):
                    self.vector(eng, d, d % self.SLOTS, d // self.SLOTS)

        assert 2 * PER * E_GROUPS == D_GROUPS + 1 and 2 * PER % 4 == 0

        with ExitStack() as ctx:
            sb, psum, sem, ring = makers = tools(nc, ctx, "layer2")
            runs = GroupSums(makers, dst_rows, dst_col, prev_last, OUT, banks=1)
            idx = sb("idx", [P, 2, J], I32)
            A = sb("A", [P, 2, J, HID])
            aT = sb("aT", [P, GROUP])
            h0 = sb("h0", [P, 2, GROUP])
            h2 = sb("h2", [P, 2, GROUP])
            xe = sb("xe", [P, 2, J * IN])
            h0t = sb("h0t", [P, 2, GROUP])
            h1t = sb("h1t", [P, 2, GROUP])
            h2t = sb("h2t", [P, 2, GROUP])
            xt = sb("xt", [P, 2, J * IN])
            msg = sb("msg", [P, 2, J, OUT])
            ue = sb("ue", [P, 2, J, OUT])
            ut = sb("ut", [P, 2, J, OUT])
            agg_out = sb("agg_out", [P, 2, J * OUT])
            pA, pH1, pO, pOT = (psum(n) for n in ("pA", "pH1", "pO", "pOT"))
            dense = DenseRows(makers, 0, 2, h1_bank=pH1)
            i_loaded, gathered = ring("i_loaded"), ring("gathered")
            e_loaded, t_loaded = ring("e_loaded"), ring("t_loaded")
            e_stored, t_stored, agg_stored = ring("e_stored"), ring("t_stored"), ring("agg_stored")
            s_A, s_H1, s_O, s_OT = (sem(f"s_{n}") for n in ("A", "H1", "O", "OT"))
            c_A, c_relu, c_h2, c_O = (sem(f"c_{n}") for n in ("A", "relu", "h2", "O"))
            c_relut, c_h2t, c_OT = (sem(f"c_{n}") for n in ("relut", "h2t", "OT"))
            s_ux, s_u, s_ut, s_begun = (sem(n) for n in ("s_ux", "s_u", "s_ut", "s_begun"))
            block = ctx.enter_context(nc.Block())
            LAST = E_GROUPS - 1

            @block.sync
            def _(eng):
                def load_e(h, slot):
                    eng.dma_start(h0[:, slot, :], at(h0_src, h)).then_inc(e_loaded[slot], 16)
                    eng.dma_start(xe[:, slot, :], at(x_src, h)).then_inc(e_loaded[slot], 16)

                def load_idx(h, slot):
                    eng.dma_start(idx[:, slot, :], cols(slot_home, h * J, J)).then_inc(i_loaded[slot], 16)

                def load_t(h, slot):
                    eng.dma_start(h0t[:, slot, :], at(h0_dst, h)).then_inc(t_loaded[slot], 16)
                    eng.dma_start(h1t[:, slot, :], at(h1_dst, h)).then_inc(t_loaded[slot], 16)
                    eng.dma_start(xt[:, slot, :], at(x_dst, h)).then_inc(t_loaded[slot], 16)

                def store_u(h, slot):
                    eng.wait_ge(s_u, h + 1)
                    eng.dma_start(at(u_src, h), ue[:, slot].rearrange("p j f -> p (j f)")).then_inc(e_stored[slot], 16)
                    eng.wait_ge(s_ut, h + 1)
                    eng.dma_start(at(u_dst, h), ut[:, slot].rearrange("p j f -> p (j f)")).then_inc(t_stored[slot], 16)

                def group(g, slot, turn):
                    if not isinstance(g, int) or g + 3 < E_GROUPS:
                        eng.wait_ge(s_A, g + 2)
                        load_idx(g + 3, (slot + 1) % 2)
                    if not isinstance(g, int) or g + 2 < E_GROUPS:
                        eng.wait_ge(runs.selected, (J + 1) * g + J + 1)
                        runs.load(eng, g + 2, slot)
                    eng.wait_ge(runs.read, g + 3)
                    eng.dma_start(at(agg2_g, g), agg_out[:, slot, :]).then_inc(agg_stored[slot], 16)
                    if not isinstance(g, int) or g + 1 < E_GROUPS:
                        store_u(g + 1, (slot + 1) % 2)
                    if not isinstance(g, int) or g + 3 < E_GROUPS:
                        load_e(g + 3, (slot + 1) % 2)
                        load_t(g + 3, (slot + 1) % 2)
                    dense.stores(eng, g, slot)
                dense.start_sync(eng)
                for h in range(2):
                    load_idx(h, h)
                    load_e(h, h)
                    load_t(h, h)
                    runs.load(eng, h, h)
                eng.wait_ge(s_A, 1)
                load_idx(2, 0)
                store_u(0, 0)
                load_e(2, 0)
                load_t(2, 0)
                group(0, 0, 0)
                group(1, 1, 0)
                loop_from(eng, 2, E_GROUPS - 3, 2, group)
                for g in range(E_GROUPS - 3, E_GROUPS):
                    group(g, g % 2, g // 2)
                dense.finish_sync(eng)
                for slot in range(2):
                    n = 16 * len(range(slot, E_GROUPS, 2)) + 16
                    eng.wait_ge(e_stored[slot], n)
                    eng.wait_ge(t_stored[slot], n)
                    eng.wait_ge(agg_stored[slot], n)

            @block.gpsimd
            def _(eng):
                def gather(h, slot, turn):
                    eng.wait_ge(i_loaded[slot], 16 * turn + 16)
                    eng.sem_inc(s_begun, 1)
                    for j in range(J):
                        eng.indirect_dma_start(A[:, slot, j, :], None, agg1,
                                               bass.IndirectOffsetOnAxis(ap=idx[:, slot, j:j + 1], axis=0))\
                            .then_inc(gathered[slot], 16)
                loop(eng, E_GROUPS, 2, gather)

            @block.tensor
            def _(eng):
                def turn_rows(g, slot, turn):
                    eng.wait_ge(gathered[slot], 16 * J * turn + 16 * J)
                    eng.wait_ge(c_A, g + 1)
                    for j in range(J):
                        ins = eng.transpose(pA[:, j * P:(j + 1) * P], A[:, slot, j, :], ident[:])
                    ins.then_inc(s_A, 1)

                def second(g, slot, turn):
                    eng.wait_ge(e_loaded[slot], 32 * turn + 32)
                    eng.wait_ge(c_A, g + 2)
                    eng.wait_ge(c_relu, g + 1)
                    if not isinstance(g, int) or g > 0:
                        eng.wait_ge(dense.relu_done, PER * g + 1)
                    eng.matmul(pH1[:], Wr1T[:], h0[:, slot, :], start=True, stop=False)
                    eng.matmul(pH1[:], Wl1T[:], aT[:], start=False, stop=True).then_inc(s_H1, 1)

                def third_t(g, slot):
                    eng.wait_ge(c_h2t, g + 1)
                    eng.wait_ge(c_OT, g + 1)
                    for j in range(J):
                        ins = eng.matmul(pOT[:, j * OUT:(j + 1) * OUT], h2t[:, slot, j * P:(j + 1) * P],
                                         W2_msg[:, OUT:], start=True, stop=True)
                    ins.then_inc(s_OT, 1)

                def third(g, slot):
                    eng.wait_ge(c_h2, g + 1)
                    eng.wait_ge(c_O, g + 1)
                    eng.wait_ge(s_ux, g + 1)
                    for j in range(J):
                        ins = eng.matmul(pO[:, j * P:(j + 1) * P], h2[:, slot, j * P:(j + 1) * P],
                                         W2_msg[:], start=True, stop=True)
                    ins.then_inc(s_O, 1)

                def group(g, slot, turn):
                    more = not isinstance(g, int) or g + 1 < E_GROUPS
                    s1, t1 = later(slot, turn, 1, 2)
                    if more:
                        turn_rows(g + 1, s1, t1)
                    eng.wait_ge(c_O, g + 2)
                    runs.add(eng, g, slot, lambda i: msg[:, slot, i, :])
                    eng.wait_ge(c_relu, g + 2)
                    dense.tensor(eng, PER * g, PER * slot, turn)
                    if more:
                        second(g + 1, s1, t1)
                    runs.carry(eng, g, slot)
                    dense.tensor(eng, PER * g + 1, PER * slot + 1, turn,
                                 (lambda: eng.wait_ge(c_relu, g + 3)) if more else None)
                    if more:
                        third(g + 1, s1)
                        third_t(g + 1, s1)
                turn_rows(0, 0, 0)
                second(0, 0, 0)
                third_t(0, 0)
                third(0, 0)
                dense.start_tensor(eng)
                group(0, 0, 0)
                group(1, 1, 0)
                loop_from(eng, 2, E_GROUPS - 3, 2, group)
                for g in range(E_GROUPS - 3, E_GROUPS):
                    group(g, g % 2, g // 2)

            @block.scalar
            def _(eng):
                eng.sem_inc(c_A, 1)
                eng.sem_inc(c_relu, 1)

                def relu_t(g, slot, turn):
                    eng.wait_ge(t_loaded[slot], 48 * turn + 48)
                    eng.activation(h2t[:, slot, :], h1t[:, slot, :], ACT.Relu, bias=SH1, scale=SC1).then_inc(c_relut, 1)

                def copy(g):
                    eng.wait_ge(s_A, g + 1)
                    eng.activation(aT[:], pA[:], ACT.Copy).then_inc(c_A, 1)

                def relu(g, slot):
                    eng.wait_ge(s_H1, g + 1)
                    eng.activation(h2[:, slot, :], pH1[:], ACT.Relu, bias=SH1, scale=SC1).then_inc(c_relu, 1)

                def group(g, slot, turn):
                    more = not isinstance(g, int) or g + 1 < E_GROUPS
                    s1, t1 = later(slot, turn, 1, 2)
                    if more:
                        copy(g + 1)
                        relu_t(g + 1, s1, t1)
                    dense.scalar(eng, PER * g, PER * slot)
                    if more:
                        relu(g + 1, s1)
                    dense.scalar(eng, PER * g + 1, PER * slot + 1)
                copy(0)
                relu_t(0, 0, 0)
                relu(0, 0)
                dense.start_scalar(eng)
                group(0, 0, 0)
                group(1, 1, 0)
                loop_from(eng, 2, E_GROUPS - 3, 2, group)
                for g in range(E_GROUPS - 3, E_GROUPS):
                    group(g, g % 2, g // 2)
                dense.finish_scalar(eng)

            @block.vector
            def _(eng):
                eng.sem_inc(c_O, 1)
                eng.sem_inc(c_OT, 1)
                eng.sem_inc(s_ux, 1)
                for slot in range(2):
                    eng.sem_inc(agg_stored[slot], 16)
                    eng.sem_inc(e_stored[slot], 16)
                    eng.sem_inc(t_stored[slot], 16)
                runs.start_vector(eng)
                b2_all = b2_row[:].unsqueeze(1).to_broadcast([P, J, OUT])

                def residual_t(g, slot):
                    eng.wait_ge(c_relut, g + 1)
                    eng.tensor_tensor(h2t[:, slot, :], h2t[:, slot, :], h0t[:, slot, :], ALU.add).then_inc(c_h2t, 1)

                def residual(g, slot):
                    eng.wait_ge(c_relu, g + 2)
                    eng.tensor_tensor(h2[:, slot, :], h2[:, slot, :], h0[:, slot, :], ALU.add).then_inc(c_h2, 1)

                def sum_t(g, slot, turn):
                    eng.wait_ge(s_OT, g + 1)
                    eng.wait_ge(t_stored[slot], 16 * turn + 16)
                    eng.tensor_tensor(ut[:, slot], pOT[:, 0:J * OUT].rearrange("p (j f) -> p j f", j=J),
                                      xt[:, slot, :].rearrange("p (j f) -> p j f", j=J), ALU.add).then_inc(c_OT, 1)
                    eng.wait_ge(c_OT, g + 2)
                    eng.tensor_tensor(ut[:, slot], ut[:, slot], b2_all, ALU.add).then_inc(s_ut, 1)

                def sum_e(g, slot, turn):
                    eng.wait_ge(s_O, g + 1)
                    eng.wait_ge(e_stored[slot], 16 * turn + 16)
                    both = pO[:].rearrange("p (j f) -> p j f", j=J)
                    eng.tensor_copy(msg[:, slot], both[:, :, 0:OUT]).then_inc(c_O, 1)
                    eng.tensor_tensor(ue[:, slot], both[:, :, OUT:], xe[:, slot, :].rearrange("p (j f) -> p j f", j=J),
                                      ALU.add).then_inc(s_ux, 1)
                    eng.wait_ge(s_ux, g + 2)
                    eng.tensor_tensor(ue[:, slot], ue[:, slot], b2_all, ALU.add).then_inc(s_u, 1)

                def group(g, slot, turn):
                    more = not isinstance(g, int) or g + 1 < E_GROUPS
                    s1, t1 = later(slot, turn, 1, 2)
                    if more:
                        residual_t(g + 1, s1)
                    dense.vector(eng, PER * g, PER * slot, turn)
                    if more:
                        runs.select(eng, g + 1, s1, t1)
                        residual(g + 1, s1)
                    runs.keep(eng, g, slot)
                    eng.wait_ge(agg_stored[slot], 16 * turn + 16)
                    runs.means(eng, slot, agg_out[:, slot, :].rearrange("p (j f) -> p j f", j=J), weight_col, g)
                    dense.vector(eng, PER * g + 1, PER * slot + 1, turn)
                    if more:
                        sum_e(g + 1, s1, t1)
                        sum_t(g + 1, s1, t1)
                runs.select(eng, 0, 0, 0)
                residual_t(0, 0)
                residual(0, 0)
                sum_t(0, 0, 0)
                sum_e(0, 0, 0)
                dense.start_vector(eng)
                group(0, 0, 0)
                group(1, 1, 0)
                loop_from(eng, 2, LAST, 2, group)
                group(LAST, LAST % 2, LAST // 2)
                dense.finish_vector(eng)

        with ExitStack() as ctx:
            sb, psum, sem, ring = makers = tools(nc, ctx, "dense")
            dense = DenseRows(makers, PER * E_GROUPS, RING)
            idx = sb("idx", [P, RING, 2, J], I32)
            ue = sb("ue", [P, RING, J, OUT])
            A = sb("A", [P, RING, J, OUT])
            x1 = sb("x1", [P, RING, J, OUT])
            stats = sb("stats", [P, RING, J, 6])
            mv = sb("mv", [P, RING, J, 2])
            rstd = sb("rstd", [P, RING, 2, J])
            e_loaded, gathered, scattered = (ring(n, RING) for n in ("e_loaded", "gathered", "scattered"))
            e_idx = sem("e_idx")
            e_sum, e_st, e_mv, e_var, e_std, e_r, e_x1, e_begun, s_begun = (
                sem(n) for n in ("e_sum", "e_st", "e_mv", "e_var", "e_std", "e_r", "e_x1", "e_begun", "s_begun"))
            block = ctx.enter_context(nc.Block())

            @block.sync
            def _(eng):
                def load_e(h, slot):
                    eng.dma_start(ue[:, slot].rearrange("p j f -> p (j f)"), at(u_src, h)).then_inc(e_loaded[slot], 16)

                def group(g, slot, turn):
                    dense.stores(eng, g, slot)
                    if not isinstance(g, int) or 0 < g < E_GROUPS - 3:
                        s3, t3 = later(slot, turn, 3, RING)
                        eng.wait_ge(scattered[s3], 16 * J * t3)
                        load_e(g + 3, s3)
                dense.start_sync(eng)
                for h in range(RING):
                    load_e(h, h)
                for g in range(RING):
                    group(g, g, 0)
                loop_from(eng, RING, E_GROUPS - 3, RING, group)
                for g in range(E_GROUPS - 3, E_GROUPS):
                    group(g, g % RING, g // RING)
                dense.finish_sync(eng)

            @block.gpsimd
            def _(eng):
                def gather(h, slot, turn):
                    if not isinstance(h, int) or h >= RING:
                        eng.wait_ge(scattered[slot], 16 * J * turn)
                    for n, column in enumerate((slot_idx, rel_pos)):
                        eng.tensor_copy(idx[:, slot, n, :], cols(column, h * J, J)).then_inc(e_idx, 1)
                    eng.wait_ge(e_idx, 2 * h + 2)
                    eng.sem_inc(s_begun, 1)
                    for j in range(J):
                        eng.indirect_dma_start(A[:, slot, j, :], None, agg2,
                                               bass.IndirectOffsetOnAxis(ap=idx[:, slot, 0, j:j + 1], axis=0))\
                            .then_inc(gathered[slot], 16)

                def scatter(h, slot):
                    eng.wait_ge(e_x1, h + 1)
                    eng.sem_inc(s_begun, 1)
                    for j in range(J):
                        eng.indirect_dma_start(x1_by_rel, bass.IndirectOffsetOnAxis(ap=idx[:, slot, 1, j:j + 1], axis=0),
                                               x1[:, slot, j, :], None).then_inc(scattered[slot], 16)

                def group(g, slot, turn):
                    if not isinstance(g, int) or g + 2 < E_GROUPS:
                        gather(g + 2, *later(slot, turn, 2, RING))
                    scatter(g, slot)
                gather(0, 0, 0)
                gather(1, 1, 0)
                for g in range(RING):
                    group(g, g, 0)
                loop_from(eng, RING, E_GROUPS - 2, RING, group)
                for g in range(E_GROUPS - 2, E_GROUPS):
                    group(g, g % RING, g // RING)
                for slot in range(RING):
                    eng.wait_ge(scattered[slot], 16 * J * len(range(slot, E_GROUPS, RING)))

            @block.tensor
            def _(eng):
                def group(g, slot, turn):
                    for j in range(PER):
                        dense.tensor(eng, PER * g + j, PER * slot + j, turn)
                dense.start_tensor(eng)
                loop(eng, E_GROUPS - 3, RING, group)
                for g in range(E_GROUPS - 3, E_GROUPS):
                    group(g, g % RING, g // RING)

            @block.scalar
            def _(eng):
                def group(g, slot, turn):
                    for j in range(PER):
                        if j == 1:
                            eng.wait_ge(e_var, g + 1)
                            eng.activation(rstd[:, slot, 0, :], mv[:, slot, :, 1], ACT.Sqrt).then_inc(e_std, 1)
                        dense.scalar(eng, PER * g + j, PER * slot + j)
                dense.start_scalar(eng)
                for g in range(RING):
                    group(g, g, 0)
                loop_from(eng, RING, E_GROUPS - 3, RING, group)
                for g in range(E_GROUPS - 3, E_GROUPS):
                    group(g, g % RING, g // RING)
                dense.finish_scalar(eng)

            @block.vector
            def _(eng):
                def rows(g, slot, turn, part):
                    if part == 0:
                        eng.wait_ge(e_loaded[slot], 16 * turn + 16)
                        eng.wait_ge(gathered[slot], 16 * J * turn + 16 * J)
                        eng.tensor_tensor(ue[:, slot], ue[:, slot], A[:, slot], ALU.add).then_inc(e_sum, 1)
                        eng.wait_ge(e_sum, g + 1)
                        for q in range(J):
                            ins = eng.bn_stats(stats[:, slot, q, :], ue[:, slot, q, :])
                        ins.then_inc(e_st, 1)
                    if part == 1:
                        eng.wait_ge(e_st, g + 1)
                        eng.sem_inc(e_begun, 1)
                        for q in range(J):
                            ins = eng.bn_aggr(mv[:, slot, q, :], stats[:, slot, q, :])
                        ins.then_inc(e_mv, 1)
                    if part == 2:
                        eng.wait_ge(e_mv, g + 1)
                        eng.tensor_scalar(mv[:, slot, :, 1], mv[:, slot, :, 1], LN_EPS, None, ALU.add).then_inc(e_var, 1)
                    if part == 3:
                        eng.wait_ge(e_std, g + 1)
                        eng.reciprocal(rstd[:, slot, 1, :], rstd[:, slot, 0, :]).then_inc(e_r, 1)
                        eng.wait_ge(e_r, g + 1)
                        for q in range(J):
                            ins = eng.tensor_scalar(x1[:, slot, q, :], ue[:, slot, q, :], mv[:, slot, q, 0:1],
                                                    rstd[:, slot, 1, q:q + 1], ALU.subtract, ALU.mult)
                        ins.then_inc(e_x1, 1)

                def group(g, slot, turn):
                    rows(g, slot, turn, 0)
                    rows(g, slot, turn, 1)
                    rows(g, slot, turn, 2)
                    dense.vector(eng, PER * g, PER * slot, turn)
                    dense.vector(eng, PER * g + 1, PER * slot + 1, turn)
                    rows(g, slot, turn, 3)
                dense.start_vector(eng)
                for g in range(RING):
                    group(g, g, 0)
                loop_from(eng, RING, E_GROUPS - 3, RING, group)
                for g in range(E_GROUPS - 3, E_GROUPS):
                    group(g, g % RING, g // RING)
                dense.finish_vector(eng)

        with ExitStack() as ctx:
            sb, psum, sem, ring = makers = tools(nc, ctx, "relations")
            idx = sb("idx", [P, RING, 2], I32)
            W = sb("W", [P, RING, 2, OUT])
            xr = sb("xr", [P, RING, J, IN])
            xrT = sb("xrT", [P, 2, 2 * P])
            msg = sb("msg", [P, RING, J, OUT])
            pT, pM = psum("pT", 2), psum("pM", 4)
            i_loaded, x_loaded, w_got, m_stored = (ring(n, RING) for n in ("i_loaded", "x_loaded", "w_got", "m_stored"))
            s_T, c_T, s_M, c_M, s_begun = (sem(n) for n in ("s_T", "c_T", "s_M", "c_M", "s_begun"))
            block = ctx.enter_context(nc.Block())
            x_tiles = x1_by_rel.rearrange("(m p q) f -> m p q f", q=J, p=P)
            msg_tiles = msg_by_rel.rearrange("(m p q) f -> m p q f", q=J, p=P)
            weight_rows = rel_weights.rearrange("r i o -> (r i) o")

            @block.sync
            def _(eng):
                def load(m, slot):
                    eng.dma_start(idx[:, slot, :], cols(weight_home, m * 2, 2)).then_inc(i_loaded[slot], 16)
                    eng.dma_start(xr[:, slot], at(x_tiles, m)).then_inc(x_loaded[slot], 16)

                def group(m, slot, turn):
                    if not isinstance(m, int) or 0 < m < R_GROUPS - 3:
                        eng.wait_ge(s_M, m)
                        load(m + 3, (slot + 3) % RING)
                    eng.wait_ge(c_M, m + 3)
                    eng.dma_start(at(msg_tiles, m), msg[:, slot]).then_inc(m_stored[slot], 16)
                for m in range(RING):
                    load(m, m)
                for m in range(RING):
                    group(m, m, 0)
                loop_from(eng, RING, R_GROUPS - 3, RING, group)
                for m in range(R_GROUPS - 3, R_GROUPS):
                    group(m, m % RING, m // RING)
                for slot in range(RING):
                    eng.wait_ge(m_stored[slot], 16 * len(range(slot, R_GROUPS, RING)) + 16)

            @block.gpsimd
            def _(eng):
                def gather(m, slot, turn):
                    eng.wait_ge(i_loaded[slot], 16 * turn + 16)
                    eng.sem_inc(s_begun, 1)
                    for h in range(2):
                        eng.indirect_dma_start(W[:, slot, h, :], None, weight_rows,
                                               bass.IndirectOffsetOnAxis(ap=idx[:, slot, h:h + 1], axis=0))\
                            .then_inc(w_got[slot], 16)
                loop(eng, R_GROUPS, RING, gather)

            @block.tensor
            def _(eng):
                def turn_rows(m, slot, turn):
                    eng.wait_ge(x_loaded[slot], 16 * turn + 16)
                    eng.wait_ge(c_T, m + 1)
                    for h in range(2):
                        ins = eng.transpose(pT[:, slot % 2, h * P:(h + 1) * P], xr[:, slot, 2 * h:2 * h + 2, :], ident[:])
                    ins.then_inc(s_T, 1)

                def products(m, slot, turn):
                    eng.wait_ge(w_got[slot], 32 * turn + 32)
                    eng.wait_ge(c_T, m + 3)
                    eng.wait_ge(c_M, m + 1)
                    for h in range(2):
                        for k in range(2):
                            half = slice(k * IN, (k + 1) * IN)
                            ins = eng.matmul(pM[:, 2 * (slot % 2) + k, h * OUT:(h + 1) * OUT], xrT[half, slot % 2, h * P:(h + 1) * P],
                                             W[half, slot, h, :], start=True, stop=True)
                    ins.then_inc(s_M, 1)

                def group(m, slot, turn):
                    if not isinstance(m, int) or m + 1 < R_GROUPS:
                        turn_rows(m + 1, *later(slot, turn, 1, RING))
                    products(m, slot, turn)
                turn_rows(0, 0, 0)
                loop(eng, R_GROUPS - 1, RING, group)
                m = R_GROUPS - 1
                group(m, m % RING, m // RING)

            @block.scalar
            def _(eng):
                eng.sem_inc(c_T, 2)

                def copy(m, slot, turn):
                    eng.wait_ge(s_T, m + 1)
                    eng.wait_ge(c_M, m + 1)
                    eng.activation(xrT[:, slot % 2, :], pT[:, slot % 2, 0:2 * P], ACT.Copy).then_inc(c_T, 1)
                loop(eng, R_GROUPS, RING, copy)

            @block.vector
            def _(eng):
                eng.sem_inc(c_M, 2)
                for slot in range(RING):
                    eng.sem_inc(m_stored[slot], 16)

                def copy(m, slot, turn):
                    eng.wait_ge(s_M, m + 1)
                    eng.wait_ge(m_stored[slot], 16 * turn + 16)
                    eng.tensor_copy(msg[:, slot].rearrange("p (h k) f -> p k h f", k=2),
                                    pM[:, 2 * (slot % 2):2 * (slot % 2) + 2, 0:P].rearrange("p k (h f) -> p k h f", h=2))\
                        .then_inc(c_M, 1)
                loop(eng, R_GROUPS, RING, copy)

        RING = 4
        with ExitStack() as ctx:
            sb, psum, sem, ring = makers = tools(nc, ctx, "final")
            runs = GroupSums(makers, dst_rows, dst_col, prev_last, OUT)
            idx = sb("idx", [P, RING, 2, J], I32)
            M = sb("M", [P, RING, J, OUT])
            v = sb("v", [P, RING, J, OUT])
            A2 = sb("A2", [P, RING, J, OUT])
            A3 = sb("A3", [P, RING, J, OUT])
            x1 = sb("x1", [P, RING, J, OUT])
            x1T = sb("x1T", [P, 2, 2 * P])
            y = sb("y", [P, RING, J, OUT])
            o = sb("o", [P, RING, J, OUT])
            stats = sb("stats", [P, 2, RING, J, 6])
            mv = sb("mv", [P, 2, RING, J, 2])
            std = sb("std", [P, 2, RING, 2, J])
            pT, pY = psum("pT"), psum("pY")
            i_loaded, t_loaded, gathered, scattered = (ring(n, RING) for n in ("i_loaded", "t_loaded", "gathered", "scattered"))
            s_v, s_x1, s_T, c_T, s_Y, c_Y, s_yb, s_y, s_o, s_begun, s_wait = (
                sem(n) for n in ("s_v", "s_x1", "s_T", "c_T", "s_Y", "c_Y", "s_yb", "s_y", "s_o", "s_begun", "s_wait"))
            n_stats, n_mv, n_var, n_std, n_r = ([sem(f"{n}{i}") for i in range(2)]
                                                for n in ("n_stats", "n_mv", "n_var", "n_std", "n_r"))
            block = ctx.enter_context(nc.Block())

            def has(h):
                return not isinstance(h, int) or 0 <= h < E_GROUPS

            @block.sync
            def _(eng):
                def load(h, slot):
                    eng.dma_start(idx[:, slot, 0, :], cols(rel_home, h * J, J)).then_inc(i_loaded[slot], 16)
                    eng.dma_start(idx[:, slot, 1, :], cols(out_home, h * J, J)).then_inc(i_loaded[slot], 16)
                    eng.dma_start(v[:, slot].rearrange("p j f -> p (j f)"), at(u_dst, h)).then_inc(t_loaded[slot], 16)
                    eng.dma_start(A2[:, slot].rearrange("p j f -> p (j f)"), at(agg2_g, h)).then_inc(t_loaded[slot], 16)

                def group(g, slot, turn):
                    if has(g + 2):
                        eng.wait_ge(runs.selected, (J + 1) * g + J + 1)
                        runs.load(eng, g + 2, slot % 2)
                    if has(g + 3) and (not isinstance(g, int) or g > 0):
                        s3, t3 = later(slot, turn, 3, RING)
                        eng.wait_ge(scattered[s3], 16 * J * t3)
                        load(g + 3, s3)
                for h in range(RING):
                    load(h, h)
                for h in range(2):
                    runs.load(eng, h, h)
                for g in range(RING):
                    group(g, g, 0)
                loop_from(eng, RING, E_GROUPS - 3, RING, group)
                for g in range(E_GROUPS - 3, E_GROUPS):
                    group(g, g % RING, g // RING)

            @block.gpsimd
            def _(eng):
                def gather(h, slot, turn):
                    eng.wait_ge(i_loaded[slot], 32 * turn + 32)
                    eng.sem_inc(s_begun, 1)
                    for j in range(J):
                        eng.indirect_dma_start(M[:, slot, j, :], None, msg_by_rel,
                                               bass.IndirectOffsetOnAxis(ap=idx[:, slot, 0, j:j + 1], axis=0))\
                            .then_inc(gathered[slot], 16)

                def scatter(h, slot):
                    eng.wait_ge(s_o, h + 1)
                    eng.sem_inc(s_begun, 1)
                    for j in range(J):
                        eng.indirect_dma_start(out, bass.IndirectOffsetOnAxis(ap=idx[:, slot, 1, j:j + 1], axis=0),
                                               o[:, slot, j, :], None, bounds_check=N_NODES - 1, oob_is_err=False)\
                            .then_inc(scattered[slot], 16)

                def group(g, slot, turn):
                    if has(g + 2):
                        gather(g + 2, *later(slot, turn, 2, RING))
                    scatter(g, slot)
                gather(0, 0, 0)
                gather(1, 1, 0)
                loop(eng, E_GROUPS - 2, RING, group)
                for g in range(E_GROUPS - 2, E_GROUPS):
                    group(g, g % RING, g // RING)
                for slot in range(RING):
                    eng.wait_ge(scattered[slot], 16 * J * len(range(slot, E_GROUPS, RING)))

            @block.tensor
            def _(eng):
                def turn_rows(h, slot):
                    eng.wait_ge(s_x1, h + 1)
                    eng.wait_ge(c_T, h + 1)
                    for i in range(2):
                        ins = eng.transpose(pT[:, i * P:(i + 1) * P], x1[:, slot, 2 * i:2 * i + 2, :], ident[:])
                    ins.then_inc(s_T, 1)

                def own(h, slot):
                    eng.wait_ge(c_T, h + 2)
                    eng.wait_ge(c_Y, h + 1)
                    for i in range(2):
                        ins = eng.matmul(pY[:, i * P:(i + 1) * P], x1T[:, slot % 2, i * P:(i + 1) * P], Ws2[:],
                                         start=True, stop=True)
                    ins.then_inc(s_Y, 1)

                def group(g, slot, turn):
                    eng.wait_ge(gathered[slot], 16 * J * turn + 16 * J)
                    runs.add(eng, g, slot % 2, lambda i: M[:, slot, i, :])
                    if has(g + 1):
                        turn_rows(g + 1, (slot + 1) % RING)
                    runs.carry(eng, g, slot % 2)
                    if has(g + 1):
                        own(g + 1, (slot + 1) % RING)
                turn_rows(0, 0)
                own(0, 0)
                loop(eng, E_GROUPS - 1, RING, group)
                g = E_GROUPS - 1
                group(g, g % RING, g // RING)

            @block.scalar
            def _(eng):
                eng.sem_inc(c_T, 1)

                def copy(h, slot):
                    eng.wait_ge(s_T, h + 1)
                    eng.wait_ge(c_Y, h + 1)
                    eng.activation(x1T[:, slot % 2, :], pT[:, 0:2 * P], ACT.Copy).then_inc(c_T, 1)

                def root(n, h, slot):
                    eng.wait_ge(n_var[n], h + 1)
                    eng.activation(std[:, n, slot, 0, :], mv[:, n, slot, :, 1], ACT.Sqrt).then_inc(n_std[n], 1)

                def group(g, slot, turn):
                    if has(g + 1):
                        copy(g + 1, (slot + 1) % RING)
                    if has(g + 2):
                        root(0, g + 2, (slot + 2) % RING)
                    root(1, g, slot)
                root(0, 0, 0)
                copy(0, 0)
                root(0, 1, 1)
                loop(eng, E_GROUPS - 2, RING, group)
                for g in range(E_GROUPS - 2, E_GROUPS):
                    group(g, g % RING, g // RING)

            @block.vector
            def _(eng):
                eng.sem_inc(c_Y, 1)
                runs.start_vector(eng)
                bias_all = bias_row[:].unsqueeze(1).to_broadcast([P, J, OUT])

                def moments(n, h, slot, rows, ready):
                    eng.wait_ge(ready, h + 1)
                    for q in range(J):
                        ins = eng.bn_stats(stats[:, n, slot, q, :], rows[:, slot, q, :])
                    ins.then_inc(n_stats[n], 1)

                def aggregate(n, h, slot):
                    eng.wait_ge(n_stats[n], h + 1)
                    eng.sem_inc(s_wait, 1)
                    for q in range(J):
                        ins = eng.bn_aggr(mv[:, n, slot, q, :], stats[:, n, slot, q, :])
                    ins.then_inc(n_mv[n], 1)
                    eng.wait_ge(n_mv[n], h + 1)
                    eng.tensor_scalar(mv[:, n, slot, :, 1], mv[:, n, slot, :, 1], LN_EPS, None, ALU.add)\
                        .then_inc(n_var[n], 1)

                def normalize(n, h, slot, rows, to, done):
                    eng.wait_ge(n_std[n], h + 1)
                    eng.reciprocal(std[:, n, slot, 1, :], std[:, n, slot, 0, :]).then_inc(n_r[n], 1)
                    eng.wait_ge(n_r[n], h + 1)
                    for q in range(J):
                        ins = eng.tensor_scalar(to[:, slot, q, :], rows[:, slot, q, :], mv[:, n, slot, q, 0:1],
                                                std[:, n, slot, 1, q:q + 1], ALU.subtract, ALU.mult)
                    ins.then_inc(done, 1)

                def first_sum(h, slot, turn):
                    eng.wait_ge(t_loaded[slot], 32 * turn + 32)
                    eng.tensor_tensor(v[:, slot], v[:, slot], A2[:, slot], ALU.add).then_inc(s_v, 1)
                    moments(0, h, slot, v, s_v)

                def own_sum(h, slot):
                    eng.wait_ge(s_Y, h + 1)
                    eng.tensor_tensor(y[:, slot], pY[:, 0:J * OUT].rearrange("p (j f) -> p j f", j=J), x1[:, slot],
                                      ALU.add).then_inc(c_Y, 1)
                    eng.wait_ge(c_Y, h + 2)
                    eng.tensor_tensor(y[:, slot], y[:, slot], bias_all, ALU.add).then_inc(s_yb, 1)

                def second_sum(h, slot):
                    eng.wait_ge(s_yb, h + 1)
                    eng.wait_ge(runs.read, h + 3)
                    eng.tensor_tensor(y[:, slot], y[:, slot], A3[:, slot], ALU.add).then_inc(s_y, 1)
                    moments(1, h, slot, y, s_y)

                def group(g, slot, turn):
                    nxt, ahead = (slot + 1) % RING, (slot + 2) % RING
                    if has(g + 1):
                        runs.select(eng, g + 1, nxt % 2, later(slot, turn, 1, RING)[1] * 2 + nxt // 2)
                    runs.keep(eng, g, slot % 2)
                    runs.means(eng, slot % 2, A3[:, slot], weight_col, g)
                    second_sum(g, slot)
                    if has(g + 2):
                        first_sum(g + 2, *later(slot, turn, 2, RING))
                        aggregate(0, g + 2, ahead)
                    aggregate(1, g, slot)
                    if has(g + 1):
                        own_sum(g + 1, nxt)
                    if has(g + 2):
                        normalize(0, g + 2, ahead, v, x1, s_x1)
                    normalize(1, g, slot, y, o, s_o)
                for h in range(2):
                    first_sum(h, h, 0)
                    aggregate(0, h, h)
                    normalize(0, h, h, v, x1, s_x1)
                runs.select(eng, 0, 0, 0)
                own_sum(0, 0)
                loop(eng, E_GROUPS - 2, RING, group)
                for g in range(E_GROUPS - 2, E_GROUPS):
                    group(g, g % RING, g // RING)


_INS = ['x', 'src', 'dst', 'edge_type_32', 'L0_gnn_Wl0', 'L0_gnn_Wr0', 'L0_gnn_b0', 'L0_gnn_Wl1', 'L0_gnn_Wr1',
        'L0_gnn_b1', 'L0_gnn_Wl2', 'L0_gnn_Wr2', 'L0_gnn_b2', 'L0_gnn_g0', 'L0_gnn_be0', 'L0_gnn_g1', 'L0_gnn_be1',
        'L1_gnn_basis', 'L1_gnn_coeff', 'L1_gnn_self_weight', 'L1_gnn_bias']


def kernel(**inputs):
    import numpy as _np
    import concourse.bacc as _bacc
    from concourse import mybir as _mybir
    from concourse.bass_utils import run_bass_kernel_spmd as _run

    nc = _bacc.Bacc("TRN2", target_bir_lowering=False, num_devices=1)
    arrays, args = {}, []
    for name in _INS:
        a = _np.ascontiguousarray(inputs[name])
        arrays[f"in_{name}"] = a
        args.append(nc.dram_tensor(f"in_{name}", a.shape, _mybir.dt.from_np(a.dtype), kind="ExternalInput").ap())
    args.append(nc.dram_tensor("out_0", (N_NODES, OUT), F32, kind="ExternalOutput").ap())
    gnn_program(nc, *args)
    return _run(nc, [arrays], core_ids=[0]).results[0]["out_0"]
```
